# Optimizing a Trainium2 kernel written in Bass

```python
import numpy as np
import jax
import jax.numpy as jnp

def _softmax(x, axis=-1):
    return jax.nn.softmax(x, axis=axis)

def _gelu(x):
    return jax.nn.gelu(x, approximate=True)

def _silu(x):
    return jax.nn.silu(x)

def _sigmoid(x):
    return jax.nn.sigmoid(x)

def _layernorm(x, axis=-1, eps=1e-05):
    m = jnp.mean(x, axis=axis, keepdims=True)
    v = jnp.var(x, axis=axis, keepdims=True)
    return (x - m) / jnp.sqrt(v + eps)

def _scatter_add(tgt, idx, src, axis=0):
    return tgt.at[idx].add(src)

def _segment_sum(src, seg, n):
    return jax.ops.segment_sum(src, seg, n)
kernel_name = 'mk_prb_d2_jaxref_r4_605626'

def setup_inputs(seed: int=0):
    np.random.seed(seed)
    _w = jnp.asarray

    def _L0_attn_setup():
        import math
        import jax, jax.numpy as jnp
        import numpy as np
        N_HEAD = 16

        def _rope_cos_sin(l, head_dim):
            scale = jnp.arange(0, head_dim, 2, dtype=jnp.float32)[:head_dim // 2]
            freqs = 1.0 / 10000.0 ** scale
            angles = jnp.arange(l, dtype=jnp.float32)[:, None] * freqs[None, :]
            return (jnp.cos(angles), jnp.sin(angles))

        def _rope_apply(x, cos, sin):
            b, l, h, hd = x.shape
            xp = x.astype(jnp.float32).reshape(b, l, h, hd // 2, 2)
            xr, xi = (xp[..., 0], xp[..., 1])
            c = cos[None, :, None, :]
            s = sin[None, :, None, :]
            out_r = xr * c - xi * s
            out_i = xr * s + xi * c
            out = jnp.stack([out_r, out_i], axis=-1).reshape(b, l, h, hd)
            return out.astype(x.dtype)
        key = jax.random.key(seed)
        ks = jax.random.split(key, 9)
        b, l, d = (2, 512, 256)
        sc = 1.0 / math.sqrt(d)
        inp = {'x': jax.random.normal(ks[0], (b, l, d), dtype=jnp.float32), 'Wq': jax.random.normal(ks[1], (d, d), dtype=jnp.float32) * sc, 'bq': jnp.zeros((d,), dtype=jnp.float32), 'Wk': jax.random.normal(ks[2], (d, d), dtype=jnp.float32) * sc, 'bk': jnp.zeros((d,), dtype=jnp.float32), 'Wv': jax.random.normal(ks[3], (d, d), dtype=jnp.float32) * sc, 'bv': jnp.zeros((d,), dtype=jnp.float32), 'Wo': jax.random.normal(ks[4], (d, d), dtype=jnp.float32) * sc, 'bo': jnp.zeros((d,), dtype=jnp.float32)}
        return inp
    _L0_attn_in = _L0_attn_setup()

    def _L0_ffn_setup():
        import jax, jax.numpy as jnp
        import numpy as np
        B, T, D, E, H, K = (4, 512, 256, 8, 512, 2)
        key = jax.random.key(seed)
        k0, k1, k2, k3 = jax.random.split(key, 4)
        x = jax.random.normal(k0, (B, T, D), dtype=jnp.float32)
        router_w = jax.random.normal(k1, (E, D), dtype=jnp.float32) * D ** (-0.5)
        w1 = jax.random.normal(k2, (E, D, H), dtype=jnp.float32) * D ** (-0.5)
        w2 = jax.random.normal(k3, (E, H, D), dtype=jnp.float32) * H ** (-0.5)
        return {'x': x, 'router_w': router_w, 'w1': w1, 'w2': w2}
    _L0_ffn_in = _L0_ffn_setup()

    def _L1_attn_setup():
        import jax, jax.numpy as jnp
        import numpy as np
        HEAD = 8
        BLOCK = 64
        D_MODEL = 256
        key = jax.random.key(seed)
        ks = jax.random.split(key, 9)
        d = D_MODEL
        s = 0.02
        return {'src': jax.random.normal(ks[0], (4, 1024, d), dtype=jnp.float32), 'Wq': jax.random.normal(ks[1], (d, d), dtype=jnp.float32) * s, 'bq': jax.random.normal(ks[2], (d,), dtype=jnp.float32) * s, 'Wk': jax.random.normal(ks[3], (d, d), dtype=jnp.float32) * s, 'bk': jax.random.normal(ks[4], (d,), dtype=jnp.float32) * s, 'Wv': jax.random.normal(ks[5], (d, d), dtype=jnp.float32) * s, 'bv': jax.random.normal(ks[6], (d,), dtype=jnp.float32) * s, 'Wo': jax.random.normal(ks[7], (d, d), dtype=jnp.float32) * s, 'bo': jax.random.normal(ks[8], (d,), dtype=jnp.float32) * s}
    _L1_attn_in = _L1_attn_setup()

    def _L1_ffn_setup():
        import jax, jax.numpy as jnp
        import numpy as np
        B, T, C, H, E = (4, 512, 256, 512, 8)
        CAPACITY_FACTOR = 1.0
        key = jax.random.key(seed)
        ks = jax.random.split(key, 5)
        scale = 0.02
        return {'x': jax.random.normal(ks[0], (B, T, C), dtype=jnp.float32), 'Wg': jax.random.normal(ks[1], (E, C), dtype=jnp.float32) * scale, 'W1': jax.random.normal(ks[2], (E, H, C), dtype=jnp.float32) * scale, 'W2': jax.random.normal(ks[3], (E, C, H), dtype=jnp.float32) * scale, 'W3': jax.random.normal(ks[4], (E, H, C), dtype=jnp.float32) * scale}
    _L1_ffn_in = _L1_ffn_setup()
    _d = {'L0_attn_x': _L0_attn_in['x'], 'L0_attn_Wq': _L0_attn_in['Wq'], 'L0_attn_bq': _L0_attn_in['bq'], 'L0_attn_Wk': _L0_attn_in['Wk'], 'L0_attn_bk': _L0_attn_in['bk'], 'L0_attn_Wv': _L0_attn_in['Wv'], 'L0_attn_bv': _L0_attn_in['bv'], 'L0_attn_Wo': _L0_attn_in['Wo'], 'L0_attn_bo': _L0_attn_in['bo'], 'L0_ffn_router_w': _L0_ffn_in['router_w'], 'L0_ffn_w1': _L0_ffn_in['w1'], 'L0_ffn_w2': _L0_ffn_in['w2'], 'L1_attn_Wq': _L1_attn_in['Wq'], 'L1_attn_bq': _L1_attn_in['bq'], 'L1_attn_Wk': _L1_attn_in['Wk'], 'L1_attn_bk': _L1_attn_in['bk'], 'L1_attn_Wv': _L1_attn_in['Wv'], 'L1_attn_bv': _L1_attn_in['bv'], 'L1_attn_Wo': _L1_attn_in['Wo'], 'L1_attn_bo': _L1_attn_in['bo'], 'L1_ffn_Wg': _L1_ffn_in['Wg'], 'L1_ffn_W1': _L1_ffn_in['W1'], 'L1_ffn_W2': _L1_ffn_in['W2'], 'L1_ffn_W3': _L1_ffn_in['W3']}
    _x0 = _d['L0_attn_x']
    _d['L0_attn_x'] = jax.random.normal(jax.random.fold_in(jax.random.key(seed), 1), (2, 2048, 256), dtype=_x0.dtype)
    del _x0
    return _d

def reference(L0_attn_x, L0_attn_Wq, L0_attn_bq, L0_attn_Wk, L0_attn_bk, L0_attn_Wv, L0_attn_bv, L0_attn_Wo, L0_attn_bo, L0_ffn_router_w, L0_ffn_w1, L0_ffn_w2, L1_attn_Wq, L1_attn_bq, L1_attn_Wk, L1_attn_bk, L1_attn_Wv, L1_attn_bv, L1_attn_Wo, L1_attn_bo, L1_ffn_Wg, L1_ffn_W1, L1_ffn_W2, L1_ffn_W3):

    def _L0_attn_ref(x, Wq, bq, Wk, bk, Wv, bv, Wo, bo):
        import math
        import jax, jax.numpy as jnp
        import numpy as np
        N_HEAD = 16

        def _rope_cos_sin(l, head_dim):
            scale = jnp.arange(0, head_dim, 2, dtype=jnp.float32)[:head_dim // 2]
            freqs = 1.0 / 10000.0 ** scale
            angles = jnp.arange(l, dtype=jnp.float32)[:, None] * freqs[None, :]
            return (jnp.cos(angles), jnp.sin(angles))

        def _rope_apply(x, cos, sin):
            b, l, h, hd = x.shape
            xp = x.astype(jnp.float32).reshape(b, l, h, hd // 2, 2)
            xr, xi = (xp[..., 0], xp[..., 1])
            c = cos[None, :, None, :]
            s = sin[None, :, None, :]
            out_r = xr * c - xi * s
            out_i = xr * s + xi * c
            out = jnp.stack([out_r, out_i], axis=-1).reshape(b, l, h, hd)
            return out.astype(x.dtype)
        b, l, d = x.shape
        h = N_HEAD
        hd = d // h
        q = (x @ Wq + bq).reshape(b, l, h, hd)
        k = (x @ Wk + bk).reshape(b, l, h, hd)
        v = (x @ Wv + bv).reshape(b, l, h, hd)
        cos, sin = _rope_cos_sin(l, hd)
        q = _rope_apply(q, cos, sin)
        k = _rope_apply(k, cos, sin)
        score = jnp.einsum('blhd,bmhd->bhlm', q, k) / math.sqrt(hd)
        ctx = jnp.einsum('bhlm,bmhd->blhd', score, v).reshape(b, l, d)
        return ctx @ Wo + bo

    def _L0_ffn_ref(x, router_w, w1, w2):
        import jax, jax.numpy as jnp
        import numpy as np
        B, T, D, E, H, K = (4, 512, 256, 8, 512, 2)
        Bb, Tt, Dd = x.shape
        N = Bb * Tt
        logits = jnp.einsum('btd,ed->bte', x, router_w)
        top_vals, top_idx = jax.lax.top_k(logits, K)
        top_w = jax.nn.softmax(top_vals, axis=-1)
        xf = x.reshape(N, Dd)
        h = jnp.einsum('nd,edh->enh', xf, w1)
        h = jnp.square(jax.nn.relu(h))
        y = jnp.einsum('enh,ehd->end', h, w2)
        idx_f = top_idx.reshape(N, K)
        w_f = top_w.reshape(N, K)
        y_sel = y[idx_f, jnp.arange(N)[:, None]]
        out = jnp.einsum('nk,nkd->nd', w_f, y_sel)
        return out.reshape(Bb, Tt, Dd)

    def _L1_attn_ref(src, Wq, bq, Wk, bk, Wv, bv, Wo, bo):
        import jax, jax.numpy as jnp
        import numpy as np
        HEAD = 8
        BLOCK = 64
        D_MODEL = 256
        B, S, D = src.shape
        H, bs = (HEAD, BLOCK)
        dk = D // H
        nb = S // bs
        q = (src @ Wq + bq).reshape(B, nb, bs, H, dk)
        k = (src @ Wk + bk).reshape(B, nb, bs, H, dk)
        v = (src @ Wv + bv).reshape(B, nb, bs, H, dk)
        scores = jnp.einsum('bnqhd,bnkhd->bhnqk', q, k) * dk ** (-0.5)
        probs = jax.nn.softmax(scores, axis=-1)
        out = jnp.einsum('bhnqk,bnkhd->bnqhd', probs, v).reshape(B, S, D)
        return out @ Wo + bo

    def _L1_ffn_ref(x, Wg, W1, W2, W3):
        import jax, jax.numpy as jnp
        import numpy as np
        B, T, C, H, E = (4, 512, 256, 512, 8)
        CAPACITY_FACTOR = 1.0
        b, t, c = x.shape
        e = Wg.shape[0]
        n = b * t
        capacity = max(1, int(CAPACITY_FACTOR * n / e))
        x_flat = x.reshape(n, c)
        scores = (x_flat @ Wg.T).T
        top_vals, token_idx = jax.lax.top_k(scores, capacity)
        token_w = jax.nn.softmax(top_vals, axis=-1)
        xg = x_flat[token_idx]
        h = jax.nn.silu(jnp.einsum('eic,ehc->eih', xg, W1)) * jnp.einsum('eic,ehc->eih', xg, W3)
        y = jnp.einsum('eih,ech->eic', h, W2) * token_w[..., None]
        out = jnp.zeros_like(x_flat).at[token_idx.reshape(-1)].add(y.reshape(-1, c))
        return out.reshape(b, t, c)
    x = L0_attn_x
    xn = _layernorm(x, axis=-1)
    x = x + _L0_attn_ref(xn, L0_attn_Wq, L0_attn_bq, L0_attn_Wk, L0_attn_bk, L0_attn_Wv, L0_attn_bv, L0_attn_Wo, L0_attn_bo) + _L0_ffn_ref(xn, L0_ffn_router_w, L0_ffn_w1, L0_ffn_w2)
    xn = _layernorm(x, axis=-1)
    x = x + _L1_attn_ref(xn, L1_attn_Wq, L1_attn_bq, L1_attn_Wk, L1_attn_bk, L1_attn_Wv, L1_attn_bv, L1_attn_Wo, L1_attn_bo) + _L1_ffn_ref(xn, L1_ffn_Wg, L1_ffn_W1, L1_ffn_W2, L1_ffn_W3)
    return x

_drawn_inputs = setup_inputs


def setup_inputs(seed=0):
    import zlib

    import numpy as np

    out = dict(_drawn_inputs(seed))
    spreads = {'L0_attn_bq': (0.0, 0.406),
     'L0_attn_bk': (0.0, 0.1),
     'L0_attn_bv': (0.0, 0.1),
     'L0_attn_bo': (0.0, 2.0)}
    factors = {'L0_ffn_router_w': 8.0,
     'L0_ffn_w1': 8.0,
     'L0_ffn_w2': 8.0,
     'L1_attn_Wq': 52.629,
     'L1_attn_bq': 64.0,
     'L1_attn_Wk': 52.345,
     'L1_attn_bk': 64.0,
     'L1_attn_Wv': 50.97,
     'L1_attn_bv': 64.0,
     'L1_attn_Wo': 50.796,
     'L1_attn_bo': 64.0,
     'L1_ffn_Wg': 64.0,
     'L1_ffn_W1': 64.0,
     'L1_ffn_W2': 64.0,
     'L1_ffn_W3': 64.0}
    for name, (base, spread) in spreads.items():
        noise = np.random.default_rng([zlib.crc32(name.encode()), seed]).standard_normal(out[name].shape)
        drawn = base * np.exp(spread * noise) if base else spread * noise
        out[name] = jnp.asarray(drawn.astype(out[name].dtype))
    for name, factor in factors.items():
        out[name] = (out[name] * factor).astype(out[name].dtype)
    return out
```

```python
import concourse.bass as bass
from concourse import mybir
from contextlib import ExitStack

F32 = mybir.dt.float32
BF16 = mybir.dt.bfloat16
I32 = mybir.dt.int32
U32 = mybir.dt.uint32
ALU = mybir.AluOpType
ACT = mybir.ActivationFunctionType
AX = mybir.AxisListType.X

P = 128
N, D = 4096, 256
NB, L = 2, 2048
NT = N // P
BT = L // P
DC = D // P
E, H = 8, 512
HC = H // P
TOPK = 2
NH0, HD0 = 16, 16
JR = HD0 // 2
NH1, DK = 8, 32
BLK = 64
CAP = N // E
ST0 = TOPK * N // P + E
ROW = D + E
BIG = 8192.0
EPS = 1e-5
ds = bass.ds
RMAX = bass.bass_isa.ReduceOp.max


def over_last(ap, n):
    return ap.unsqueeze(2).broadcast_to([ap.shape[0], ap.shape[1], n])


def over_mid(ap, n):
    return ap.unsqueeze(1).broadcast_to([ap.shape[0], n, ap.shape[1]])


class Step:

    def __init__(self, half, par):
        self.half, self.par, self.t = half, par, 2 * half + par

    def back(self, k):
        q = self.par - k
        return Step(self.half + (q >> 1), q & 1)

    def at_least(self, k):
        return not isinstance(self.half, int) or self.t >= k


def in_range(s, n):
    return not isinstance(s.half, int) or 0 <= s.t < n


def two_layers(nc, x, wqkv0, bq0, bkv0, wo0, bo0, rw0, w1_0, w2_0,
               wqkv1, bqk1, bv1, wo1, bo1, wg1, w13_1, w2_1, cos_q, sin_q, cos_k, sin_k, out):
    xg0_d = nc.dram_tensor("rows_layer0", [N, ROW], F32).ap()
    xg1_d = nc.dram_tensor("rows_layer1", [N, ROW], F32).ap()
    xb_d = nc.dram_tensor("x_plus_bias", [N, D], F32).ap()
    x1_d = nc.dram_tensor("x_layer1", [N, D], F32).ap()
    xb1_d = nc.dram_tensor("x1_plus_bias", [N, D], F32).ap()

    def rows(dram, t, lo=0, hi=D):
        return dram[ds(t * P, P), lo:hi]

    ctx = ExitStack()
    with ctx:
        def sb(name, shape, dt=F32):
            return ctx.enter_context(nc.sbuf_tensor(name, shape, dt))

        def sem(name):
            return ctx.enter_context(nc.semaphore(name))

        def sem2(name):
            return [sem(name + "_even"), sem(name + "_odd")]

        wqkv0_s = sb("wqkv0_s", [P, DC, 3 * D])
        wo0_s = sb("wo0_s", [P, DC, D])
        wqkv1_s = sb("wqkv1_s", [P, DC, 3 * D])
        wo1_s = sb("wo1_s", [P, DC, D])
        rw0_s = sb("rw0_s", [P, DC, E])
        wg1_s = sb("wg1_s", [P, DC, E])
        bq0_s = sb("bq0_s", [P, DC])
        bqk1_s = sb("bqk1_s", [P, 2 * DC])
        bkv0_s = sb("bkv0_s", [P, 2 * D])
        bv1_s = sb("bv1_s", [P, D])
        bo0_s = sb("bo0_s", [P, D])
        bo1_s = sb("bo1_s", [P, D])
        cosk_s = sb("cosk_s", [P, BT * JR])
        sink_s = sb("sink_s", [P, BT * 2 * JR])
        ident = sb("ident", [P, P])
        headmask = sb("headmask", [P, 2, P // 2])
        eps_c = sb("eps_c", [P, 1])
        upper = sb("upper", [P, P], BF16)
        ones = sb("ones", [P, P], BF16)
        iota_e = sb("iota_e", [P, E])
        iota_p = sb("iota_p", [P, P], BF16)
        iota_t = sb("iota_t", [P, ST0])
        iota_128m = sb("iota_128m", [P, NT])
        pid1 = sb("pid1", [P, 1])
        cval = sb("cval", [P, TOPK * NT])
        not_first = sb("not_first", [P, E, NT], BF16)
        bit_i = sb("bit_i", [P, NT], I32)

        r1 = sb("r1", [P, E, 2 * DC * H])
        r2 = sb("r2", [P, NT * D])
        r3 = sb("r3", [P, 64 * P + 64 * 2 * ST0], BF16)
        rt = sb("rt", [P, 3 * L])
        rw = sb("rw", [P, 6272])

        qk_all = r1[:, :, :].rearrange("p e n -> p (e n)").rearrange("p (m n) -> p m n", m=4)
        qrot_all = r2[:, :].rearrange("p (c n) -> p c n", c=DC)
        v_all = r2[:, :].rearrange("p (t n) -> p t n", t=NT)
        cosq_s = rt[:, 0:L]
        sinq_s = rt[:, L:3 * L].rearrange("p (r n) -> p r n", r=2)

        top_v = sb("top_v", [P, NT * TOPK])
        top_i = sb("top_i", [P, NT * TOPK])
        pid0 = sb("pid0", [P, 1])
        one8 = sb("one8", [P, E])
        hot_lo = r3[:, 0:TOPK * NT * P].rearrange("p (n m) -> p n m", m=P)
        hot_hi = r3[:, TOPK * NT * P:TOPK * NT * (P + 2 * ST0)].rearrange("p (n m) -> p n m", m=2 * ST0)
        hot1_hi = r3[:, 0:NT * E * 32].rearrange("p (c m) -> p c m", c=NT)
        hot1_lo = r3[:, NT * E * 32:NT * E * 64].rearrange("p (c k e m) -> p c k e m", c=NT, k=2, e=E)

        taken = [0]

        def scratch(shape, dt=F32, reset=False):
            if reset:
                taken[0] = 0
            n = 1
            for k in shape:
                n *= k
            words = n if dt != BF16 else n // 2
            v = rt[:, taken[0]:taken[0] + words]
            taken[0] += words
            assert taken[0] <= 3 * L
            v = v if dt == F32 else v.bitcast(dt)
            if len(shape) == 2:
                v = v.rearrange("p (a b) -> p a b", a=shape[0])
            elif len(shape) == 3:
                v = v.rearrange("p (a b c) -> p a b c", a=shape[0], b=shape[1])
            return v

        m_k = [scratch([E, NT], reset=True), scratch([E, NT])]
        r_tmp = [scratch([E, NT]), scratch([E, NT])]
        incl, excl = scratch([E, NT]), scratch([E, NT])
        m_all = [scratch([2, D]), scratch([2, D])]
        r_big = scratch([2 * ST0 * E])
        small_mask = scratch([E * NT], BF16)
        top_d, top_e, top_w = scratch([NT]), scratch([NT]), scratch([TOPK, NT])
        n_tiles, t_incl, t_excl = scratch([E]), scratch([E]), scratch([E])
        slot_f, slot_i, slot_lh = scratch([TOPK, NT]), scratch([2, TOPK * NT], I32), scratch([2, TOPK * NT])
        te_f, inv_f, inv_z = scratch([ST0]), scratch([2 * ST0]), scratch([ST0])
        s_both = scratch([2 * E * NT], BF16, reset=True)
        s_in = [scratch([E, NT]), scratch([E, NT])]
        s_ex = [scratch([E, NT]), scratch([E, NT])]
        s_exp = scratch([E, NT])
        s_ri = [scratch([E, NT], I32), scratch([E, NT], I32)]
        s_zp, s_need = scratch([E]), scratch([E])
        s_iv = [scratch([2, 4, 16]), scratch([2, 4, 16])]
        s_id = scratch([2, 16])
        onesf = scratch([P])
        idx0 = sb("idx0", [P, ST0], I32)
        idx1 = sb("idx1", [P, E * (CAP // P)], I32)
        tile_e = sb("tile_e", [P, ST0], I32)
        tile_1h = sb("tile_1h", [P, ST0 * E], BF16)
        gate0 = sb("gate0", [P, ST0])
        tail = r3[:, NT * E * 64:NT * E * 64 + 3 * E * NT]
        sc_all = tail[:, 0:2 * E * NT].bitcast(F32).rearrange("p (e t) -> p e t", e=E)
        e_cmp = tail[:, 2 * E * NT:3 * E * NT].rearrange("p (e t) -> p e t", e=E)

        used = [0]

        def work(shape, reset=False):
            if reset:
                used[0] = 0
            n = 1
            for k in shape:
                n *= k
            v = rw[:, used[0]:used[0] + n]
            used[0] += n
            assert used[0] <= 6272, used[0]
            if len(shape) == 2:
                v = v.rearrange("p (a b) -> p a b", a=shape[0])
            elif len(shape) == 3:
                v = v.rearrange("p (a b c) -> p a b c", a=shape[0], b=shape[1])
            elif len(shape) == 4:
                v = v.rearrange("p (a b c d) -> p a b c d", a=shape[0], b=shape[1], c=shape[2])
            return v

        bank = [ctx.enter_context(nc.psum_tensor(f"bank{i}", [P, 512], F32)) for i in range(4)]
        banks47 = ctx.enter_context(nc.psum_tensor("banks47", [P, 4, 512], F32))
        bank += [banks47[:, i, :] for i in range(4)]

        consts = sem("consts_loaded")
        consts_b = sem("late_consts_loaded")
        made = sem("constants_made")
        w0_in = sem("experts0_loaded")
        stage_end = sem("stage_ended")
        seq = sem("vector_chain")
        pseq = sem("pool_chain")

        stages = [0]

        def end_stage(eng, n):
            eng.drain().then_inc(stage_end, 1)
            eng.wait_ge(stage_end, 5 * n)

        block = ctx.enter_context(nc.Block())

        a_x = work([2, D], reset=True)
        a_xn = work([2, D])
        a_xT = work([2, DC, P])
        a_kv = work([2, 2 * D])
        a_kr = work([2, D])
        a_t = work([2, D])
        a_q = work([2, DC, P])
        a_pt = work([2, D])
        a_xb = work([2, D])
        a_lg = work([2, E])
        a_st = work([2, 6])
        a_mv = work([2, 2])
        a_sd = work([2, 1])
        a_rs = work([2, 1])
        a_top = work([2, E])
        a_ti = work([2, E])
        kvm = work([NB, DC, P])
        a_kvm = [[kvm[:, b, g, :] for g in range(DC)] for b in range(NB)]

        class S:
            pass

        def ln_sems(z):
            s = S()
            s.x_in = sem2(f"x_loaded_{z}")
            s.stats, s.moments, s.std = sem(f"stats_{z}"), sem(f"moments_{z}"), sem(f"std_{z}")
            s.rstd, s.xn = sem(f"rstd_{z}"), sem(f"xn_ready_{z}")
            s.xn_out = sem2(f"xn_stored_{z}")
            s.xb, s.xb_out = sem(f"xb_ready_{z}"), sem2(f"xb_stored_{z}")
            s.xT_ps, s.xT = sem(f"xT_in_psum_{z}"), sem(f"xT_ready_{z}")
            return s

        sa, sd = ln_sems("a"), ln_sems("d")
        kv_ps, kv_sb, lg_ps, lg_sb = sem("kv_in_psum"), sem("kv_ready"), sem("logits_in_psum"), sem("logits_ready")
        q_ps, q_sb = sem("q_in_psum"), sem("q_ready")
        top_m, top_done, top_kept = sem("top_placed"), sem("top_found"), sem("top_kept")
        kprod, krot = sem("k_products"), sem("k_rotated")
        qprod, qrot = sem("q_products"), sem("q_rotated")
        st_ps = sem("ktv_in_psum")

        mask_r, rank_ps = sem("pair_mask_ready"), sem("ranks_in_psum")
        hot_r, inv_ps = sem("one_hots_ready"), sem("slots_in_psum")
        e_sb, d_sb = sem("top_exp_ready"), sem("top_diff_ready")
        gates_r, gates_out = sem("gates_ready"), sem("gates_stored")
        kvm_r, m_ps, m_sb = sem("ktv_masked"), sem("m_in_psum"), sem("m_ready")
        ql_in, xb_in = sem2("q_tile_loaded"), sem2("xb_tile_loaded")
        ao_ps, ao_sb, x1_out = sem("attn0_in_psum"), sem("attn0_added"), sem2("x1_stored")

        c_xg = work([2, ROW], reset=True)
        c_xT = work([2, DC, P])
        c_r = work([2, H])
        c_h = work([2, H])
        c_hT = work([2, HC, P])
        c_y = work([2, D])
        c_gt = work([2, E])
        c_gi = sb("c_gi", [P, 2], I32)
        c_si = sb("c_si", [P, 2], I32)
        xg_clear, gi_r, si_r, xg_in = sem("rows_cleared"), sem("gather_index"), sem("scatter_index"), sem2("rows_gathered")
        cT_ps, cT_sb, h_ps, relu_sb, h_sb = (sem("rows_T_in_psum"), sem("rows_T_ready"), sem("h_in_psum"),
                                             sem("relu_ready"), sem("h_ready"))
        hT_ps, hT_sb, y_ps, y_sb = sem("hT_in_psum"), sem("hT_ready"), sem("y_in_psum"), sem("y_ready")
        gate_r, y_out = sem("gate_ready"), sem("y_scattered")

        d_x = work([2, D], reset=True)
        d_xn = work([2, D])
        d_xT = work([2, DC, P])
        d_xb = work([2, D])
        d_sc = work([2, E])
        d_st = work([2, 6])
        d_mv = work([2, 2])
        d_sd = work([2, 1])
        d_rs = work([2, 1])
        qk1_ps, qk1_sb, v1_ps, v1_sb = sem("qk1_in_psum"), sem("qk1_ready"), sem("v1_in_psum"), sem("v1_ready")
        sc_ps, sc_sb, sc_kept, sc_out = sem("scores_in_psum"), sem("scores_ready"), sem("scores_kept"), sem2("scores_stored")

        NP = NH1 // 2
        e_qk = work([2, 4, P], reset=True)
        e_v = work([2, 2, 2, P])
        e_s = work([NH1, BLK])
        e_p = work([2, NH1, BLK])
        e_pT = work([NP, P])
        e_o = work([2, D])
        e_oT = work([2, DC, P])
        e_y = work([2, D])
        e_xb = work([2, D])
        e_mx = work([NH1])
        e_sum = work([2, NH1])
        e_rc = work([2, NH1])
        e_part = sb("e_part", [P, 2, E], BF16)
        key_r, cand_r, thr_r, cmp_r = sem("key_kept"), sem("candidate_ready"), sem("threshold_ready"), sem("compared")
        key = sb("key", [P, E], I32)
        cand = sb("cand", [P, E], I32)
        thr = sb("thr", [P, E], I32)
        flip = sb("flip", [P, E], I32)
        got = sb("got", [P, E], I32)
        scmax = sb("scmax", [P, E])
        nscmax = sb("nscmax", [P, E])
        pmax = sb("pmax", [P, E])
        vz = sem("v_spread_cleared")
        qkl, vl, xbl = sem2("qk_tile_loaded"), sem2("v_tile_loaded"), sem2("xb1_tile_loaded")
        s_ps, mx_r, sub_r, p_r, sum_r, rc_r = (sem("att_in_psum"), sem("row_max"), sem("shifted"), sem("exp_ready"),
                                               sem("row_sum"), sem("row_rcp"))
        pT_ps, pT_sb, o_ps, o_sb, oT_ps, oT_sb = (sem("pT_in_psum"), sem("pT_ready"), sem("o_in_psum"), sem("o_ready"),
                                                  sem("oT_in_psum"), sem("oT_ready"))
        y1_ps, y1_sb, fin_r, fin_out = sem("y1_in_psum"), sem("y1_ready"), sem("final_ready"), sem2("final_stored")
        part_r, cnt_ps, cnt_used = sem("counts_ready"), sem("counts_in_psum"), sem("counts_used")
        pm_r, gmax_r, ngm_r = sem("partition_max"), sem("global_max"), sem("negated_max")
        ex_r, z_r, z_ps, rz_r = sem("score_exp"), sem("exp_sums"), sem("exp_sums_in_psum"), sem("exp_rcp")
        both_r, rank1_ps, hot1_r, inv1_ps, idx1_r = (sem("above_and_ties"), sem("ranks1_in_psum"), sem("one_hots1_ready"),
                                                     sem("slots1_in_psum"), sem("index1_ready"))

        f1 = r1[:, :, :].rearrange("p e n -> p (e n)")
        TE = CAP // P
        f_xg = f1[:, 0:2 * TE * ROW].rearrange("p (b i n) -> p b i n", b=2, i=TE)
        o1 = 2 * TE * ROW
        f_xT = f1[:, o1:o1 + 2 * DC * CAP].rearrange("p (b c n) -> p b c n", b=2, c=DC)
        o2 = o1 + 2 * DC * CAP
        f_g = f1[:, o2:o2 + 2 * CAP].rearrange("p (b n) -> p b n", b=2)
        o3 = o2 + 2 * CAP
        f_h = f1[:, o3:o3 + 2 * HC * CAP].rearrange("p (b c n) -> p b c n", b=2, c=HC)
        o4 = o3 + 2 * HC * CAP
        f_y = f1[:, o4:o4 + TE * D].rearrange("p (i n) -> p i n", i=TE)
        f_w = [rt[:, 3072 * b:3072 * (b + 1)] for b in range(2)]
        f_gi = sb("f_gi", [P, TE], I32)
        f_si = sb("f_si", [P, TE], I32)
        f_we = sb("f_we", [P, 2, TE])
        f_wg = sb("f_wg", [P, 2, TE])
        rz = sb("rz", [P, E])
        fw_in = sem2("expert1_loaded")
        fgi_r, fsi_r, fx_in = sem("gather1_index"), sem("scatter1_index"), sem2("rows1_gathered")
        fT_ps, fT_sb, h13_ps, g_r, hh_r = (sem("rows1_T_in_psum"), sem("rows1_T_ready"), sem("h13_in_psum"),
                                           sem("silu_ready"), sem("hidden1_ready"))
        fy_ps, fy_sb, fwe_r, fwg_r, fy_out = (sem("y1e_in_psum"), sem("y1e_ready"), sem("weight_exp"),
                                              sem("weight_ready"), sem("y1e_scattered"))

        @block.sync
        def _(sp):
            def load_x(z, s, src, dst):
                sp.dma_start(dst[:, s.par, :], rows(src, s.t)).then_inc(z.x_in[s.par], 16)

            load_x(sa, Step(0, 0), x, a_x)
            load_x(sa, Step(0, 1), x, a_x)
            for dst, src in ((wqkv0_s[:, :, :], wqkv0.rearrange("(c p) n -> p c n", p=P)),
                             (rw0_s[:, :, :], rw0.rearrange("(c p) n -> p c n", p=P)),
                             (bq0_s[:, :], bq0[:, :]),
                             (bkv0_s[:, :], bkv0.partition_broadcast(P)),
                             (bo0_s[:, :], bo0.partition_broadcast(P)),
                             (cosk_s[:, :], cos_k[:, :]),
                             (sink_s[:, :], sin_k[:, :]),
                             (cosq_s, cos_q[:, :]),
                             (sinq_s, sin_q.rearrange("p (r n) -> p r n", r=2))):
                sp.dma_start(dst, src).then_inc(consts, 16)
            for dst, src in ((wo0_s[:, :, :], wo0.rearrange("(c p) n -> p c n", p=P)),
                             (wqkv1_s[:, :, :], wqkv1.rearrange("(c p) n -> p c n", p=P)),
                             (wo1_s[:, :, :], wo1.rearrange("(c p) n -> p c n", p=P)),
                             (wg1_s[:, :, :], wg1.rearrange("(c p) n -> p c n", p=P)),
                             (bqk1_s[:, :], bqk1[:, :]),
                             (bv1_s[:, :], bv1.partition_broadcast(P)),
                             (bo1_s[:, :], bo1.partition_broadcast(P))):
                sp.dma_start(dst, src).then_inc(consts_b, 16)
            for e in range(E):
                sp.dma_start(r1[:, e, 0:DC * H].rearrange("p (c n) -> p c n", c=DC),
                             w1_0[e].rearrange("(c p) n -> p c n", p=P)).then_inc(w0_in, 16)
                sp.dma_start(r1[:, e, DC * H:2 * DC * H].rearrange("p (c n) -> p c n", c=HC),
                             w2_0[e].rearrange("(c p) n -> p c n", p=P)).then_inc(w0_in, 16)

            def step_a(s, more=True):
                sp.wait_ge(sa.xn, s.t + 1)
                sp.dma_start(rows(xg0_d, s.t), a_xn[:, s.par, :]).then_inc(sa.xn_out[s.par], 16)
                sp.wait_ge(sa.xb, s.t + 1)
                sp.dma_start(rows(xb_d, s.t), a_xb[:, s.par, :]).then_inc(sa.xb_out[s.par], 16)
                if more:
                    load_x(sa, Step(s.half + 1, s.par), x, a_x)

            with sp.Fori(0, NT // 2 - 1) as m:
                for par in range(2):
                    step_a(Step(m, par))
            for par in range(2):
                step_a(Step(NT // 2 - 1, par), more=False)
            for par in range(2):
                sp.wait_ge(sa.xn_out[par], 16 * (NT // 2))
                sp.wait_ge(sa.xb_out[par], 16 * (NT // 2))

            def load_b(s):
                sp.dma_start(a_q[:, s.par, :, :], qrot_all[:, :, ds(s.t * P, P)]).then_inc(ql_in[s.par], 16)
                sp.dma_start(a_xb[:, s.par, :], rows(xb_d, s.t)).then_inc(xb_in[s.par], 16)

            sp.wait_ge(qrot, NT)
            for par in range(2):
                load_b(Step(0, par))
            sp.wait_ge(gates_r, 1)
            sp.dma_start(xg0_d.rearrange("(t p) n -> p t n", p=P)[:, :, D:ROW],
                         a_kv[:, 0, 0:NT * E].rearrange("p (t e) -> p t e", t=NT)).then_inc(gates_out, 16)

            def step_b(s, more=True):
                sp.wait_ge(ao_sb, s.t + 1)
                sp.dma_start(rows(x1_d, s.t), a_xn[:, s.par, :]).then_inc(x1_out[s.par], 16)
                if more:
                    load_b(Step(s.half + 1, s.par))

            with sp.Fori(0, NT // 2 - 1) as m:
                for par in range(2):
                    step_b(Step(m, par))
            for par in range(2):
                step_b(Step(NT // 2 - 1, par), more=False)
            for par in range(2):
                sp.wait_ge(x1_out[par], 16 * (NT // 2))
            sp.wait_ge(gates_out, 16)
            end_stage(sp, 1)

            end_stage(sp, 2)

            for par in range(2):
                load_x(sd, Step(0, par), x1_d, d_x)

            def step_d(s, more=True):
                sp.wait_ge(sd.xn, s.t + 1)
                sp.dma_start(rows(xg1_d, s.t), d_xn[:, s.par, :]).then_inc(sd.xn_out[s.par], 16)
                sp.wait_ge(sd.xb, s.t + 1)
                sp.dma_start(rows(xb1_d, s.t), d_xb[:, s.par, :]).then_inc(sd.xb_out[s.par], 16)
                if more:
                    load_x(sd, Step(s.half + 1, s.par), x1_d, d_x)
                if s.at_least(1):
                    b = s.back(1)
                    sp.wait_ge(sc_sb, b.t + 1)
                    sp.dma_start(rows(xg1_d, b.t, D, ROW), d_sc[:, b.par, :]).then_inc(sc_out[b.par], 16)

            step_d(Step(0, 0))
            step_d(Step(0, 1))
            with sp.Fori(1, NT // 2 - 1) as m:
                for par in range(2):
                    step_d(Step(m, par))
            for par in range(2):
                step_d(Step(NT // 2 - 1, par), more=False)
            sp.wait_ge(sc_sb, NT)
            sp.dma_start(rows(xg1_d, NT - 1, D, ROW), d_sc[:, 1, :]).then_inc(sc_out[1], 16)
            for par in range(2):
                sp.wait_ge(sd.xn_out[par], 16 * (NT // 2))
                sp.wait_ge(sd.xb_out[par], 16 * (NT // 2))
                sp.wait_ge(sc_out[par], 16 * (NT // 2))
            end_stage(sp, 3)

            def load_qk(s):
                if s.at_least(2):
                    sp.wait_ge(s_ps, s.t - 1)
                sp.dma_start(e_qk[:, s.par, :, :], qk_all[:, :, ds(s.t * P, P)]).then_inc(qkl[s.par], 16)

            def load_v(s):
                if s.at_least(2):
                    sp.wait_ge(o_ps, s.t - 1)
                for b in range(2):
                    for hp in range(2):
                        sp.dma_start(e_v[BLK * hp:BLK * hp + BLK, s.par, b, hp, :],
                                     r2[BLK * b:BLK * b + BLK, ds(s.t * D + P * hp, P)]).then_inc(vl[s.par], 16)

            def load_xb1(s):
                sp.dma_start(e_xb[:, s.par, :], rows(xb1_d, s.t)).then_inc(xbl[s.par], 16)

            def store_e(s, more=True):
                sp.wait_ge(fin_r, s.t + 1)
                sp.dma_start(rows(out, s.t), e_y[:, s.par, :]).then_inc(fin_out[s.par], 16)
                if more:
                    load_xb1(Step(s.half + 1, s.par))

            sp.wait_ge(vz, 1)
            for par in range(2):
                load_qk(Step(0, par))
                load_v(Step(0, par))
                load_xb1(Step(0, par))
            for t in (2, 3):
                load_qk(Step(1, t - 2))
                if t == 3:
                    load_v(Step(1, 0))
            with sp.Fori(2, NT // 2) as m:
                for par in range(2):
                    s = Step(m, par)
                    load_qk(s)
                    load_v(s.back(1))
                    store_e(s.back(4))
            load_v(Step(NT // 2 - 1, 1))
            for t in range(NT - 4, NT):
                store_e(Step(t // 2, t % 2), more=t < NT - 2)
            for par in range(2):
                sp.wait_ge(fin_out[par], 16 * (NT // 2))
            end_stage(sp, 4)

            def load_w(s):
                w = f_w[s.par]
                sp.dma_start(w[:, 0:2 * DC * H].rearrange("p (c n) -> p c n", c=DC),
                             w13_1[ds(s.t, 1)].rearrange("o (c p) n -> p (o c) n", p=P)).then_inc(fw_in[s.par], 16)
                sp.dma_start(w[:, 2 * DC * H:3072].rearrange("p (c n) -> p c n", c=HC),
                             w2_1[ds(s.t, 1)].rearrange("o (c p) n -> p (o c) n", p=P)).then_inc(fw_in[s.par], 16)

            for par in range(2):
                load_w(Step(0, par))
            with sp.Fori(1, E // 2) as m:
                for par in range(2):
                    s = Step(m, par)
                    sp.wait_ge(fy_ps, TE * (s.t - 1))
                    load_w(s)
            sp.wait_ge(fy_out, 16 * TE * E)

        @block.tensor
        def _(pe):
            def transpose_x(z, s, xn, n=NT):
                pe.wait_ge(z.xn, s.t + 1)
                if s.at_least(1):
                    pe.wait_ge(z.xT, s.t)
                for c in range(DC):
                    last = pe.transpose(bank[0][:, c * P:(c + 1) * P], xn[:, s.par, c * P:(c + 1) * P], ident[:, :])
                last.then_inc(z.xT_ps, 1)

            pe.wait_ge(consts, 16 * 9)
            pe.wait_ge(made, 1)

            def step_a(s, first=False):
                if in_range(s.back(1), NT) and s.at_least(1):
                    b = s.back(1)
                    xT = a_xT[:, b.par, :, :]
                    pe.wait_ge(sa.xT, b.t + 1)
                    if b.at_least(2):
                        pe.wait_ge(kv_sb, b.t - 1)
                    for c in range(DC):
                        last = pe.matmul(bank[1 + b.par][:, :], xT[:, c, :], wqkv0_s[:, c, D:3 * D],
                                         start=c == 0, stop=c == DC - 1)
                    last.then_inc(kv_ps, 1)
                if in_range(s, NT):
                    transpose_x(sa, s, a_xn)
                if in_range(s.back(1), NT) and s.at_least(1):
                    if b.at_least(2):
                        pe.wait_ge(q_sb, 2 * (b.t - 1))
                    for r in range(DC):
                        for c in range(DC):
                            last = pe.matmul(bank[5 + b.par][:, r * P:(r + 1) * P], wqkv0_s[:, c, r * P:(r + 1) * P],
                                             xT[:, c, :], start=c == 0, stop=c == DC - 1)
                    last.then_inc(q_ps, 1)
                    if b.at_least(1):
                        pe.wait_ge(lg_sb, b.t)
                    for c in range(DC):
                        last = pe.matmul(bank[7][:, 0:E], xT[:, c, :], rw0_s[:, c, :], start=c == 0, stop=c == DC - 1)
                    last.then_inc(lg_ps, 1)
                if s.at_least(3) and in_range(s.back(3), NT):
                    b = s.back(3)
                    start = isinstance(b.half, int) and b.t % BT == 0
                    stop = isinstance(b.half, int) and b.t % BT == BT - 1
                    pe.wait_ge(krot, b.t + 1)
                    if start and b.t:
                        pe.wait_ge(kvm_r, 1)
                    kr = a_kr[:, b.par, :].rearrange("p (r h) -> p r h", r=2)
                    for g in range(2):
                        last = pe.matmul(bank[3 + g][:, 0:P], a_kv[:, b.par, D + g * P:D + (g + 1) * P],
                                         kr[:, :, g * 64:(g + 1) * 64], start=start, stop=stop)
                    last.then_inc(st_ps, 1)

            for t in range(4):
                step_a(Step(t // 2, t % 2))
            with pe.Fori(2, 9) as m:
                for par in range(2):
                    step_a(Step(m, par))
            for t in (18, 19):
                step_a(Step(t // 2, t % 2))
            with pe.Fori(10, NT // 2) as m:
                for par in range(2):
                    step_a(Step(m, par))
            for t in (32, 33, 34):
                step_a(Step(t // 2, t % 2))

            pe.wait_ge(consts_b, 16 * 7)
            pe.wait_ge(mask_r, 1)
            pe.wait_ge(kv_sb, NT)
            pe.matmul(bank[1][:, 0:E * NT], upper[:, :], small_mask, start=True, stop=True)
            pe.matmul(bank[1][:, E * NT:2 * E * NT], ones[:, :], small_mask, start=True, stop=True).then_inc(rank_ps, 1)
            pe.wait_ge(q_sb, 2 * NT)

            for b in range(NB):
                pe.wait_ge(kvm_r, b + 1)
                for r in range(2):
                    for g in range(2):
                        last = pe.matmul(bank[5 + b][64 * g:64 * g + 64, r * D:(r + 1) * D],
                                         a_kvm[b][g][:, r * 64:(r + 1) * 64], wo0_s[:, g, :], start=True, stop=True)
                last.then_inc(m_ps, 1)

            def step_b(s, batch):
                pe.wait_ge(ql_in[s.par], 16 * (s.half + 1))
                pe.wait_ge(m_sb, batch + 1)
                if s.at_least(2):
                    pe.wait_ge(ao_sb, s.t - 1)
                for r in range(2):
                    last = pe.matmul(bank[2 + s.par][:, 0:D], a_q[:, s.par, r, :], m_all[batch][:, r, :],
                                     start=r == 0, stop=r == 1)
                last.then_inc(ao_ps, 1)

            for batch in range(NB):
                lo = batch * BT // 2
                if batch == 0:
                    step_b(Step(0, 0), 0)
                    step_b(Step(0, 1), 0)
                    lo = 1
                with pe.Fori(lo, (batch + 1) * BT // 2) as m:
                    for par in range(2):
                        step_b(Step(m, par), batch)

            pe.wait_ge(hot_r, 1)
            for n in range(TOPK * NT):
                last = pe.matmul(bank[0][:, 0:2 * ST0], hot_lo[:, n, :], hot_hi[:, n, :],
                                 start=n == 0, stop=n == TOPK * NT - 1)
            last.then_inc(inv_ps, 1)
            pe.wait_ge(w0_in, 16 * 2 * E)
            end_stage(pe, 1)

            regs = [None, None]

            def step_c(s):
                if s.at_least(1) and in_range(s.back(1), ST0):
                    b = s.back(1)
                    e1 = pe.value_load(tile_e[0:1, ds(b.t, 1)], min_val=0, max_val=E - 1)
                    pe.wait_ge(cT_sb, b.t + 1)
                    if b.at_least(2):
                        pe.wait_ge(relu_sb, b.t - 1)
                    for c in range(DC):
                        last = pe.matmul(bank[1 + b.par][:, :], c_xT[:, b.par, c, :],
                                         r1[:, ds(e1, 1), c * H:(c + 1) * H], start=c == 0, stop=c == DC - 1)
                    last.then_inc(h_ps, 1)
                if in_range(s, ST0):
                    pe.wait_ge(xg_in[s.par], 16 * (s.half + 1))
                    if s.at_least(1):
                        pe.wait_ge(cT_sb, s.t)
                    for c in range(DC):
                        last = pe.transpose(bank[0][:, c * P:(c + 1) * P], c_xg[:, s.par, c * P:(c + 1) * P], ident[:, :])
                    last.then_inc(cT_ps, 1)
                if s.at_least(2) and in_range(s.back(2), ST0):
                    b = s.back(2)
                    e2 = pe.value_load(tile_e[0:1, ds(b.t, 1)], min_val=0, max_val=E - 1)
                    pe.wait_ge(hT_sb, b.t + 1)
                    if b.at_least(2):
                        pe.wait_ge(y_sb, b.t - 1)
                    for c in range(HC):
                        last = pe.matmul(bank[5 + b.par][:, 0:D], c_hT[:, b.par, c, :],
                                         r1[:, ds(e2, 1), DC * H + c * D:DC * H + (c + 1) * D],
                                         start=c == 0, stop=c == HC - 1)
                    last.then_inc(y_ps, 1)
                if s.at_least(1) and in_range(s.back(1), ST0):
                    b = s.back(1)
                    pe.wait_ge(h_sb, b.t + 1)
                    if b.at_least(2):
                        pe.wait_ge(hT_sb, b.t - 1)
                    for c in range(HC):
                        last = pe.transpose(bank[3 + b.par][:, c * P:(c + 1) * P], c_h[:, b.par, c * P:(c + 1) * P],
                                            ident[:, :])
                    last.then_inc(hT_ps, 1)

            for t in range(4):
                step_c(Step(t // 2, t % 2))
            with pe.Fori(2, ST0 // 2) as m:
                for par in range(2):
                    step_c(Step(m, par))
            for t in (ST0, ST0 + 1):
                step_c(Step(t // 2, t % 2))
            end_stage(pe, 2)

            def step_d(s):
                if s.at_least(1) and in_range(s.back(1), NT):
                    b = s.back(1)
                    xT = d_xT[:, b.par, :, :]
                    pe.wait_ge(sd.xT, b.t + 1)
                    if b.at_least(2):
                        pe.wait_ge(qk1_sb, 4 * (b.t - 1))
                    for j in range(2 * DC):
                        for c in range(DC):
                            last = pe.matmul(bank[1 + b.par][:, j * P:(j + 1) * P], wqkv1_s[:, c, j * P:(j + 1) * P],
                                             xT[:, c, :], start=c == 0, stop=c == DC - 1)
                    last.then_inc(qk1_ps, 1)
                if in_range(s, NT):
                    transpose_x(sd, s, d_xn)
                if s.at_least(1) and in_range(s.back(1), NT):
                    if b.at_least(2):
                        pe.wait_ge(v1_sb, b.t - 1)
                    for c in range(DC):
                        last = pe.matmul(bank[3 + b.par][:, 0:D], xT[:, c, :], wqkv1_s[:, c, 2 * D:3 * D],
                                         start=c == 0, stop=c == DC - 1)
                    last.then_inc(v1_ps, 1)
                    if b.at_least(1):
                        pe.wait_ge(sc_sb, b.t)
                    for c in range(DC):
                        last = pe.matmul(bank[5][:, 0:E], xT[:, c, :], wg1_s[:, c, :], start=c == 0, stop=c == DC - 1)
                    last.then_inc(sc_ps, 1)

            for t in range(4):
                step_d(Step(t // 2, t % 2))
            with pe.Fori(2, NT // 2) as m:
                for par in range(2):
                    step_d(Step(m, par))
            step_d(Step(NT // 2, 0))
            end_stage(pe, 3)

            def step_e(s):
                if in_range(s, NT):
                    pe.wait_ge(qkl[s.par], 16 * (s.half + 1))
                    if s.at_least(1):
                        pe.wait_ge(sub_r, s.t)
                    for j in range(2):
                        for b in range(2):
                            for g in range(4):
                                last = pe.matmul(banks47[BLK * b:BLK * b + BLK, g, BLK * j:BLK * j + BLK],
                                                 e_qk[DK * g:DK * g + DK, s.par, j, BLK * b:BLK * b + BLK],
                                                 e_qk[DK * g:DK * g + DK, s.par, DC + j, BLK * b:BLK * b + BLK],
                                                 start=True, stop=True, tile_position=(DK * g, BLK * b))
                    last.then_inc(s_ps, 1)
                if s.at_least(2) and in_range(s.back(2), NT):
                    b = s.back(2)
                    pe.wait_ge(o_sb, b.t + 1)
                    if b.at_least(1):
                        pe.wait_ge(oT_sb, b.t)
                    for c in range(DC):
                        last = pe.transpose(bank[2][:, c * P:(c + 1) * P], e_o[:, b.par, c * P:(c + 1) * P], ident[:, :])
                    last.then_inc(oT_ps, 1)
                if s.at_least(1) and in_range(s.back(1), NT):
                    b = s.back(1)
                    pe.wait_ge(p_r, b.t + 1)
                    if b.at_least(1):
                        pe.wait_ge(pT_sb, b.t)
                    for g in range(NP):
                        last = pe.transpose(bank[0][:, g * P:(g + 1) * P],
                                            e_p[:, b.par, 2 * g:2 * g + 2, :], ident[:, :])
                    last.then_inc(pT_ps, 1)
                if s.at_least(3) and in_range(s.back(3), NT):
                    b = s.back(3)
                    pe.wait_ge(oT_sb, b.t + 1)
                    if b.at_least(1):
                        pe.wait_ge(y1_sb, b.t)
                    pe.wait_ge(cnt_used, b.t + 3 if not (isinstance(b.half, int) and b.t + 3 > NT) else NT)
                    for c in range(DC):
                        last = pe.matmul(bank[3][:, 0:D], e_oT[:, b.par, c, :], wo1_s[:, c, :],
                                         start=c == 0, stop=c == DC - 1)
                    last.then_inc(y1_ps, 1)
                if s.at_least(1) and in_range(s.back(1), NT):
                    b = s.back(1)
                    pe.wait_ge(vl[b.par], 64 * (b.half + 1))
                    pe.wait_ge(pT_sb, b.t + 1)
                    if b.at_least(1):
                        pe.wait_ge(o_sb, b.t)
                    for k in range(2):
                        for g in range(NP):
                            last = pe.matmul(bank[1][BLK * k:BLK * k + BLK, g * 64:(g + 1) * 64],
                                             e_pT[:, g, BLK * k:BLK * k + BLK],
                                             e_v[:, b.par, k, :, DK * g:DK * g + DK], start=True, stop=True)
                    last.then_inc(o_ps, 1)
                if in_range(s, NT):
                    pe.wait_ge(part_r, s.t + 1)
                    if s.at_least(3):
                        pe.wait_ge(y1_sb, s.t - 2)
                    pe.matmul(bank[3][:, D:D + E], ones[:, :], e_part[:, s.par, :], start=True, stop=True)\
                      .then_inc(cnt_ps, 1)

            for t in range(4):
                step_e(Step(t // 2, t % 2))
            with pe.Fori(2, NT // 2) as m:
                for par in range(2):
                    step_e(Step(m, par))
            for t in (NT, NT + 1, NT + 2):
                step_e(Step(t // 2, t % 2))

            pe.wait_ge(both_r, 1)
            for k, w in enumerate((upper, ones)):
                last = pe.matmul(bank[k][:, :], w[:, :], s_both, start=True, stop=True)
            last.then_inc(rank1_ps, 1)
            pe.wait_ge(z_r, 1)
            pe.matmul(bank[2][:, 0:E], onesf, s_zp, start=True, stop=True).then_inc(z_ps, 1)
            pe.wait_ge(hot1_r, 1)
            for q in range(2):
                for c in range(NT):
                    last = pe.matmul(bank[4 + q][:, 0:128], hot1_hi[:, c, q * P:(q + 1) * P],
                                     hot1_lo[:, c, :, q * 4:(q + 1) * 4, :],
                                     start=c == 0, stop=c == NT - 1)
            last.then_inc(inv1_ps, 1)
            end_stage(pe, 4)

            def transpose_f(s):
                pe.wait_ge(fx_in[s.par], 16 * TE * (s.half + 1))
                if s.at_least(1):
                    pe.wait_ge(fT_sb, 2 * s.t)
                for c in range(DC):
                    for i in range(TE):
                        last = pe.transpose(bank[4 + c][:, i * P:(i + 1) * P],
                                            f_xg[:, s.par, i, c * P:(c + 1) * P], ident[:, :])
                last.then_inc(fT_ps, 1)

            def step_f(s, more=True):
                pe.wait_ge(fw_in[s.par], 32 * (s.half + 1))
                pe.wait_ge(fT_sb, 2 * (s.t + 1))
                w = f_w[s.par]
                for hb in range(HC):
                    if hb >= 2 or s.at_least(1):
                        pe.wait_ge(hh_r, HC * s.t + hb - 1)
                    for k in range(2):
                        for c in range(DC):
                            o = c * 2 * H + k * H + hb * P
                            last = pe.matmul(bank[2 * (hb % 2) + k][:, :], w[:, o:o + P], f_xT[:, s.par, c, :],
                                             start=c == 0, stop=c == DC - 1)
                    last.then_inc(h13_ps, 1)
                if more:
                    transpose_f(Step(s.half + s.par, 1 - s.par))
                pe.wait_ge(hh_r, HC * (s.t + 1))
                for i in range(TE):
                    if i >= 2 or s.at_least(1):
                        pe.wait_ge(fy_sb, TE * s.t + i - 1)
                    for c in range(HC):
                        last = pe.matmul(bank[6 + i % 2][:, 0:D], f_h[:, s.par, c, i * P:(i + 1) * P],
                                         w[:, 2 * DC * H + c * D:2 * DC * H + (c + 1) * D],
                                         start=c == 0, stop=c == HC - 1)
                    last.then_inc(fy_ps, 1)

            transpose_f(Step(0, 0))
            step_f(Step(0, 0))
            step_f(Step(0, 1))
            with pe.Fori(1, E // 2 - 1) as m:
                for par in range(2):
                    step_f(Step(m, par))
            step_f(Step(E // 2 - 1, 0))
            step_f(Step(E // 2 - 1, 1), more=False)

        @block.scalar
        def _(act):
            def sqrt_and_copy(z, s, mv, sdv, xT):
                act.wait_ge(z.moments, s.t + 1)
                act.activation(sdv[:, s.par, :], mv[:, s.par, 1:2], ACT.Sqrt, bias=eps_c[:, :]).then_inc(z.std, 1)

            def copy_xT(z, s, xT, users):
                act.wait_ge(z.xT_ps, s.t + 1)
                for u, n in users:
                    if s.at_least(2):
                        act.wait_ge(u, n * (s.t - 1))
                act.activation(xT[:, s.par, :, :], bank[0][:, 0:D], ACT.Copy).then_inc(z.xT, 1)

            act.wait_ge(made, 1)
            act.wait_ge(consts, 16 * 9)

            def step_a(s):
                if in_range(s, NT):
                    sqrt_and_copy(sa, s, a_mv, a_sd, a_xT)
                    copy_xT(sa, s, a_xT, [(lg_ps, 1)])
                if s.at_least(1) and in_range(s.back(1), NT):
                    b = s.back(1)
                    act.wait_ge(q_ps, b.t + 1)
                    if b.at_least(2):
                        act.wait_ge(qprod, b.t - 1)
                    for r in range(DC):
                        act.activation(a_q[:, b.par, r, :], bank[5 + b.par][:, r * P:(r + 1) * P], ACT.Identity,
                                       bias=bq0_s[:, r:r + 1]).then_inc(q_sb, 1)
                    act.wait_ge(lg_ps, b.t + 1)
                    if b.at_least(2):
                        act.wait_ge(top_m, b.t - 1)
                    act.activation(a_lg[:, b.par, :], bank[7][:, 0:E], ACT.Copy).then_inc(lg_sb, 1)

            for t in range(4):
                step_a(Step(t // 2, t % 2))
            with act.Fori(2, NT // 2) as m:
                for par in range(2):
                    step_a(Step(m, par))
            step_a(Step(NT // 2, 0))

            act.wait_ge(d_sb, 1)
            act.activation(top_e, top_d, ACT.Exp).then_inc(e_sb, 1)
            for b in range(NB):
                act.wait_ge(m_ps, b + 1)
                act.activation(m_all[b], bank[5 + b][:, :], ACT.Copy).then_inc(m_sb, 1)
            end_stage(act, 1)

            def step_c(s):
                if s.at_least(1) and in_range(s.back(1), ST0):
                    b = s.back(1)
                    act.wait_ge(h_ps, b.t + 1)
                    if b.at_least(2):
                        act.wait_ge(h_sb, b.t - 1)
                    act.activation(c_r[:, b.par, :], bank[1 + b.par][:, :], ACT.Relu).then_inc(relu_sb, 1)
                if in_range(s, ST0):
                    act.wait_ge(cT_ps, s.t + 1)
                    if s.at_least(2):
                        act.wait_ge(h_ps, s.t - 1)
                    act.activation(c_xT[:, s.par, :, :], bank[0][:, 0:D], ACT.Copy).then_inc(cT_sb, 1)
                if s.at_least(1) and in_range(s.back(1), ST0):
                    act.wait_ge(hT_ps, b.t + 1)
                    if b.at_least(2):
                        act.wait_ge(y_ps, b.t - 1)
                    act.activation(c_hT[:, b.par, :, :], bank[3 + b.par][:, :], ACT.Copy).then_inc(hT_sb, 1)

            for t in range(4):
                step_c(Step(t // 2, t % 2))
            with act.Fori(2, ST0 // 2) as m:
                for par in range(2):
                    step_c(Step(m, par))
            step_c(Step(ST0 // 2, 0))
            end_stage(act, 2)

            def step_d(s):
                if in_range(s, NT):
                    sqrt_and_copy(sd, s, d_mv, d_sd, d_xT)
                    copy_xT(sd, s, d_xT, [(sc_ps, 1)])
                if s.at_least(1) and in_range(s.back(1), NT):
                    b = s.back(1)
                    act.wait_ge(qk1_ps, b.t + 1)
                    for j in range(2 * DC):
                        act.activation(qk_all[:, j, ds(b.t * P, P)], bank[1 + b.par][:, j * P:(j + 1) * P],
                                       ACT.Identity, bias=bqk1_s[:, j:j + 1]).then_inc(qk1_sb, 1)
                    act.wait_ge(sc_ps, b.t + 1)
                    if b.at_least(2):
                        act.wait_ge(sc_kept, b.t - 1)
                        act.wait_ge(sc_out[b.par], 16 * b.half)
                    act.activation(d_sc[:, b.par, :], bank[5][:, 0:E], ACT.Copy).then_inc(sc_sb, 1)

            for t in range(4):
                step_d(Step(t // 2, t % 2))
            with act.Fori(2, NT // 2) as m:
                for par in range(2):
                    step_d(Step(m, par))
            step_d(Step(NT // 2, 0))
            end_stage(act, 3)

            def step_e(s):
                if s.at_least(2) and in_range(s.back(2), NT):
                    b = s.back(2)
                    act.wait_ge(oT_ps, b.t + 1)
                    if b.at_least(2):
                        act.wait_ge(y1_ps, b.t - 1)
                    act.activation(e_oT[:, b.par, :, :], bank[2][:, 0:D], ACT.Copy).then_inc(oT_sb, 1)
                if s.at_least(1) and in_range(s.back(1), NT):
                    b = s.back(1)
                    act.wait_ge(pT_ps, b.t + 1)
                    if b.at_least(1):
                        act.wait_ge(o_ps, b.t)
                    act.activation(e_pT[:, :, :], bank[0][:, :], ACT.Copy).then_inc(pT_sb, 1)
                if in_range(s, NT):
                    act.wait_ge(sub_r, s.t + 1)
                    if s.at_least(2):
                        act.wait_ge(pT_ps, s.t - 1)
                        act.wait_ge(sum_r, s.t - 1)
                    act.activation(e_p[:, s.par, :, :], e_s[:, :, :], ACT.Exp, scale=DK ** -0.5).then_inc(p_r, 1)
                if s.at_least(3) and in_range(s.back(3), NT):
                    b = s.back(3)
                    act.wait_ge(y1_ps, b.t + 1)
                    if b.at_least(2):
                        act.wait_ge(fin_out[b.par], 16 * b.half)
                    act.activation(e_y[:, b.par, :], bank[3][:, 0:D], ACT.Copy).then_inc(y1_sb, 1)

            for t in range(6):
                step_e(Step(t // 2, t % 2))
            with act.Fori(3, NT // 2) as m:
                for par in range(2):
                    step_e(Step(m, par))
            for t in (NT, NT + 1, NT + 2):
                step_e(Step(t // 2, t % 2))

            act.wait_ge(ngm_r, 1)
            for e in range(E):
                last = act.activation(s_exp[:, e, :], sc_all[:, e, :], ACT.Exp, bias=nscmax[:, e:e + 1])
            last.then_inc(ex_r, 1)
            end_stage(act, 4)

            def copy_fT(s):
                act.wait_ge(fT_ps, s.t + 1)
                if s.at_least(2):
                    act.wait_ge(h13_ps, HC * (s.t - 1))
                for c in range(DC):
                    act.activation(f_xT[:, s.par, c, :], bank[4 + c][:, :], ACT.Copy).then_inc(fT_sb, 1)

            def step_f(s, e, more=True):
                for hb in range(HC):
                    act.wait_ge(h13_ps, HC * s.t + hb + 1)
                    if hb >= 2 or s.at_least(1):
                        act.wait_ge(hh_r, HC * s.t + hb - 1)
                    act.activation(f_g[:, hb % 2, :], bank[2 * (hb % 2)][:, :], ACT.Silu).then_inc(g_r, 1)
                act.wait_ge(fx_in[s.par], 16 * TE * (s.half + 1))
                if s.at_least(2):
                    act.wait_ge(fwg_r, s.t - 1)
                act.activation(f_we[:, s.par, :].unsqueeze(2), f_xg[:, s.par, :, ds(D + e, 1)], ACT.Exp,
                               bias=nscmax[:, ds(e, 1)]).then_inc(fwe_r, 1)
                if more:
                    copy_fT(Step(s.half + s.par, 1 - s.par))

            copy_fT(Step(0, 0))
            step_f(Step(0, 0), 0)
            step_f(Step(0, 1), 1)
            with act.Fori(1, E // 2 - 1) as m:
                for par in range(2):
                    step_f(Step(m, par), 2 * m + par)
            step_f(Step(E // 2 - 1, 0), E - 2)
            step_f(Step(E // 2 - 1, 1), E - 1, more=False)

        @block.vector
        def _(dve):
            chain = [0]

            def link(ins):
                chain[0] += 1
                ins.then_inc(seq, 1)
                dve.wait_ge(seq, chain[0])

            def stats(z, s, xt, st):
                dve.wait_ge(z.x_in[s.par], 16 * (s.half + 1))
                dve.bn_stats(st[:, s.par, :], xt[:, s.par, :]).then_inc(z.stats, 1)

            def moments(z, s, st, mv):
                dve.bn_aggr(mv[:, s.par, :], st[:, s.par, :]).then_inc(z.moments, 1)

            def normalise(z, s, xt, mv, sdv, rs, xn):
                dve.wait_ge(z.std, s.t + 1)
                dve.reciprocal(rs[:, s.par, :], sdv[:, s.par, :]).then_inc(z.rstd, 1)
                dve.wait_ge(z.rstd, s.t + 1)
                if s.at_least(2):
                    dve.wait_ge(z.xT_ps, s.t - 1)
                    dve.wait_ge(z.xn_out[s.par], 16 * s.half)
                dve.tensor_scalar(xn[:, s.par, :], xt[:, s.par, :], mv[:, s.par, 0:1], rs[:, s.par, :],
                                  ALU.subtract, ALU.mult).then_inc(z.xn, 1)

            dve.wait_ge(made, 1)
            dve.wait_ge(consts, 16 * 9)

            def step_a(s, second=False):
                if in_range(s, NT):
                    stats(sa, s, a_x, a_st)
                    if not s.at_least(2):
                        dve.wait_ge(sa.stats, s.t + 1)
                        moments(sa, s, a_st, a_mv)
                if s.at_least(2) and in_range(s.back(2), NT):
                    b = s.back(2)
                    tb = b.t - BT if second else b.t
                    dve.wait_ge(kv_ps, b.t + 1)
                    dve.wait_ge(lg_sb, b.t + 1)
                    if b.at_least(2):
                        dve.wait_ge(st_ps, b.t - 1)
                    if in_range(s, NT):
                        dve.wait_ge(sa.stats, s.t + 1)
                    kv = a_kv[:, b.par, :]
                    dve.tensor_tensor(kv, bank[1 + b.par][:, :], bkv0_s[:, :], ALU.add).then_inc(kv_sb, 1)
                    if in_range(s, NT):
                        moments(sa, s, a_st, a_mv)
                    dve.max(a_top[:, b.par, :], a_lg[:, b.par, :]).then_inc(top_done, 1)
                    dve.wait_ge(kv_sb, b.t + 1)
                    dve.wait_ge(top_done, b.t + 1)
                    k4 = kv[:, 0:D].rearrange("p (r h j) -> p r h j", r=2, h=NH0)
                    t4 = [a_t[:, i, :].rearrange("p (r h j) -> p r h j", r=2, h=NH0) for i in range(2)]
                    cos = cosk_s[:, ds(tb * JR, JR)]
                    for r in range(2):
                        sin = sink_s[:, ds(tb * 2 * JR + r * JR, JR)]
                        dve.tensor_tensor(t4[0][:, r], k4[:, r], over_mid(cos, NH0), ALU.mult).then_inc(kprod, 1)
                        dve.tensor_tensor(t4[1][:, r], k4[:, 1 - r], over_mid(sin, NH0), ALU.mult).then_inc(kprod, 1)
                    dve.max_index(a_ti[:, b.par, :].bitcast(U32), a_top[:, b.par, :], a_lg[:, b.par, :]).then_inc(top_m, 1)
                    dve.wait_ge(kprod, 4 * (b.t + 1))
                    dve.tensor_tensor(a_kr[:, b.par, :], a_t[:, 0, :], a_t[:, 1, :], ALU.add).then_inc(krot, 1)
                    dve.tensor_copy(top_v[:, ds(b.t * TOPK, TOPK)], a_top[:, b.par, 0:TOPK]).then_inc(top_kept, 1)
                    dve.wait_ge(top_m, b.t + 1)
                    dve.tensor_copy(top_i[:, ds(b.t * TOPK, TOPK)], a_ti[:, b.par, 0:TOPK].bitcast(U32)).then_inc(top_kept, 1)
                if in_range(s, NT):
                    normalise(sa, s, a_x, a_mv, a_sd, a_rs, a_xn)

            for t in range(4):
                step_a(Step(t // 2, t % 2))
            with dve.Fori(2, 9) as m:
                for par in range(2):
                    step_a(Step(m, par))
            step_a(Step(9, 0), second=True)
            for g in range(2):
                dve.wait_ge(st_ps, BT)
                last = dve.tensor_tensor(a_kvm[0][g], bank[3 + g][:, 0:P], headmask[:, :, :].rearrange("p a b -> p (a b)"),
                                         ALU.mult)
            last.then_inc(kvm_r, 1)
            step_a(Step(9, 1), second=True)
            with dve.Fori(10, NT // 2) as m:
                for par in range(2):
                    step_a(Step(m, par), second=True)
            for t in (32, 33):
                step_a(Step(t // 2, t % 2), second=True)
            for g in range(2):
                dve.wait_ge(st_ps, NT)
                last = dve.tensor_tensor(a_kvm[1][g], bank[3 + g][:, 0:P], headmask[:, :, :].rearrange("p a b -> p (a b)"),
                                         ALU.mult)
            last.then_inc(kvm_r, 1)

            dve.wait_ge(qrot, NT)
            dve.wait_ge(top_kept, TOPK * NT)
            tv, ti = (v[:, :].rearrange("p (t k) -> p t k", k=TOPK) for v in (top_v, top_i))
            for par in range(2):
                dve.wait_ge(sa.xn_out[par], 16 * (NT // 2))
            link(dve.tensor_tensor(top_d, tv[:, :, 1], tv[:, :, 0], ALU.subtract))
            dve.sem_inc(d_sb, 1)
            for k in range(TOPK):
                link(dve.tensor_tensor(m_k[k], over_last(iota_e[:, :], NT), over_mid(ti[:, :, k], E), ALU.is_equal))
            dve.tensor_tensor(small_mask.rearrange("p (e t) -> p e t", e=E), m_k[0], m_k[1], ALU.add).then_inc(mask_r, 1)
            dve.wait_ge(e_sb, 1)
            link(dve.tensor_scalar(top_w[:, 0, :], top_e, 1.0, None, ALU.add))
            link(dve.reciprocal(top_w[:, 0, :], top_w[:, 0, :]))
            link(dve.tensor_tensor(top_w[:, 1, :], top_w[:, 0, :], top_e, ALU.mult))
            for k in range(TOPK):
                link(dve.tensor_tensor(r_tmp[k], m_k[k], over_mid(top_w[:, k, :], E), ALU.mult))
            dve.tensor_tensor(a_kv[:, 0, 0:NT * E].rearrange("p (t e) -> p e t", t=NT), r_tmp[0], r_tmp[1], ALU.add)\
               .then_inc(gates_r, 1)
            dve.wait_ge(rank_ps, 1)
            rank_v = bank[1][:, 0:E * NT].rearrange("p (e t) -> p e t", e=E)
            tot_v = bank[1][:, E * NT:2 * E * NT]
            link(dve.tensor_tensor_scan(incl.rearrange("p e t -> p (e t)"), not_first[:, :, :].rearrange("p e t -> p (e t)"),
                                        tot_v, 0.0, ALU.mult, ALU.add))
            link(dve.tensor_tensor(excl, incl, tot_v.rearrange("p (e t) -> p e t", e=E), ALU.subtract))
            link(dve.tensor_tensor(r_tmp[0], over_last(incl[:, :, NT - 1], NT), over_mid(iota_128m[:, :], E), ALU.is_gt))
            link(dve.tensor_reduce(n_tiles, r_tmp[0], AX, ALU.add))
            link(dve.tensor_tensor_scan(t_incl, one8[:, :], n_tiles, 0.0, ALU.mult, ALU.add))
            link(dve.tensor_tensor(t_excl, t_incl, n_tiles, ALU.subtract))
            link(dve.tensor_tensor(excl, excl, rank_v, ALU.add))
            link(dve.scalar_tensor_tensor(excl, over_last(t_excl, NT), float(P), excl, ALU.mult, ALU.add))
            for k in range(TOPK):
                link(dve.tensor_tensor(r_tmp[k], m_k[k], excl, ALU.mult))
                link(dve.tensor_reduce(slot_f[:, k, :], r_tmp[k].rearrange("p e t -> p t e"), AX, ALU.add))
            link(dve.tensor_copy(slot_i[:, 0, :], slot_f.rearrange("p k t -> p (k t)")))
            link(dve.tensor_scalar(slot_i[:, 1, :], slot_i[:, 0, :], 7, None, ALU.logical_shift_right))
            link(dve.tensor_scalar(slot_i[:, 0, :], slot_i[:, 0, :], P - 1, None, ALU.bitwise_and))
            link(dve.tensor_copy(slot_lh.rearrange("p a n -> p (a n)"), slot_i.rearrange("p a n -> p (a n)")))
            for n in range(TOPK * NT):
                dve.tensor_scalar(hot_lo[:, n, :], iota_p[:, :], slot_lh[:, 0, n:n + 1], None, ALU.is_equal)
                dve.tensor_scalar(hot_hi[:, n, 0:ST0], iota_t[:, :], slot_lh[:, 1, n:n + 1], pid1[:, :],
                                  ALU.is_equal, ALU.mult)
                last = dve.tensor_scalar(hot_hi[:, n, ST0:2 * ST0], iota_t[:, :], slot_lh[:, 1, n:n + 1],
                                         cval[:, n:n + 1], ALU.is_equal, ALU.mult)
            last.then_inc(hot_r, 1)
            t1 = r_big[:, 0:ST0 * E].rearrange("p (j e) -> p j e", e=E)
            t2 = r_big[:, ST0 * E:2 * ST0 * E].rearrange("p (j e) -> p j e", e=E)
            link(dve.tensor_tensor(t1, over_last(iota_t[:, :], E), over_mid(t_incl, ST0), ALU.is_ge))
            link(dve.tensor_tensor(t2, over_last(iota_t[:, :], E), over_mid(t_excl, ST0), ALU.is_ge))
            link(dve.tensor_tensor(tile_1h[:, :].rearrange("p (j e) -> p j e", e=E), t2, t1, ALU.subtract))
            link(dve.tensor_reduce(te_f, t1, AX, ALU.add))
            link(dve.tensor_scalar(tile_e[:, :], te_f, float(E - 1), None, ALU.min))

            def step_b(s):
                dve.wait_ge(ao_ps, s.t + 1)
                dve.wait_ge(xb_in[s.par], 16 * (s.half + 1))
                if s.at_least(2):
                    dve.wait_ge(x1_out[s.par], 16 * s.half)
                dve.tensor_tensor(a_xn[:, s.par, :], bank[2 + s.par][:, 0:D], a_xb[:, s.par, :], ALU.add)\
                   .then_inc(ao_sb, 1)

            step_b(Step(0, 0))
            step_b(Step(0, 1))
            with dve.Fori(1, NT // 2) as m:
                for par in range(2):
                    step_b(Step(m, par))

            dve.wait_ge(inv_ps, 1)
            link(dve.tensor_copy(inv_f, bank[0][:, 0:2 * ST0]))
            link(dve.tensor_scalar(inv_z, inv_f[:, 0:ST0], 0.0, BIG, ALU.is_equal, ALU.mult))
            link(dve.scalar_tensor_tensor(inv_z, inv_f[:, ST0:2 * ST0], float(P), inv_z, ALU.mult, ALU.add))
            link(dve.scalar_tensor_tensor(idx0[:, :], inv_f[:, 0:ST0], -1.0, inv_z, ALU.add, ALU.add))
            end_stage(dve, 1)

            def step_c(s):
                if s.at_least(1) and in_range(s.back(1), ST0):
                    b = s.back(1)
                    dve.wait_ge(relu_sb, b.t + 1)
                    if b.at_least(2):
                        dve.wait_ge(hT_ps, b.t - 1)
                    dve.tensor_tensor(c_h[:, b.par, :], c_r[:, b.par, :], c_r[:, b.par, :], ALU.mult).then_inc(h_sb, 1)
                if in_range(s, ST0):
                    dve.wait_ge(xg_in[s.par], 16 * (s.half + 1))
                    dve.scalar_tensor_tensor(c_gt[:, s.par, :], c_xg[:, s.par, D:ROW], 1.0, tile_1h[:, ds(s.t * E, E)],
                                             ALU.mult, ALU.mult, accum_out=gate0[:, ds(s.t, 1)]).then_inc(gate_r, 1)
                if s.at_least(2) and in_range(s.back(2), ST0):
                    b = s.back(2)
                    dve.wait_ge(y_ps, b.t + 1)
                    dve.wait_ge(gate_r, b.t + 1)
                    if b.at_least(2):
                        dve.wait_ge(y_out, 16 * (b.t - 1))
                    dve.tensor_scalar(c_y[:, b.par, :], bank[5 + b.par][:, 0:D], gate0[:, ds(b.t, 1)], None, ALU.mult)\
                       .then_inc(y_sb, 1)

            for t in range(4):
                step_c(Step(t // 2, t % 2))
            with dve.Fori(2, ST0 // 2) as m:
                for par in range(2):
                    step_c(Step(m, par))
            for t in (ST0, ST0 + 1):
                step_c(Step(t // 2, t % 2))
            end_stage(dve, 2)

            def step_d(s):
                if in_range(s, NT):
                    stats(sd, s, d_x, d_st)
                    if not s.at_least(2):
                        dve.wait_ge(sd.stats, s.t + 1)
                        moments(sd, s, d_st, d_mv)
                if s.at_least(2) and in_range(s.back(2), NT):
                    b = s.back(2)
                    dve.wait_ge(v1_ps, b.t + 1)
                    if in_range(s, NT):
                        dve.wait_ge(sd.stats, s.t + 1)
                    dve.tensor_tensor(r2[:, ds(b.t * D, D)], bank[3 + b.par][:, 0:D], bv1_s[:, :], ALU.add)\
                       .then_inc(v1_sb, 1)
                    if in_range(s, NT):
                        moments(sd, s, d_st, d_mv)
                    dve.wait_ge(sc_sb, b.t + 1)
                    dve.tensor_copy(sc_all[:, :, ds(b.t, 1)], d_sc[:, b.par, :].unsqueeze(2)).then_inc(sc_kept, 1)
                if in_range(s, NT):
                    normalise(sd, s, d_x, d_mv, d_sd, d_rs, d_xn)

            for t in range(4):
                step_d(Step(t // 2, t % 2))
            with dve.Fori(2, NT // 2) as m:
                for par in range(2):
                    step_d(Step(m, par))
            for t in (NT, NT + 1):
                step_d(Step(t // 2, t % 2))
            dve.wait_ge(sc_kept, NT)
            dve.tensor_reduce(pmax[:, :], sc_all[:, :, :], AX, ALU.max).then_inc(pm_r, 1)
            end_stage(dve, 3)

            def judge(s, first=False):
                dve.wait_ge(cnt_ps, s.t + 1)
                if first:
                    dve.tensor_scalar(flip[:, :], bank[3][:, D:D + E], CAP - 0.5, -1.0, ALU.is_lt, ALU.mult)\
                       .then_inc(cnt_used, 1)
                else:
                    dve.tensor_scalar(got[:, :], bank[3][:, D:D + E], CAP - 0.5, -1.0, ALU.is_ge, ALU.mult)\
                       .then_inc(cnt_used, 1)
                    dve.wait_ge(cnt_used, s.t + 1)
                    dve.scalar_tensor_tensor(key[:, :], got[:, :], bit_i[:, ds(s.t, 1)], key[:, :],
                                             ALU.bitwise_and, ALU.bitwise_or).then_inc(key_r, 1)

            def propose(s, first=False):
                if not first:
                    dve.wait_ge(cnt_used, s.t)
                    dve.wait_ge(key_r, s.t)
                    dve.tensor_scalar(cand[:, :], key[:, :], bit_i[:, ds(s.t, 1)], None, ALU.bitwise_or).then_inc(cand_r, 1)
                    dve.wait_ge(cand_r, s.t)
                    dve.tensor_tensor(thr[:, :], cand[:, :], flip[:, :], ALU.bitwise_xor).then_inc(thr_r, 1)
                dve.wait_ge(thr_r, s.t + 1)
                dve.tensor_tensor(e_cmp[:, :, :], sc_all[:, :, :], over_last(thr[:, :].bitcast(F32), NT),
                                  ALU.is_ge).then_inc(cmp_r, 1)
                dve.wait_ge(cmp_r, s.t + 1)
                with nc.allow_low_precision(reason="counts up to 32 are exact in bfloat16"):
                    dve.tensor_reduce(e_part[:, s.par, :], e_cmp[:, :, :], AX, ALU.add).then_inc(part_r, 1)

            def step_e(s, first=False, second=False):
                if in_range(s, NT):
                    if not first:
                        judge(s.back(1), first=second)
                        if second:
                            link(dve.memset(key[:, :], 0))
                            dve.sem_inc(key_r, 1)
                    propose(s, first=first)
                    dve.wait_ge(s_ps, s.t + 1)
                    sv = banks47[:, :, 0:P].rearrange("p g (j k) -> p g j k", j=2)
                    dve.tensor_reduce(e_mx.rearrange("p (g j) -> p g j", g=4), sv, AX, ALU.max).then_inc(mx_r, 1)
                    dve.wait_ge(mx_r, s.t + 1)
                    if s.at_least(1):
                        dve.wait_ge(p_r, s.t)
                    dve.tensor_tensor(e_s.rearrange("p (g j) k -> p g j k", g=4), sv,
                                      e_mx.rearrange("p (g j) -> p g j", g=4).unsqueeze(3).broadcast_to([P, 4, 2, BLK]),
                                      ALU.subtract).then_inc(sub_r, 1)
                if s.at_least(1) and in_range(s.back(1), NT):
                    b = s.back(1)
                    dve.wait_ge(p_r, b.t + 1)
                    dve.tensor_reduce(e_sum[:, b.par, :], e_p[:, b.par, :, :], AX, ALU.add).then_inc(sum_r, 1)
                    dve.wait_ge(sum_r, b.t + 1)
                    dve.reciprocal(e_rc[:, b.par, :], e_sum[:, b.par, :]).then_inc(rc_r, 1)
                    dve.wait_ge(rc_r, b.t + 1)
                    dve.wait_ge(o_ps, b.t + 1)
                    if b.at_least(2):
                        dve.wait_ge(oT_ps, b.t - 1)
                    dve.tensor_tensor(e_o[:, b.par, :].rearrange("p (h d) -> p h d", h=NH1),
                                      bank[1][:, 0:D].rearrange("p (h d) -> p h d", h=NH1),
                                      over_last(e_rc[:, b.par, :], DK), ALU.mult).then_inc(o_sb, 1)

            link(dve.memset(thr[:, :], 0))
            dve.sem_inc(thr_r, 1)
            step_e(Step(0, 0), first=True)
            step_e(Step(0, 1), second=True)
            step_e(Step(1, 0))
            step_e(Step(1, 1))
            with dve.Fori(2, NT // 2) as m:
                for par in range(2):
                    step_e(Step(m, par))
            judge(Step(NT // 2 - 1, 1))
            step_e(Step(NT // 2, 0))

            dve.wait_ge(key_r, NT)
            link(dve.tensor_tensor(thr[:, :], key[:, :], flip[:, :], ALU.bitwise_xor))
            tau = over_last(thr[:, :].bitcast(F32), NT)
            both = s_both.rearrange("p (k e t) -> p k e t", k=2, e=E)
            link(dve.tensor_tensor(both[:, 0], sc_all[:, :, :], tau, ALU.is_gt))
            link(dve.tensor_tensor(both[:, 1], sc_all[:, :, :], tau, ALU.is_equal))
            dve.sem_inc(both_r, 1)
            dve.wait_ge(rank1_ps, 1)
            for k in range(2):
                tot = bank[1][:, k * E * NT:(k + 1) * E * NT]
                link(dve.tensor_tensor_scan(s_in[k].rearrange("p e t -> p (e t)"),
                                            not_first[:, :, :].rearrange("p e t -> p (e t)"), tot, 0.0, ALU.mult, ALU.add))
                link(dve.tensor_tensor(s_ex[k], s_in[k], tot.rearrange("p (e t) -> p e t", e=E), ALU.subtract))
                link(dve.tensor_tensor(s_ex[k], s_ex[k],
                                       bank[0][:, k * E * NT:(k + 1) * E * NT].rearrange("p (e t) -> p e t", e=E), ALU.add))
            link(dve.tensor_scalar(s_need, s_in[0][:, :, NT - 1], -1.0, float(CAP), ALU.mult, ALU.add))
            need = over_last(s_need, NT)
            link(dve.tensor_tensor(s_in[0], s_ex[1], need, ALU.is_lt))
            link(dve.tensor_tensor(s_in[0], s_in[0], both[:, 1], ALU.mult))
            link(dve.tensor_tensor(s_in[0], s_in[0], both[:, 0], ALU.add))
            link(dve.tensor_tensor(s_ex[1], s_ex[1], need, ALU.min))
            link(dve.tensor_tensor(s_ex[0], s_ex[0], s_ex[1], ALU.add))
            dve.wait_ge(ex_r, 1)
            link(dve.tensor_tensor(s_exp, s_exp, s_in[0], ALU.mult))
            link(dve.tensor_reduce(s_zp, s_exp, AX, ALU.add))
            dve.sem_inc(z_r, 1)
            link(dve.scalar_tensor_tensor(s_ex[0], s_ex[0], -BIG, s_in[0], ALU.add, ALU.mult))
            link(dve.tensor_scalar(s_ex[0], s_ex[0], BIG, None, ALU.add))
            link(dve.tensor_copy(s_ri[0], s_ex[0]))
            link(dve.tensor_scalar(s_ri[1], s_ri[0], 4, None, ALU.logical_shift_right))
            link(dve.tensor_scalar(s_ri[0], s_ri[0], 15, None, ALU.bitwise_and))
            link(dve.tensor_copy(s_ex[1], s_ri[1]))
            link(dve.tensor_copy(s_ex[0], s_ri[0]))
            iota32 = over_mid(iota_p[:, 0:32], E)
            iota16 = over_mid(iota_p[:, 0:16], E)
            for c in range(NT):
                dve.tensor_tensor(hot1_hi[:, c, :].rearrange("p (e k) -> p e k", e=E), iota32,
                                  over_last(s_ex[1][:, :, c], 32), ALU.is_equal)
                last = dve.tensor_tensor(hot1_lo[:, c, 1, :, :], iota16, over_last(s_ex[0][:, :, c], 16),
                                         ALU.is_equal)
            link(last)
            for c in range(NT):
                last = dve.tensor_scalar(hot1_lo[:, c, 0, :, :], hot1_lo[:, c, 1, :, :], pid0[:, :], None, ALU.mult)
            link(last)
            for c in range(NT):
                last = dve.tensor_scalar(hot1_lo[:, c, 1, :, :], hot1_lo[:, c, 1, :, :], float(c), None, ALU.mult)
            link(last)
            dve.sem_inc(hot1_r, 1)
            dve.wait_ge(z_ps, 1)
            dve.reciprocal(rz[:, :], bank[2][:, 0:E]).then_inc(rz_r, 1)
            dve.wait_ge(inv1_ps, 1)
            for q in range(2):
                iv = bank[4 + q][:, 0:128].rearrange("p (k g n) -> p k g n", k=2, g=4)
                link(dve.tensor_copy(s_iv[q], iv))
                for g in range(4):
                    pq = slice(32 * g, 32 * g + 32)
                    link(dve.scalar_tensor_tensor(s_id[pq, q, :], s_iv[q][pq, 1, g, :], float(P), s_iv[q][pq, 0, g, :],
                                                  ALU.mult, ALU.add))
                    for a in range(4):
                        last = dve.tensor_copy(idx1[32 * a:32 * a + 32, 4 * (4 * q + g):4 * (4 * q + g) + 4], s_id[pq, q, 4 * a:4 * a + 4])
            link(last)
            dve.sem_inc(idx1_r, 1)
            end_stage(dve, 4)

            def step_f(s, e):
                for hb in range(HC):
                    dve.wait_ge(g_r, HC * s.t + hb + 1)
                    if s.at_least(2):
                        dve.wait_ge(fy_ps, TE * (s.t - 1))
                    dve.tensor_tensor(f_h[:, s.par, hb, :], f_g[:, hb % 2, :], bank[2 * (hb % 2) + 1][:, :], ALU.mult)\
                       .then_inc(hh_r, 1)
                dve.wait_ge(fwe_r, s.t + 1)
                dve.tensor_scalar(f_wg[:, s.par, :], f_we[:, s.par, :], rz[:, ds(e, 1)], None, ALU.mult).then_inc(fwg_r, 1)
                dve.wait_ge(fwg_r, s.t + 1)
                if s.at_least(1):
                    dve.wait_ge(fy_out, 16 * TE * s.t)
                for i in range(TE):
                    dve.wait_ge(fy_ps, TE * s.t + i + 1)
                    dve.tensor_scalar(f_y[:, i, :], bank[6 + i % 2][:, 0:D], f_wg[:, s.par, i:i + 1], None, ALU.mult)\
                       .then_inc(fy_sb, 1)

            for t in range(2):
                step_f(Step(0, t), t)
            with dve.Fori(1, E // 2) as m:
                for par in range(2):
                    step_f(Step(m, par), 2 * m + par)

        @block.gpsimd
        def _(pool):
            chain = [0]

            def link(ins):
                chain[0] += 1
                ins.then_inc(pseq, 1)
                pool.wait_ge(pseq, chain[0])

            link(pool.memset(ident[:, :], 0.0))
            pool.affine_select(out=ident[:, :], in_=ident[:, :], compare_op=ALU.not_equal, fill=1.0, base=0,
                               pattern=[[-1, P]], channel_multiplier=1)
            pool.memset(eps_c[:, :], EPS)
            link(pool.memset(ones[:, :], 1.0))
            pool.affine_select(out=upper[:, :], in_=ones[:, :], compare_op=ALU.is_gt, fill=0.0, base=0,
                               pattern=[[1, P]], channel_multiplier=-1)
            link(pool.memset(headmask[:, :, :], 0.25))
            hm = headmask[:, :, :].rearrange("p r (h j) -> p r h j", h=8)
            link(pool.affine_select(out=hm, in_=hm, compare_op=ALU.is_ge, fill=0.0, base=0,
                                    pattern=[[0, 2], [-HD0, 8], [0, JR]], channel_multiplier=1))
            link(pool.affine_select(out=hm, in_=hm, compare_op=ALU.is_ge, fill=0.0, base=HD0 - 1,
                                    pattern=[[0, 2], [HD0, 8], [0, JR]], channel_multiplier=-1))
            pool.iota(iota_e[:, :], pattern=[[1, E]], base=0, channel_multiplier=0, allow_small_or_imprecise_dtypes=True)
            pool.iota(iota_p[:, :], pattern=[[1, P]], base=0, channel_multiplier=0, allow_small_or_imprecise_dtypes=True)
            pool.iota(iota_t[:, :], pattern=[[1, ST0]], base=0, channel_multiplier=0, allow_small_or_imprecise_dtypes=True)
            pool.iota(iota_128m[:, :], pattern=[[P, NT]], base=0, channel_multiplier=0, allow_small_or_imprecise_dtypes=True)
            pool.iota(pid1[:, :], pattern=[[0, 1]], base=1, channel_multiplier=1, allow_small_or_imprecise_dtypes=True)
            pool.iota(pid0[:, :], pattern=[[0, 1]], base=0, channel_multiplier=1, allow_small_or_imprecise_dtypes=True)
            pool.iota(cval[:, :], pattern=[[0, TOPK], [1, NT]], base=0, channel_multiplier=0,
                      allow_small_or_imprecise_dtypes=True)
            pool.memset(one8[:, :], 1.0)
            link(pool.memset(not_first[:, :, :], 1.0))
            link(pool.memset(not_first[:, :, 0:1], 0.0))
            for i in range(1, NT):
                last = pool.memset(bit_i[:, i:i + 1], 1 << (NT - 1 - i))
            link(last)
            pool.sem_inc(made, 1)
            last_row = pool.to_reg(N - 1)
            pool.wait_ge(consts, 16 * 9)

            def add_bias(z, s, xt, xb, bo):
                pool.wait_ge(z.x_in[s.par], 16 * (s.half + 1))
                if s.at_least(2):
                    pool.wait_ge(z.xb_out[s.par], 16 * s.half)
                pool.tensor_tensor(xb[:, s.par, :], xt[:, s.par, :], bo[:, :], ALU.add).then_inc(z.xb, 1)

            def step_a(s, second):
                if in_range(s, NT):
                    add_bias(sa, s, a_x, a_xb, bo0_s)
                if s.at_least(2) and in_range(s.back(2), NT):
                    b = s.back(2)
                    tb = b.t - BT if second else b.t
                    pool.wait_ge(q_sb, 2 * (b.t + 1))
                    q = a_q[:, b.par, :, :]
                    t = [a_pt[:, i, :].rearrange("p (r n) -> p r n", r=2) for i in range(2)]
                    cq = cosq_s[:, ds(tb * P, P)]
                    if b.at_least(1):
                        pool.wait_ge(qrot, b.t)
                    for r in range(2):
                        pool.tensor_tensor(t[0][:, r, :], q[:, r, :], cq, ALU.mult)
                        last = pool.tensor_tensor(t[1][:, r, :], q[:, 1 - r, :], sinq_s[:, r, ds(tb * P, P)], ALU.mult)
                    last.then_inc(qprod, 1)
                    pool.wait_ge(qprod, b.t + 1)
                    pool.tensor_tensor(qrot_all[:, :, ds(b.t * P, P)], t[0], t[1], ALU.add).then_inc(qrot, 1)

            for t in range(4):
                step_a(Step(t // 2, t % 2), False)
            with pool.Fori(2, 9) as m:
                for par in range(2):
                    step_a(Step(m, par), False)
            with pool.Fori(9, NT // 2) as m:
                for par in range(2):
                    step_a(Step(m, par), True)
            for t in (32, 33):
                step_a(Step(t // 2, t % 2), True)
            end_stage(pool, 1)

            pool.memset(c_xg, 0.0).then_inc(xg_clear, 1)
            pool.wait_ge(xg_clear, 1)

            def gather(s):
                if s.at_least(2):
                    pool.wait_ge(xg_in[s.par], 16 * s.half)
                pool.tensor_copy(c_gi[:, s.par:s.par + 1], idx0[:, ds(s.t, 1)]).then_inc(gi_r, 1)
                pool.wait_ge(gi_r, s.t + 1)
                if s.at_least(2):
                    pool.wait_ge(cT_ps, s.t - 1)
                    pool.wait_ge(gate_r, s.t - 1)
                pool.nop(nofuse=True)
                pool.indirect_dma_start(c_xg[:, s.par, :], None, xg0_d[:, :],
                                        bass.IndirectOffsetOnAxis(c_gi[:, s.par:s.par + 1], 0),
                                        bounds_check=last_row, oob_is_err=False).then_inc(xg_in[s.par], 16)

            def scatter(s):
                if s.at_least(1):
                    pool.wait_ge(y_out, 16 * s.t)
                pool.tensor_copy(c_si[:, s.par:s.par + 1], idx0[:, ds(s.t, 1)]).then_inc(si_r, 1)
                pool.wait_ge(si_r, s.t + 1)
                pool.wait_ge(y_sb, s.t + 1)
                pool.nop(nofuse=True)
                pool.indirect_dma_start(x1_d[:, :], bass.IndirectOffsetOnAxis(c_si[:, s.par:s.par + 1], 0),
                                        c_y[:, s.par, :], None, bounds_check=last_row, oob_is_err=False,
                                        compute_op=ALU.add).then_inc(y_out, 16)

            for t in range(4):
                gather(Step(t // 2, t % 2))
            for t in (4, 5):
                scatter(Step(0, t - 4))
                gather(Step(2, t - 4))
            with pool.Fori(3, ST0 // 2) as m:
                for par in range(2):
                    s = Step(m, par)
                    scatter(s.back(4))
                    gather(s)
            for t in range(ST0 - 4, ST0):
                scatter(Step(t // 2, t % 2))
            pool.wait_ge(y_out, 16 * ST0)
            end_stage(pool, 2)

            for t in range(2):
                add_bias(sd, Step(0, t), d_x, d_xb, bo1_s)
            with pool.Fori(1, NT // 2) as m:
                for par in range(2):
                    add_bias(sd, Step(m, par), d_x, d_xb, bo1_s)
            end_stage(pool, 3)

            for i in range(2):
                pool.memset(e_v[:, i], 0.0)
            link(pool.memset(onesf, 1.0))
            pool.sem_inc(vz, 1)
            pool.wait_ge(pm_r, 1)
            pool.partition_all_reduce(scmax[:, :], pmax[:, :], P, RMAX).then_inc(gmax_r, 1)
            pool.wait_ge(gmax_r, 1)
            pool.tensor_scalar(nscmax[:, :], scmax[:, :], -1.0, None, ALU.mult).then_inc(ngm_r, 1)

            def add_x(s):
                pool.wait_ge(y1_sb, s.t + 1)
                pool.wait_ge(xbl[s.par], 16 * (s.half + 1))
                pool.tensor_tensor(e_y[:, s.par, :], e_y[:, s.par, :], e_xb[:, s.par, :], ALU.add).then_inc(fin_r, 1)

            with pool.Fori(0, NT // 2) as m:
                for par in range(2):
                    add_x(Step(m, par))
            end_stage(pool, 4)

            def gather1(s, e):
                if s.at_least(2):
                    pool.wait_ge(fT_ps, s.t - 1)
                    pool.wait_ge(fwe_r, s.t - 1)
                if s.at_least(1):
                    pool.wait_ge(fx_in[(s.back(1)).par], 16 * TE * (s.back(1).half + 1))
                pool.tensor_copy(f_gi[:, :], idx1[:, ds(e * TE, TE)]).then_inc(fgi_r, 1)
                pool.wait_ge(fgi_r, s.t + 1)
                for i in range(TE):
                    pool.nop(nofuse=True)
                    pool.indirect_dma_start(f_xg[:, s.par, i, :], None, xg1_d[:, :],
                                            bass.IndirectOffsetOnAxis(f_gi[:, i:i + 1], 0),
                                            bounds_check=last_row, oob_is_err=False).then_inc(fx_in[s.par], 16)

            def scatter1(s, e):
                if s.at_least(1):
                    pool.wait_ge(fy_out, 16 * TE * s.t)
                pool.tensor_copy(f_si[:, :], idx1[:, ds(e * TE, TE)]).then_inc(fsi_r, 1)
                pool.wait_ge(fsi_r, s.t + 1)
                for i in range(TE):
                    pool.wait_ge(fy_sb, TE * s.t + i + 1)
                    pool.nop(nofuse=True)
                    pool.indirect_dma_start(out[:, :], bass.IndirectOffsetOnAxis(f_si[:, i:i + 1], 0),
                                            f_y[:, i, :], None, bounds_check=last_row, oob_is_err=False,
                                            compute_op=ALU.add).then_inc(fy_out, 16)

            gather1(Step(0, 0), 0)
            gather1(Step(0, 1), 1)
            for t in (2, 3):
                gather1(Step(1, t - 2), t)
                scatter1(Step(0, t - 2), t - 2)
            with pool.Fori(2, E // 2) as m:
                for par in range(2):
                    s = Step(m, par)
                    gather1(s, 2 * m + par)
                    scatter1(s.back(2), 2 * m + par - 2)
            for t in (E - 2, E - 1):
                scatter1(Step(t // 2, t % 2), t)


def kernel(**inputs):
    import numpy as np
    import concourse.bacc as bacc
    from concourse.bass_utils import run_bass_kernel_spmd

    a = {k: np.asarray(v) for k, v in inputs.items()}

    pairs = np.arange(D).reshape(NH0 * JR, 2).T.reshape(-1)
    wq, wk, wv = (a["L0_attn_" + n] for n in ("Wq", "Wk", "Wv"))
    heads = np.arange(D).reshape(2, NH1 // 2, DK).transpose(1, 0, 2).reshape(-1)

    scale = np.arange(0, HD0, 2, dtype=np.float32)[:JR]
    with np.errstate(over="ignore"):
        freqs = np.float32(1.0) / np.power(np.float32(10000.0), scale)
    angles = np.arange(L, dtype=np.float32)[:, None] * freqs[None, :]
    cos = np.cos(angles.astype(np.float64)).astype(np.float32)
    sin = np.sin(angles.astype(np.float64)).astype(np.float32)
    signed = np.stack([-sin, sin], axis=1)
    cos_k = cos.reshape(BT, P, JR).transpose(1, 0, 2).reshape(P, BT * JR)
    sin_k = signed.reshape(BT, P, 2, JR).transpose(1, 0, 2, 3).reshape(P, BT * 2 * JR)
    cos_q = np.tile(cos.T, (NH0, 1))
    sin_q = np.tile(signed.transpose(2, 1, 0), (NH0, 1, 1)).reshape(P, 2 * L)

    arrays = {
        "x": a["L0_attn_x"].reshape(N, D),
        "wqkv0": np.concatenate([wq[:, pairs], wk[:, pairs], wv], axis=1),
        "bq0": a["L0_attn_bq"][pairs].reshape(DC, P).T,
        "bkv0": np.concatenate([a["L0_attn_bk"][pairs], a["L0_attn_bv"]]),
        "wo0": a["L0_attn_Wo"], "bo0": a["L0_attn_bo"],
        "rw0": a["L0_ffn_router_w"].T,
        "w1_0": a["L0_ffn_w1"], "w2_0": a["L0_ffn_w2"],
        "wqkv1": np.concatenate([a["L1_attn_Wq"], a["L1_attn_Wk"], a["L1_attn_Wv"]], axis=1),
        "bqk1": np.concatenate([a["L1_attn_bq"], a["L1_attn_bk"]]).reshape(2 * DC, P).T, "bv1": a["L1_attn_bv"],
        "wo1": a["L1_attn_Wo"][heads], "bo1": a["L1_attn_bo"],
        "wg1": a["L1_ffn_Wg"].T,
        "w13_1": np.concatenate([a["L1_ffn_W1"].transpose(0, 2, 1), a["L1_ffn_W3"].transpose(0, 2, 1)], axis=2),
        "w2_1": a["L1_ffn_W2"].transpose(0, 2, 1),
        "cos_q": cos_q, "sin_q": sin_q, "cos_k": cos_k, "sin_k": sin_k,
    }
    arrays = {k: np.ascontiguousarray(v) for k, v in arrays.items()}

    nc = bacc.Bacc("TRN2", target_bir_lowering=False, num_devices=1)
    args = [nc.dram_tensor("in_" + k, v.shape, mybir.dt.from_np(v.dtype), kind="ExternalInput").ap()
            for k, v in arrays.items()]
    args.append(nc.dram_tensor("out_x", (N, D), F32, kind="ExternalOutput").ap())
    two_layers(nc, *args)
    r = run_bass_kernel_spmd(nc, [{"in_" + k: v for k, v in arrays.items()}], core_ids=[0])
    return r.results[0]["out_x"].reshape(NB, L, D)
```

```python
import concourse.bass as bass
from concourse import mybir
from contextlib import ExitStack

F32 = mybir.dt.float32
BF16 = mybir.dt.bfloat16
I32 = mybir.dt.int32
U32 = mybir.dt.uint32
ALU = mybir.AluOpType
ACT = mybir.ActivationFunctionType
AX = mybir.AxisListType.X

P = 128
N, D = 4096, 256
NB, L = 2, 2048
NT = N // P
BT = L // P
DC = D // P
E, H = 8, 512
HC = H // P
TOPK = 2
NH0, HD0 = 16, 16
JR = HD0 // 2
NH1, DK = 8, 32
BLK = 64
CAP = N // E
ST0 = TOPK * N // P + E
ROW = D + E
BIG = 8192.0
EPS = 1e-5
ds = bass.ds
RMAX = bass.bass_isa.ReduceOp.max


def over_last(ap, n):
    return ap.unsqueeze(2).broadcast_to([ap.shape[0], ap.shape[1], n])


def over_mid(ap, n):
    return ap.unsqueeze(1).broadcast_to([ap.shape[0], n, ap.shape[1]])


class Step:

    def __init__(self, half, par):
        self.half, self.par, self.t = half, par, 2 * half + par

    def back(self, k):
        q = self.par - k
        return Step(self.half + (q >> 1), q & 1)

    def at_least(self, k):
        return not isinstance(self.half, int) or self.t >= k


def in_range(s, n):
    return not isinstance(s.half, int) or 0 <= s.t < n


def two_layers(nc, x, wqkv0, bq0, bkv0, wo0, bo0, rw0, w1_0, w2_0,
               wqkv1, bqk1, bv1, wo1, bo1, wg1, w13_1, w2_1, cos_q, sin_q, cos_k, sin_k, out):
    xg0_d = nc.dram_tensor("rows_layer0", [N, ROW], F32).ap()
    xg1_d = nc.dram_tensor("rows_layer1", [N, ROW], F32).ap()
    xb_d = nc.dram_tensor("x_plus_bias", [N, D], F32).ap()
    x1_d = nc.dram_tensor("x_layer1", [N, D], F32).ap()
    xb1_d = nc.dram_tensor("x1_plus_bias", [N, D], F32).ap()

    def rows(dram, t, lo=0, hi=D):
        return dram[ds(t * P, P), lo:hi]

    ctx = ExitStack()
    with ctx:
        def sb(name, shape, dt=F32):
            return ctx.enter_context(nc.sbuf_tensor(name, shape, dt))

        def sem(name):
            return ctx.enter_context(nc.semaphore(name))

        def sem2(name):
            return [sem(name + "_even"), sem(name + "_odd")]

        wqkv0_s = sb("wqkv0_s", [P, DC, 3 * D])
        wo0_s = sb("wo0_s", [P, DC, D])
        wqkv1_s = sb("wqkv1_s", [P, DC, 3 * D])
        wo1_s = sb("wo1_s", [P, DC, D])
        rw0_s = sb("rw0_s", [P, DC, E])
        wg1_s = sb("wg1_s", [P, DC, E])
        bq0_s = sb("bq0_s", [P, DC])
        bqk1_s = sb("bqk1_s", [P, 2 * DC])
        bkv0_s = sb("bkv0_s", [P, 2 * D])
        bv1_s = sb("bv1_s", [P, D])
        bo0_s = sb("bo0_s", [P, D])
        bo1_s = sb("bo1_s", [P, D])
        cosk_s = sb("cosk_s", [P, BT * JR])
        sink_s = sb("sink_s", [P, BT * 2 * JR])
        ident = sb("ident", [P, P])
        headmask = sb("headmask", [P, 2, P // 2])
        eps_c = sb("eps_c", [P, 1])
        upper = sb("upper", [P, P], BF16)
        ones = sb("ones", [P, P], BF16)
        iota_e = sb("iota_e", [P, E])
        iota_p = sb("iota_p", [P, P], BF16)
        iota_t = sb("iota_t", [P, ST0])
        iota_128m = sb("iota_128m", [P, NT])
        pid1 = sb("pid1", [P, 1])
        number1 = sb("number1", [P, TOPK * NT])
        not_first = sb("not_first", [P, E, NT], BF16)
        bit_i = sb("bit_i", [P, NT], I32)

        r1 = sb("r1", [P, E, 2 * DC * H])
        r2 = sb("r2", [P, NT * D])
        r3 = sb("r3", [P, NT * E * 64 + 3 * E * NT], BF16)
        rt = sb("rt", [P, 3 * L])
        rw = sb("rw", [P, 6272])

        qk_all = r1[:, :, :].rearrange("p e n -> p (e n)").rearrange("p (m n) -> p m n", m=4)
        qrot_all = r2[:, :].rearrange("p (c n) -> p c n", c=DC)
        v_all = r2[:, :].rearrange("p (t n) -> p t n", t=NT)
        cosq_s = rt[:, 0:L]
        sinq_s = rt[:, L:3 * L].rearrange("p (r n) -> p r n", r=2)

        top_v = sb("top_v", [P, NT * TOPK])
        top_i = sb("top_i", [P, NT * TOPK])
        pid0 = sb("pid0", [P, 1])
        one8 = sb("one8", [P, E])
        GB = 4
        GN = TOPK * GB
        r3f = r3[:, :].bitcast(F32)
        hot_lo = r3f[:, 0:2 * GN * P].rearrange("p (b n m) -> p b n m", b=2, n=GN)
        o = 2 * GN * P
        hot_hi = r3f[:, o:o + 2 * GN * ST0].rearrange("p (b n m) -> p b n m", b=2, n=GN)
        o += 2 * GN * ST0
        b_q = r3f[:, o:o + 2 * DC * GB * P].rearrange("p (b c n) -> p b c n", b=2, c=DC)
        o += 2 * DC * GB * P
        b_xb = r3f[:, o:o + 2 * GB * D].rearrange("p (b j n) -> p b j n", b=2, j=GB)
        hot1_hi = r3[:, 0:NT * E * 32].rearrange("p (c m) -> p c m", c=NT)
        hot1_lo = r3[:, NT * E * 32:NT * E * 64].rearrange("p (c k e m) -> p c k e m", c=NT, k=2, e=E)

        taken = [0]

        def scratch(shape, dt=F32, reset=False):
            if reset:
                taken[0] = 0
            n = 1
            for k in shape:
                n *= k
            words = n if dt != BF16 else n // 2
            v = rt[:, taken[0]:taken[0] + words]
            taken[0] += words
            assert taken[0] <= 3 * L
            v = v if dt == F32 else v.bitcast(dt)
            if len(shape) == 2:
                v = v.rearrange("p (a b) -> p a b", a=shape[0])
            elif len(shape) == 3:
                v = v.rearrange("p (a b c) -> p a b c", a=shape[0], b=shape[1])
            return v

        m_k = [scratch([E, NT], reset=True), scratch([E, NT])]
        r_tmp = [scratch([E, NT]), scratch([E, NT])]
        incl, excl = scratch([E, NT]), scratch([E, NT])
        m_all = [scratch([2, D]), scratch([2, D])]
        r_big = scratch([2 * ST0 * E])
        small_mask = scratch([E * NT], BF16)
        top_d, top_e, top_w = scratch([NT]), scratch([NT]), scratch([TOPK, NT])
        n_tiles, t_incl, t_excl = scratch([E]), scratch([E]), scratch([E])
        slot_f, slot_i, slot_lh = scratch([TOPK, NT]), scratch([2, TOPK * NT], I32), scratch([2, TOPK * NT])
        te_f, inv_f, inv_z = scratch([ST0]), scratch([ST0]), scratch([ST0])
        gates = scratch([NT, E])
        s_both = scratch([2 * E * NT], BF16, reset=True)
        s_in = [scratch([E, NT]), scratch([E, NT])]
        s_before = scratch([2 * E * NT], BF16)
        s_tot = scratch([E])
        s_ex = [scratch([E, NT]), scratch([E, NT])]
        s_exp = scratch([E, NT])
        s_ri = [scratch([E, NT], I32), scratch([E, NT], I32)]
        s_zp, s_need = scratch([E]), scratch([E])
        s_iv = [scratch([2, 4, 16]), scratch([2, 4, 16])]
        s_id = scratch([2, 16])
        onesf = scratch([P])
        idx0 = sb("idx0", [P, ST0], I32)
        idx1 = sb("idx1", [P, E * (CAP // P)], I32)
        tile_e = sb("tile_e", [P, ST0], I32)
        tile_1h = sb("tile_1h", [P, ST0 * E], BF16)
        gate0 = sb("gate0", [P, ST0])
        tail = r3[:, NT * E * 64:NT * E * 64 + 3 * E * NT]
        sc_all = tail[:, 0:2 * E * NT].bitcast(F32).rearrange("p (e t) -> p e t", e=E)
        e_cmp = tail[:, 2 * E * NT:3 * E * NT].rearrange("p (e t) -> p e t", e=E)

        used = [0]

        def work(shape, reset=False):
            if reset:
                used[0] = 0
            n = 1
            for k in shape:
                n *= k
            v = rw[:, used[0]:used[0] + n]
            used[0] += n
            assert used[0] <= 6272, used[0]
            if len(shape) == 2:
                v = v.rearrange("p (a b) -> p a b", a=shape[0])
            elif len(shape) == 3:
                v = v.rearrange("p (a b c) -> p a b c", a=shape[0], b=shape[1])
            elif len(shape) == 4:
                v = v.rearrange("p (a b c d) -> p a b c d", a=shape[0], b=shape[1], c=shape[2])
            return v

        bank = [ctx.enter_context(nc.psum_tensor(f"bank{i}", [P, 512], F32)) for i in range(4)]
        banks47 = ctx.enter_context(nc.psum_tensor("banks47", [P, 4, 512], F32))
        bank += [banks47[:, i, :] for i in range(4)]

        consts = sem("consts_loaded")
        tables = sem("rotary_tables_of_q_loaded")
        consts_b = sem("late_consts_loaded")
        made = sem("constants_made")
        w0_in = sem("experts0_loaded")
        stage_end = sem("stage_ended")
        seq = sem("vector_chain")
        pseq = sem("pool_chain")

        stages = [0]

        def end_stage(eng, n):
            eng.drain().then_inc(stage_end, 1)
            eng.wait_ge(stage_end, 5 * n)

        block = ctx.enter_context(nc.Block())

        a_x = work([2, D], reset=True)
        a_xn = work([2, D])
        a_xT = work([2, DC, P])
        a_kv = work([2, 2 * D])
        a_kr = work([2, D])
        a_t = work([2, D])
        a_q = work([2, DC, P])
        a_pt = work([2, D])
        a_xb = work([2, D])
        a_lg = work([2, E])
        a_st = work([2, 6])
        a_mv = work([2, 2])
        a_sd = work([2, 1])
        a_rs = work([2, 1])
        a_top = work([2, E])
        a_ti = work([2, E])
        kvm = work([NB, DC, P])
        a_kvm = [[kvm[:, b, g, :] for g in range(DC)] for b in range(NB)]

        b_x1 = work([2, GB, D], reset=True)

        class S:
            pass

        def ln_sems(z):
            s = S()
            s.x_in = sem2(f"x_loaded_{z}")
            s.stats, s.moments, s.std = sem(f"stats_{z}"), sem(f"moments_{z}"), sem(f"std_{z}")
            s.rstd, s.xn = sem(f"rstd_{z}"), sem(f"xn_ready_{z}")
            s.xn_out = sem2(f"xn_stored_{z}")
            s.xb, s.xb_out = sem(f"xb_ready_{z}"), sem2(f"xb_stored_{z}")
            s.xT_ps, s.xT = sem(f"xT_in_psum_{z}"), sem(f"xT_ready_{z}")
            return s

        sa, sd = ln_sems("a"), ln_sems("d")
        kv_ps, kv_sb, lg_ps, lg_sb = sem("kv_in_psum"), sem("kv_ready"), sem("logits_in_psum"), sem("logits_ready")
        q_ps, q_sb = sem("q_in_psum"), sem("q_ready")
        top_m, top_done, top_kept = sem("top_placed"), sem("top_found"), sem("top_kept")
        kprod, krot = sem("k_products"), sem("k_rotated")
        qprod, qrot = sem("q_products"), sem("q_rotated")
        st_ps = sem("ktv_in_psum")

        mask_r, rank_ps = sem("pair_mask_ready"), sem("ranks_in_psum")
        hot_r, inv_ps = sem("one_hots_ready"), sem("slots_in_psum")
        SB = NT // GB
        attn_bank = (2, 3, 4, 7)
        e_sb, d_sb = sem("top_exp_ready"), sem("top_diff_ready")
        gates_r, gates_out = sem("gates_ready"), sem("gates_stored")
        kvm_r, m_ps, m_sb = sem("ktv_masked"), sem("m_in_psum"), sem("m_ready")
        ql_in, xb_in = sem2("q_tile_loaded"), sem2("xb_tile_loaded")
        ao_ps, ao_sb, x1_out = sem("attn0_in_psum"), sem("attn0_added"), sem2("x1_stored")

        c_xg = work([2, ROW], reset=True)
        c_xT = work([2, DC, P])
        c_r = work([2, H])
        c_w1 = work([2, DC, H])
        c_hT = work([2, HC, P])
        c_y = work([2, D])
        c_gt = work([2, E])
        c_gi = sb("c_gi", [P, 2], I32)
        c_si = sb("c_si", [P, 2], I32)
        xg_clear, gi_r, si_r, xg_in = sem("rows_cleared"), sem("gather_index"), sem("scatter_index"), sem2("rows_gathered")
        w1_r, cT_ps, cT_sb = sem("w1_copied"), sem("rows_T_in_psum"), sem("rows_T_ready")
        hT_ps, relu_sb, hT_sb = sem("hT_in_psum"), sem("relu_ready"), sem("hT_ready")
        y_ps, y_sb = sem("y_in_psum"), sem("y_ready")
        gate_r, y_out = sem("gate_ready"), sem("y_scattered")

        d_x = work([2, D], reset=True)
        d_xn = work([2, D])
        d_xT = work([2, DC, P])
        d_xb = work([2, D])
        d_sc = work([2, E])
        d_st = work([2, 6])
        d_mv = work([2, 2])
        d_sd = work([2, 1])
        d_rs = work([2, 1])
        qk1_ps, qk1_sb, v1_ps, v1_sb = sem("qk1_in_psum"), sem("qk1_ready"), sem("v1_in_psum"), sem("v1_ready")
        sc_ps, sc_sb, sc_kept, sc_out = sem("scores_in_psum"), sem("scores_ready"), sem("scores_kept"), sem2("scores_stored")

        NP = NH1 // 2
        e_qk = work([2, 4, P], reset=True)
        e_v = work([2, 2, 2, P])
        e_s = work([NH1, BLK])
        e_p = work([2, NH1, BLK])
        e_pT = work([NP, P])
        e_o = work([2, D])
        e_oT = work([2, DC, P])
        e_y = work([2, D])
        e_xb = work([2, D])
        e_mx = work([NH1])
        e_one = work([2])
        e_rc = work([2, NH1])
        e_part = sb("e_part", [P, 2, E], BF16)
        key_r, cand_r, thr_r, cmp_r = sem("key_kept"), sem("candidate_ready"), sem("threshold_ready"), sem("compared")
        key = sb("key", [P, E], I32)
        cand = sb("cand", [P, E], I32)
        thr = sb("thr", [P, E], I32)
        flip = sb("flip", [P, E], I32)
        got = sb("got", [P, E], I32)
        scmax = sb("scmax", [P, E])
        nscmax = sb("nscmax", [P, E])
        pmax = sb("pmax", [P, E])
        vz = sem("v_spread_cleared")
        qkl, vl, xbl = sem2("qk_tile_loaded"), sem2("v_tile_loaded"), sem2("xb1_tile_loaded")
        s_ps, mx_r, sub_r, p_r, sum_r, rc_r = (sem("att_in_psum"), sem("row_max"), sem("shifted"), sem("exp_ready"),
                                               sem("row_sum"), sem("row_rcp"))
        pT_ps, pT_sb, o_ps, o_sb, oT_ps, oT_sb = (sem("pT_in_psum"), sem("pT_ready"), sem("o_in_psum"), sem("o_ready"),
                                                  sem("oT_in_psum"), sem("oT_ready"))
        y1_ps, y1_sb, fin_r, fin_out = sem("y1_in_psum"), sem("y1_ready"), sem("final_ready"), sem2("final_stored")
        part_r, cnt_ps, cnt_used = sem("counts_ready"), sem("counts_in_psum"), sem("counts_used")
        pm_r, gmax_r, ngm_r = sem("partition_max"), sem("global_max"), sem("negated_max")
        ex_r, z_r, z_ps, rz_r = sem("score_exp"), sem("exp_sums"), sem("exp_sums_in_psum"), sem("exp_rcp")
        lo_r = sem("low_one_hots_ready")
        rank1_used, inv1_used = sem("ranks1_copied"), sem("slots1_copied")
        SR = NT // 2
        SH, HT = 20, 4
        both_r, rank1_ps, hot1_r, inv1_ps, idx1_r = (sem("above_and_ties"), sem("ranks1_in_psum"), sem("one_hots1_ready"),
                                                     sem("slots1_in_psum"), sem("index1_ready"))

        f1 = r1[:, :, :].rearrange("p e n -> p (e n)")
        TE = CAP // P
        f_xg = f1[:, 0:2 * TE * ROW].rearrange("p (b i n) -> p b i n", b=2, i=TE)
        o1 = 2 * TE * ROW
        f_xT = f1[:, o1:o1 + 2 * DC * CAP].rearrange("p (b c n) -> p b c n", b=2, c=DC)
        o2 = o1 + 2 * DC * CAP
        f_g = f1[:, o2:o2 + 2 * CAP].rearrange("p (b n) -> p b n", b=2)
        o3 = o2 + 2 * CAP
        f_h = f1[:, o3:o3 + 2 * HC * CAP].rearrange("p (b c n) -> p b c n", b=2, c=HC)
        o4 = o3 + 2 * HC * CAP
        f_y = f1[:, o4:o4 + TE * D].rearrange("p (i n) -> p i n", i=TE)
        f_w = [rt[:, 3072 * b:3072 * (b + 1)] for b in range(2)]
        f_gi = sb("f_gi", [P, TE], I32)
        f_si = sb("f_si", [P, TE], I32)
        f_we = sb("f_we", [P, 2, TE])
        f_wg = sb("f_wg", [P, 2, TE])
        rz = sb("rz", [P, E])
        fw_in = sem2("expert1_loaded")
        fgi_r, fsi_r, fx_in = sem("gather1_index"), sem("scatter1_index"), sem2("rows1_gathered")
        fT_ps, fT_sb, h13_ps, g_r, hh_r = (sem("rows1_T_in_psum"), sem("rows1_T_ready"), sem("h13_in_psum"),
                                           sem("silu_ready"), sem("hidden1_ready"))
        fy_ps, fy_sb, fwe_r, fwg_r, fy_out = (sem("y1e_in_psum"), sem("y1e_ready"), sem("weight_exp"),
                                              sem("weight_ready"), sem("y1e_scattered"))

        @block.sync
        def _(sp):
            def load_x(z, s, src, dst):
                sp.dma_start(dst[:, s.par, :], rows(src, s.t)).then_inc(z.x_in[s.par], 16)

            load_x(sa, Step(0, 0), x, a_x)
            load_x(sa, Step(0, 1), x, a_x)
            for dst, src in ((wqkv0_s[:, :, :], wqkv0.rearrange("(c p) n -> p c n", p=P)),
                             (rw0_s[:, :, :], rw0.rearrange("(c p) n -> p c n", p=P)),
                             (bq0_s[:, :], bq0[:, :]),
                             (bkv0_s[:, :], bkv0.partition_broadcast(P)),
                             (bo0_s[:, :], bo0.partition_broadcast(P)),
                             (cosk_s[:, :], cos_k[:, :]),
                             (sink_s[:, :], sin_k[:, :])):
                sp.dma_start(dst, src).then_inc(consts, 16)

            def step_a(s, more=True):
                sp.wait_ge(sa.xn, s.t + 1)
                sp.dma_start(rows(xg0_d, s.t), a_xn[:, s.par, :]).then_inc(sa.xn_out[s.par], 16)
                sp.wait_ge(sa.xb, s.t + 1)
                sp.dma_start(rows(xb_d, s.t), a_xb[:, s.par, :]).then_inc(sa.xb_out[s.par], 16)
                if more:
                    load_x(sa, Step(s.half + 1, s.par), x, a_x)

            with sp.Fori(0, E) as m:
                for par in range(2):
                    step_a(Step(m, par))
                sp.dma_start(r1[:, ds(m, 1), 0:DC * H].rearrange("p e (c n) -> p (e c) n", c=DC),
                             w1_0[ds(m, 1)].rearrange("e (c p) n -> p (e c) n", p=P)).then_inc(w0_in, 16)
                sp.dma_start(r1[:, ds(m, 1), DC * H:2 * DC * H].rearrange("p e (c n) -> p (e c) n", c=HC),
                             w2_0[ds(m, 1)].rearrange("e (c p) n -> p (e c) n", p=P)).then_inc(w0_in, 16)
            with sp.Fori(E, NT // 2 - 1) as m:
                for par in range(2):
                    step_a(Step(m, par))
            for par in range(2):
                step_a(Step(NT // 2 - 1, par), more=False)

            def group(s):
                return s.par * L + s.half * GB * P

            def load_q(s):
                sp.dma_start(b_q[:, s.par, :, :], qrot_all[:, :, ds(group(s), GB * P)]).then_inc(ql_in[s.par], 16)

            def load_xb(s):
                sp.dma_start(b_xb[:, s.par, :, :], xb_d[ds(group(s), GB * P), :].rearrange("(j p) n -> p j n", p=P))\
                  .then_inc(xb_in[s.par], 16)

            sp.wait_ge(qrot, NT)
            for par in range(2):
                load_q(Step(0, par))
            for par in range(2):
                sp.wait_ge(sa.xb_out[par], 16 * (NT // 2))
            for par in range(2):
                load_xb(Step(0, par))
            for par in range(2):
                sp.wait_ge(sa.xn_out[par], 16 * (NT // 2))
            sp.wait_ge(gates_r, 1)
            sp.dma_start(xg0_d.rearrange("(t p) n -> p t n", p=P)[:, :, D:ROW], gates).then_inc(gates_out, 16)

            def step_b(s, more=True):
                sp.wait_ge(ao_sb, GB * (s.t + 1))
                sp.dma_start(x1_d[ds(group(s), GB * P), :].rearrange("(j p) n -> p j n", p=P), b_x1[:, s.par, :, :])\
                  .then_inc(x1_out[s.par], 16)
                if more:
                    load_q(Step(s.half + 1, s.par))
                    load_xb(Step(s.half + 1, s.par))

            with sp.Fori(0, SB // 2 - 1) as m:
                for par in range(2):
                    step_b(Step(m, par))
            for par in range(2):
                step_b(Step(SB // 2 - 1, par), more=False)
            for par in range(2):
                sp.wait_ge(x1_out[par], 16 * (SB // 2))
            sp.wait_ge(gates_out, 16)
            end_stage(sp, 1)

            end_stage(sp, 2)

            for par in range(2):
                load_x(sd, Step(0, par), x1_d, d_x)

            def step_d(s, more=True):
                sp.wait_ge(sd.xn, s.t + 1)
                sp.dma_start(rows(xg1_d, s.t), d_xn[:, s.par, :]).then_inc(sd.xn_out[s.par], 16)
                sp.wait_ge(sd.xb, s.t + 1)
                sp.dma_start(rows(xb1_d, s.t), d_xb[:, s.par, :]).then_inc(sd.xb_out[s.par], 16)
                if more:
                    load_x(sd, Step(s.half + 1, s.par), x1_d, d_x)
                if s.at_least(1):
                    b = s.back(1)
                    sp.wait_ge(sc_sb, b.t + 1)
                    sp.dma_start(rows(xg1_d, b.t, D, ROW), d_sc[:, b.par, :]).then_inc(sc_out[b.par], 16)

            step_d(Step(0, 0))
            step_d(Step(0, 1))
            with sp.Fori(1, NT // 2 - 1) as m:
                for par in range(2):
                    step_d(Step(m, par))
            for par in range(2):
                step_d(Step(NT // 2 - 1, par), more=False)
            sp.wait_ge(sc_sb, NT)
            sp.dma_start(rows(xg1_d, NT - 1, D, ROW), d_sc[:, 1, :]).then_inc(sc_out[1], 16)
            for par in range(2):
                sp.wait_ge(sd.xn_out[par], 16 * (NT // 2))
                sp.wait_ge(sd.xb_out[par], 16 * (NT // 2))
                sp.wait_ge(sc_out[par], 16 * (NT // 2))
            end_stage(sp, 3)

            def load_w(s):
                w = f_w[s.par]
                sp.dma_start(w[:, 0:2 * DC * H].rearrange("p (c n) -> p c n", c=DC),
                             w13_1[ds(s.t, 1)].rearrange("o (c p) n -> p (o c) n", p=P)).then_inc(fw_in[s.par], 16)
                sp.dma_start(w[:, 2 * DC * H:3072].rearrange("p (c n) -> p c n", c=HC),
                             w2_1[ds(s.t, 1)].rearrange("o (c p) n -> p (o c) n", p=P)).then_inc(fw_in[s.par], 16)

            def load_qk(s):
                if s.at_least(2):
                    sp.wait_ge(s_ps, s.t - 1)
                sp.dma_start(e_qk[:, s.par, :, :], qk_all[:, :, ds(s.t * P, P)]).then_inc(qkl[s.par], 16)

            def load_v(s):
                if s.at_least(2):
                    sp.wait_ge(o_ps, s.t - 1)
                for b in range(2):
                    for hp in range(2):
                        sp.dma_start(e_v[BLK * hp:BLK * hp + BLK, s.par, b, hp, :],
                                     r2[BLK * b:BLK * b + BLK, ds(s.t * D + P * hp, P)]).then_inc(vl[s.par], 16)

            def load_xb1(s):
                sp.dma_start(e_xb[:, s.par, :], rows(xb1_d, s.t)).then_inc(xbl[s.par], 16)

            def store_e(s, more=True):
                sp.wait_ge(fin_r, s.t + 1)
                sp.dma_start(rows(out, s.t), e_y[:, s.par, :]).then_inc(fin_out[s.par], 16)
                if more:
                    load_xb1(Step(s.half + 1, s.par))

            sp.wait_ge(vz, 1)
            for par in range(2):
                load_qk(Step(0, par))
                load_v(Step(0, par))
                load_xb1(Step(0, par))
            for t in (2, 3):
                load_qk(Step(1, t - 2))
                if t == 3:
                    load_v(Step(1, 0))
            with sp.Fori(2, NT // 2) as m:
                for par in range(2):
                    s = Step(m, par)
                    load_qk(s)
                    load_v(s.back(1))
                    store_e(s.back(4))
            load_v(Step(NT // 2 - 1, 1))
            for t in range(NT - 4, NT):
                store_e(Step(t // 2, t % 2), more=t < NT - 2)
            sp.wait_ge(idx1_r, 1)
            for par in range(2):
                load_w(Step(0, par))
            for par in range(2):
                sp.wait_ge(fin_out[par], 16 * (NT // 2))
            end_stage(sp, 4)

            with sp.Fori(1, E // 2) as m:
                for par in range(2):
                    s = Step(m, par)
                    sp.wait_ge(fy_ps, TE * (s.t - 1))
                    load_w(s)
            sp.wait_ge(fy_out, 16 * TE * E)

        @block.tensor
        def _(pe):
            def transpose_x(z, s, xn, n=NT):
                pe.wait_ge(z.xn, s.t + 1)
                if s.at_least(1):
                    pe.wait_ge(z.xT, s.t)
                for c in range(DC):
                    last = pe.transpose(bank[0][:, c * P:(c + 1) * P], xn[:, s.par, c * P:(c + 1) * P], ident[:, :])
                last.then_inc(z.xT_ps, 1)

            pe.wait_ge(consts, 16 * 7)
            pe.wait_ge(made, 1)

            def step_a(s, first=False):
                if in_range(s.back(1), NT) and s.at_least(1):
                    b = s.back(1)
                    xT = a_xT[:, b.par, :, :]
                    pe.wait_ge(sa.xT, b.t + 1)
                    if b.at_least(2):
                        pe.wait_ge(kv_sb, b.t - 1)
                    for c in range(DC):
                        last = pe.matmul(bank[1 + b.par][:, :], xT[:, c, :], wqkv0_s[:, c, D:3 * D],
                                         start=c == 0, stop=c == DC - 1)
                    last.then_inc(kv_ps, 1)
                if in_range(s, NT):
                    transpose_x(sa, s, a_xn)
                if in_range(s.back(1), NT) and s.at_least(1):
                    if b.at_least(2):
                        pe.wait_ge(q_sb, 2 * (b.t - 1))
                    for r in range(DC):
                        for c in range(DC):
                            last = pe.matmul(bank[5 + b.par][:, r * P:(r + 1) * P], wqkv0_s[:, c, r * P:(r + 1) * P],
                                             xT[:, c, :], start=c == 0, stop=c == DC - 1)
                    last.then_inc(q_ps, 1)
                    if b.at_least(1):
                        pe.wait_ge(lg_sb, b.t)
                    for c in range(DC):
                        last = pe.matmul(bank[7][:, 0:E], xT[:, c, :], rw0_s[:, c, :], start=c == 0, stop=c == DC - 1)
                    last.then_inc(lg_ps, 1)
                if s.at_least(3) and in_range(s.back(3), NT):
                    b = s.back(3)
                    start = isinstance(b.half, int) and b.t % BT == 0
                    stop = isinstance(b.half, int) and b.t % BT == BT - 1
                    pe.wait_ge(krot, b.t + 1)
                    if start and b.t:
                        pe.wait_ge(kvm_r, 1)
                    kr = a_kr[:, b.par, :].rearrange("p (r h) -> p r h", r=2)
                    for g in range(2):
                        last = pe.matmul(bank[3 + g][:, 0:P], a_kv[:, b.par, D + g * P:D + (g + 1) * P],
                                         kr[:, :, g * 64:(g + 1) * 64], start=start, stop=stop)
                    last.then_inc(st_ps, 1)

            for t in range(4):
                step_a(Step(t // 2, t % 2))
            with pe.Fori(2, 9) as m:
                for par in range(2):
                    step_a(Step(m, par))
            for t in (18, 19):
                step_a(Step(t // 2, t % 2))
            with pe.Fori(10, NT // 2) as m:
                for par in range(2):
                    step_a(Step(m, par))
            for t in (32, 33, 34):
                step_a(Step(t // 2, t % 2))

            pe.wait_ge(consts_b, 16 * 7)
            pe.wait_ge(mask_r, 1)
            pe.wait_ge(kv_sb, NT)
            pe.matmul(bank[1][:, 0:E * NT], upper[:, :], small_mask, start=True, stop=True)
            pe.matmul(bank[1][:, E * NT:2 * E * NT], ones[:, :], small_mask, start=True, stop=True).then_inc(rank_ps, 1)
            pe.wait_ge(q_sb, 2 * NT)

            for b in range(NB):
                pe.wait_ge(kvm_r, b + 1)
                for r in range(2):
                    for g in range(2):
                        last = pe.matmul(bank[5 + b][64 * g:64 * g + 64, r * D:(r + 1) * D],
                                         a_kvm[b][g][:, r * 64:(r + 1) * 64], wo0_s[:, g, :], start=True, stop=True)
                last.then_inc(m_ps, 1)

            def invert(s, start=False, stop=False):
                pe.wait_ge(hot_r, s.t + 1)
                for n in range(GN):
                    last = pe.matmul(bank[0][:, 0:ST0], hot_lo[:, s.par, n, :], hot_hi[:, s.par, n, :],
                                     start=start and n == 0, stop=stop and n == GN - 1)
                last.then_inc(inv_ps, 1)

            def step_b(s):
                pe.wait_ge(ql_in[s.par], 16 * (s.half + 1))
                for j in range(GB):
                    if s.at_least(1):
                        pe.wait_ge(ao_sb, GB * (s.t - 1) + j + 1)
                    for r in range(2):
                        last = pe.matmul(bank[attn_bank[j]][:, 0:D], b_q[:, s.par, r, j * P:(j + 1) * P],
                                         m_all[s.par][:, r, :], start=r == 0, stop=r == 1)
                    last.then_inc(ao_ps, 1)
                if s.at_least(1):
                    b = s.back(1)
                    invert(b, start=isinstance(b.half, int) and b.t == 0)

            pe.wait_ge(m_sb, NB)
            step_b(Step(0, 0))
            step_b(Step(0, 1))
            with pe.Fori(1, SB // 2) as m:
                for par in range(2):
                    step_b(Step(m, par))
            invert(Step(SB // 2 - 1, 1), stop=True)
            pe.wait_ge(w0_in, 16 * 2 * E)
            end_stage(pe, 1)

            def step_c(s):
                if in_range(s, ST0):
                    pe.wait_ge(xg_in[s.par], 16 * (s.half + 1))
                    if s.at_least(2):
                        pe.wait_ge(cT_sb, s.t - 1)
                    for c in range(DC):
                        last = pe.transpose(bank[(0, 3)[s.par]][:, c * P:(c + 1) * P], c_xg[:, s.par, c * P:(c + 1) * P],
                                            ident[:, :])
                    last.then_inc(cT_ps, 1)
                if s.at_least(1) and in_range(s.back(1), ST0):
                    b = s.back(1)
                    pe.wait_ge(w1_r, b.t + 1)
                    pe.wait_ge(cT_sb, b.t + 1)
                    if b.at_least(2):
                        pe.wait_ge(relu_sb, b.t - 1)
                    for k in range(HC):
                        for c in range(DC):
                            last = pe.matmul(bank[1 + b.par][:, k * P:(k + 1) * P], c_w1[:, b.par, c, k * P:(k + 1) * P],
                                             c_xT[:, b.par, c, :], start=c == 0, stop=c == DC - 1)
                    last.then_inc(hT_ps, 1)
                if s.at_least(2) and in_range(s.back(2), ST0):
                    b = s.back(2)
                    e2 = pe.value_load(tile_e[0:1, ds(b.t, 1)], min_val=0, max_val=E - 1)
                    pe.wait_ge(hT_sb, b.t + 1)
                    if b.at_least(2):
                        pe.wait_ge(y_sb, b.t - 1)
                    for c in range(HC):
                        last = pe.matmul(bank[5 + b.par][:, 0:D], c_hT[:, b.par, c, :],
                                         r1[:, ds(e2, 1), DC * H + c * D:DC * H + (c + 1) * D],
                                         start=c == 0, stop=c == HC - 1)
                    last.then_inc(y_ps, 1)

            for t in range(4):
                step_c(Step(t // 2, t % 2))
            with pe.Fori(2, ST0 // 2) as m:
                for par in range(2):
                    step_c(Step(m, par))
            for t in (ST0, ST0 + 1):
                step_c(Step(t // 2, t % 2))
            end_stage(pe, 2)

            def step_d(s):
                if s.at_least(1) and in_range(s.back(1), NT):
                    b = s.back(1)
                    xT = d_xT[:, b.par, :, :]
                    pe.wait_ge(sd.xT, b.t + 1)
                    if b.at_least(2):
                        pe.wait_ge(qk1_sb, 4 * (b.t - 1))
                    for j in range(2 * DC):
                        for c in range(DC):
                            last = pe.matmul(bank[1 + b.par][:, j * P:(j + 1) * P], wqkv1_s[:, c, j * P:(j + 1) * P],
                                             xT[:, c, :], start=c == 0, stop=c == DC - 1)
                    last.then_inc(qk1_ps, 1)
                if in_range(s, NT):
                    transpose_x(sd, s, d_xn)
                if s.at_least(1) and in_range(s.back(1), NT):
                    if b.at_least(2):
                        pe.wait_ge(v1_sb, b.t - 1)
                    for c in range(DC):
                        last = pe.matmul(bank[3 + b.par][:, 0:D], xT[:, c, :], wqkv1_s[:, c, 2 * D:3 * D],
                                         start=c == 0, stop=c == DC - 1)
                    last.then_inc(v1_ps, 1)
                    if b.at_least(1):
                        pe.wait_ge(sc_sb, b.t)
                    for c in range(DC):
                        last = pe.matmul(bank[5][:, 0:E], xT[:, c, :], wg1_s[:, c, :], start=c == 0, stop=c == DC - 1)
                    last.then_inc(sc_ps, 1)

            for t in range(4):
                step_d(Step(t // 2, t % 2))
            with pe.Fori(2, NT // 2) as m:
                for par in range(2):
                    step_d(Step(m, par))
            step_d(Step(NT // 2, 0))
            end_stage(pe, 3)

            pe.wait_ge(vz, 1)

            def count(s, r, bk):
                pe.wait_ge(part_r, 2 * s.t + r + 1)
                pe.matmul(bank[bk][:, D:D + E], ones[:, :], e_part[:, r, :], start=True, stop=True).then_inc(cnt_ps, 1)

            def step_e(s, search=False, copied=None):
                if in_range(s, NT):
                    pe.wait_ge(qkl[s.par], 16 * (s.half + 1))
                    if s.at_least(1):
                        pe.wait_ge(sub_r, s.t)
                    for j in range(2):
                        for b in range(2):
                            for g in range(4):
                                last = pe.matmul(banks47[BLK * b:BLK * b + BLK, g, BLK * j:BLK * j + BLK],
                                                 e_qk[DK * g:DK * g + DK, s.par, j, BLK * b:BLK * b + BLK],
                                                 e_qk[DK * g:DK * g + DK, s.par, DC + j, BLK * b:BLK * b + BLK],
                                                 start=True, stop=True, tile_position=(DK * g, BLK * b))
                    last.then_inc(s_ps, 1)
                if copied is not None:
                    pe.wait_ge(copied, 1)
                if s.at_least(3) and in_range(s.back(3), NT):
                    b = s.back(3)
                    pe.wait_ge(oT_sb, b.t + 1)
                    if b.at_least(1):
                        pe.wait_ge(y1_sb, b.t)
                    if search or (isinstance(s.half, int) and s.t == SR):
                        pe.wait_ge(cnt_used, 2 * s.t - 1)
                    for c in range(DC):
                        last = pe.matmul(bank[3][:, 0:D], e_oT[:, b.par, c, :], wo1_s[:, c, :],
                                         start=c == 0, stop=c == DC - 1)
                    last.then_inc(y1_ps, 1)
                if s.at_least(1) and in_range(s.back(1), NT):
                    b = s.back(1)
                    pe.wait_ge(p_r, b.t + 1)
                    if b.at_least(1):
                        pe.wait_ge(pT_sb, b.t)
                    for g in range(NP):
                        last = pe.transpose(bank[0][:, g * P:(g + 1) * P],
                                            e_p[:, b.par, 2 * g:2 * g + 2, :], ident[:, :])
                    last.then_inc(pT_ps, 1)
                if search:
                    if s.at_least(3):
                        pe.wait_ge(y1_sb, s.t - 2)
                    count(s, 0, 3)
                if s.at_least(2) and in_range(s.back(2), NT):
                    b = s.back(2)
                    pe.wait_ge(o_sb, b.t + 1)
                    if b.at_least(1):
                        pe.wait_ge(oT_sb, b.t)
                    if search or (isinstance(s.half, int) and s.t == SR):
                        pe.wait_ge(cnt_used, 2 * s.t)
                    for c in range(DC):
                        last = pe.transpose(bank[2][:, c * P:(c + 1) * P], e_o[:, b.par, c * P:(c + 1) * P], ident[:, :])
                    last.then_inc(oT_ps, 1)
                if s.at_least(1) and in_range(s.back(1), NT):
                    b = s.back(1)
                    pe.wait_ge(vl[b.par], 64 * (b.half + 1))
                    pe.wait_ge(pT_sb, b.t + 1)
                    if b.at_least(1):
                        pe.wait_ge(o_sb, b.t)
                    for k in range(2):
                        for g in range(NP):
                            rows_k = slice(BLK * k, BLK * k + BLK)
                            pe.matmul(bank[1][rows_k, g * 64:(g + 1) * 64], e_pT[:, g, rows_k],
                                      e_v[:, b.par, k, :, DK * g:DK * g + DK], start=True, stop=True)
                            last = pe.matmul(bank[1][rows_k, D + 2 * g:D + 2 * g + 2], e_pT[:, g, rows_k], e_one[:, :],
                                             start=True, stop=True)
                    last.then_inc(o_ps, 1)
                if search:
                    if s.at_least(2):
                        pe.wait_ge(oT_sb, s.t - 1)
                    count(s, 1, 2)

            def free_banks(t):
                pe.wait_ge(o_sb, t)
                pe.wait_ge(oT_sb, t - 1)
                pe.wait_ge(y1_sb, t - 2)

            for t in range(4):
                step_e(Step(t // 2, t % 2), search=True)
            with pe.Fori(2, SR // 2) as m:
                for par in range(2):
                    step_e(Step(m, par), search=True)
            step_e(Step(SR // 2, 0))
            step_e(Step(SR // 2, 1))
            pe.wait_ge(both_r, 1)
            free_banks(SR + 1)
            for k in range(2):
                half = slice(k * E * NT, (k + 1) * E * NT)
                pe.matmul(bank[3 - k][:, D:2 * D], upper[:, :], s_both[:, half], start=True, stop=False)
                pe.matmul(bank[3 - k][:, D:2 * D], ones[:, :], s_before[:, half], start=False, stop=True)
            pe.matmul(bank[1][:, 2 * D - E:2 * D], onesf, s_tot, start=True, stop=True).then_inc(rank1_ps, 1)
            step_e(Step(SR // 2 + 1, 0), copied=rank1_used)
            step_e(Step(SR // 2 + 1, 1))
            with pe.Fori(SH // 2, (SH + NT // HT) // 2) as m:
                for par in range(2):
                    step_e(Step(m, par))
            t = SH + NT // HT
            step_e(Step(t // 2, 0))
            pe.wait_ge(z_r, 1)
            pe.wait_ge(hot1_r, NT // HT)
            free_banks(t)
            pe.matmul(bank[1][:, 2 * D - E:2 * D], onesf, s_zp, start=True, stop=True).then_inc(z_ps, 1)
            for q in range(2):
                for c in range(NT):
                    last = pe.matmul(bank[3][:, D + q * P:D + (q + 1) * P], hot1_hi[:, c, q * P:(q + 1) * P],
                                     hot1_lo[:, c, :, q * 4:(q + 1) * 4, :],
                                     start=c == 0, stop=c == NT - 1)
            last.then_inc(inv1_ps, 1)
            step_e(Step(t // 2, 1), copied=inv1_used)
            for t in range(SH + NT // HT + 2, NT + 3):
                step_e(Step(t // 2, t % 2))
            end_stage(pe, 4)

            def transpose_f(s):
                pe.wait_ge(fx_in[s.par], 16 * TE * (s.half + 1))
                if s.at_least(1):
                    pe.wait_ge(fT_sb, 2 * s.t)
                for c in range(DC):
                    for i in range(TE):
                        last = pe.transpose(bank[4 + c][:, i * P:(i + 1) * P],
                                            f_xg[:, s.par, i, c * P:(c + 1) * P], ident[:, :])
                last.then_inc(fT_ps, 1)

            def step_f(s, more=True):
                pe.wait_ge(fw_in[s.par], 32 * (s.half + 1))
                pe.wait_ge(fT_sb, 2 * (s.t + 1))
                w = f_w[s.par]
                for hb in range(HC):
                    if hb >= 2 or s.at_least(1):
                        pe.wait_ge(hh_r, HC * s.t + hb - 1)
                    for k in range(2):
                        for c in range(DC):
                            o = c * 2 * H + k * H + hb * P
                            last = pe.matmul(bank[2 * (hb % 2) + k][:, :], w[:, o:o + P], f_xT[:, s.par, c, :],
                                             start=c == 0, stop=c == DC - 1)
                    last.then_inc(h13_ps, 1)
                if more:
                    transpose_f(Step(s.half + s.par, 1 - s.par))
                pe.wait_ge(hh_r, HC * (s.t + 1))
                for i in range(TE):
                    if i >= 2 or s.at_least(1):
                        pe.wait_ge(fy_sb, TE * s.t + i - 1)
                    for c in range(HC):
                        last = pe.matmul(bank[6 + i % 2][:, 0:D], f_h[:, s.par, c, i * P:(i + 1) * P],
                                         w[:, 2 * DC * H + c * D:2 * DC * H + (c + 1) * D],
                                         start=c == 0, stop=c == HC - 1)
                    last.then_inc(fy_ps, 1)

            transpose_f(Step(0, 0))
            step_f(Step(0, 0))
            step_f(Step(0, 1))
            with pe.Fori(1, E // 2 - 1) as m:
                for par in range(2):
                    step_f(Step(m, par))
            step_f(Step(E // 2 - 1, 0))
            step_f(Step(E // 2 - 1, 1), more=False)

        @block.scalar
        def _(act):
            def sqrt_and_copy(z, s, mv, sdv, xT):
                act.wait_ge(z.moments, s.t + 1)
                act.activation(sdv[:, s.par, :], mv[:, s.par, 1:2], ACT.Sqrt, bias=eps_c[:, :]).then_inc(z.std, 1)

            def copy_xT(z, s, xT, users):
                act.wait_ge(z.xT_ps, s.t + 1)
                for u, n in users:
                    if s.at_least(2):
                        act.wait_ge(u, n * (s.t - 1))
                act.activation(xT[:, s.par, :, :], bank[0][:, 0:D], ACT.Copy).then_inc(z.xT, 1)

            for dst, src in ((cosq_s, cos_q[:, :]),
                             (sinq_s, sin_q.rearrange("p (r n) -> p r n", r=2))):
                act.dma_start(dst, src).then_inc(tables, 16)
            for dst, src in ((wo0_s[:, :, :], wo0.rearrange("(c p) n -> p c n", p=P)),
                             (wqkv1_s[:, :, :], wqkv1.rearrange("(c p) n -> p c n", p=P)),
                             (wo1_s[:, :, :], wo1.rearrange("(c p) n -> p c n", p=P)),
                             (wg1_s[:, :, :], wg1.rearrange("(c p) n -> p c n", p=P)),
                             (bqk1_s[:, :], bqk1[:, :]),
                             (bv1_s[:, :], bv1.partition_broadcast(P)),
                             (bo1_s[:, :], bo1.partition_broadcast(P))):
                act.dma_start(dst, src).then_inc(consts_b, 16)
            act.wait_ge(made, 1)
            act.wait_ge(consts, 16 * 7)

            def step_a(s):
                if in_range(s, NT):
                    sqrt_and_copy(sa, s, a_mv, a_sd, a_xT)
                    copy_xT(sa, s, a_xT, [(lg_ps, 1)])
                if s.at_least(1) and in_range(s.back(1), NT):
                    b = s.back(1)
                    act.wait_ge(q_ps, b.t + 1)
                    if b.at_least(2):
                        act.wait_ge(qprod, b.t - 1)
                    for r in range(DC):
                        act.activation(a_q[:, b.par, r, :], bank[5 + b.par][:, r * P:(r + 1) * P], ACT.Identity,
                                       bias=bq0_s[:, r:r + 1]).then_inc(q_sb, 1)
                    act.wait_ge(lg_ps, b.t + 1)
                    if b.at_least(2):
                        act.wait_ge(top_m, b.t - 1)
                    act.activation(a_lg[:, b.par, :], bank[7][:, 0:E], ACT.Copy).then_inc(lg_sb, 1)

            for t in range(4):
                step_a(Step(t // 2, t % 2))
            with act.Fori(2, NT // 2) as m:
                for par in range(2):
                    step_a(Step(m, par))
            step_a(Step(NT // 2, 0))

            act.wait_ge(d_sb, 1)
            act.activation(top_e, top_d, ACT.Exp).then_inc(e_sb, 1)
            for b in range(NB):
                act.wait_ge(m_ps, b + 1)
                act.activation(m_all[b], bank[5 + b][:, :], ACT.Copy).then_inc(m_sb, 1)
            end_stage(act, 1)

            def step_c(s):
                if in_range(s, ST0):
                    act.wait_ge(cT_ps, s.t + 1)
                    if s.at_least(2):
                        act.wait_ge(hT_ps, s.t - 1)
                    act.activation(c_xT[:, s.par, :, :], bank[(0, 3)[s.par]][:, 0:D], ACT.Copy).then_inc(cT_sb, 1)
                if s.at_least(1) and in_range(s.back(1), ST0):
                    b = s.back(1)
                    act.wait_ge(hT_ps, b.t + 1)
                    if b.at_least(2):
                        act.wait_ge(hT_sb, b.t - 1)
                    act.activation(c_r[:, b.par, :], bank[1 + b.par][:, :], ACT.Relu).then_inc(relu_sb, 1)

            for t in range(4):
                step_c(Step(t // 2, t % 2))
            with act.Fori(2, ST0 // 2) as m:
                for par in range(2):
                    step_c(Step(m, par))
            step_c(Step(ST0 // 2, 0))
            end_stage(act, 2)

            def step_d(s):
                if in_range(s, NT):
                    sqrt_and_copy(sd, s, d_mv, d_sd, d_xT)
                    copy_xT(sd, s, d_xT, [(sc_ps, 1)])
                if s.at_least(1) and in_range(s.back(1), NT):
                    b = s.back(1)
                    act.wait_ge(qk1_ps, b.t + 1)
                    for j in range(2 * DC):
                        act.activation(qk_all[:, j, ds(b.t * P, P)], bank[1 + b.par][:, j * P:(j + 1) * P],
                                       ACT.Identity, bias=bqk1_s[:, j:j + 1]).then_inc(qk1_sb, 1)
                    act.wait_ge(sc_ps, b.t + 1)
                    if b.at_least(2):
                        act.wait_ge(sc_kept, b.t - 1)
                        act.wait_ge(sc_out[b.par], 16 * b.half)
                    act.activation(d_sc[:, b.par, :], bank[5][:, 0:E], ACT.Copy).then_inc(sc_sb, 1)

            for t in range(4):
                step_d(Step(t // 2, t % 2))
            with act.Fori(2, NT // 2) as m:
                for par in range(2):
                    step_d(Step(m, par))
            step_d(Step(NT // 2, 0))
            end_stage(act, 3)

            def step_e(s):
                if s.at_least(3) and in_range(s.back(3), NT):
                    b = s.back(3)
                    act.wait_ge(y1_ps, b.t + 1)
                    if b.at_least(2):
                        act.wait_ge(fin_out[b.par], 16 * b.half)
                    act.activation(e_y[:, b.par, :], bank[3][:, 0:D], ACT.Copy).then_inc(y1_sb, 1)
                if s.at_least(1) and in_range(s.back(1), NT):
                    b = s.back(1)
                    act.wait_ge(pT_ps, b.t + 1)
                    if b.at_least(1):
                        act.wait_ge(o_ps, b.t)
                    act.activation(e_pT[:, :, :], bank[0][:, :], ACT.Copy).then_inc(pT_sb, 1)
                if s.at_least(2) and in_range(s.back(2), NT):
                    b = s.back(2)
                    act.wait_ge(oT_ps, b.t + 1)
                    if b.at_least(2):
                        act.wait_ge(y1_ps, b.t - 1)
                    act.activation(e_oT[:, b.par, :, :], bank[2][:, 0:D], ACT.Copy).then_inc(oT_sb, 1)
                if in_range(s, NT):
                    act.wait_ge(sub_r, s.t + 1)
                    if s.at_least(2):
                        act.wait_ge(pT_ps, s.t - 1)
                    act.activation(e_p[:, s.par, :, :], e_s[:, :, :], ACT.Exp, scale=DK ** -0.5).then_inc(p_r, 1)

            for t in range(6):
                step_e(Step(t // 2, t % 2))
            with act.Fori(3, SR // 2) as m:
                for par in range(2):
                    step_e(Step(m, par))
            act.wait_ge(ngm_r, 1)
            for e in range(E):
                last = act.activation(s_exp[:, e, :], sc_all[:, e, :], ACT.Exp, bias=nscmax[:, e:e + 1])
            last.then_inc(ex_r, 1)
            with act.Fori(SR // 2, NT // 2) as m:
                for par in range(2):
                    step_e(Step(m, par))
            for t in (NT, NT + 1, NT + 2):
                step_e(Step(t // 2, t % 2))
            end_stage(act, 4)

            def copy_fT(s):
                act.wait_ge(fT_ps, s.t + 1)
                if s.at_least(2):
                    act.wait_ge(h13_ps, HC * (s.t - 1))
                for c in range(DC):
                    act.activation(f_xT[:, s.par, c, :], bank[4 + c][:, :], ACT.Copy).then_inc(fT_sb, 1)

            def step_f(s, e, more=True):
                for hb in range(HC):
                    act.wait_ge(h13_ps, HC * s.t + hb + 1)
                    if hb >= 2 or s.at_least(1):
                        act.wait_ge(hh_r, HC * s.t + hb - 1)
                    act.activation(f_g[:, hb % 2, :], bank[2 * (hb % 2)][:, :], ACT.Silu).then_inc(g_r, 1)
                act.wait_ge(fx_in[s.par], 16 * TE * (s.half + 1))
                if s.at_least(2):
                    act.wait_ge(fwg_r, s.t - 1)
                act.activation(f_we[:, s.par, :].unsqueeze(2), f_xg[:, s.par, :, ds(D + e, 1)], ACT.Exp,
                               bias=nscmax[:, ds(e, 1)]).then_inc(fwe_r, 1)
                if more:
                    copy_fT(Step(s.half + s.par, 1 - s.par))

            copy_fT(Step(0, 0))
            step_f(Step(0, 0), 0)
            step_f(Step(0, 1), 1)
            with act.Fori(1, E // 2 - 1) as m:
                for par in range(2):
                    step_f(Step(m, par), 2 * m + par)
            step_f(Step(E // 2 - 1, 0), E - 2)
            step_f(Step(E // 2 - 1, 1), E - 1, more=False)

        @block.vector
        def _(dve):
            chain = [0]

            def link(ins):
                chain[0] += 1
                ins.then_inc(seq, 1)
                dve.wait_ge(seq, chain[0])

            def stats(z, s, xt, st):
                dve.wait_ge(z.x_in[s.par], 16 * (s.half + 1))
                dve.bn_stats(st[:, s.par, :], xt[:, s.par, :]).then_inc(z.stats, 1)

            def moments(z, s, st, mv):
                dve.bn_aggr(mv[:, s.par, :], st[:, s.par, :]).then_inc(z.moments, 1)

            def normalise(z, s, xt, mv, sdv, rs, xn):
                dve.wait_ge(z.std, s.t + 1)
                dve.reciprocal(rs[:, s.par, :], sdv[:, s.par, :]).then_inc(z.rstd, 1)
                dve.wait_ge(z.rstd, s.t + 1)
                if s.at_least(2):
                    dve.wait_ge(z.xT_ps, s.t - 1)
                    dve.wait_ge(z.xn_out[s.par], 16 * s.half)
                dve.tensor_scalar(xn[:, s.par, :], xt[:, s.par, :], mv[:, s.par, 0:1], rs[:, s.par, :],
                                  ALU.subtract, ALU.mult).then_inc(z.xn, 1)

            dve.wait_ge(made, 1)
            dve.wait_ge(consts, 16 * 7)

            def step_a(s, second=False):
                if in_range(s, NT):
                    normalise(sa, s, a_x, a_mv, a_sd, a_rs, a_xn)
                n = s.back(-1)
                if in_range(n, NT):
                    stats(sa, n, a_x, a_st)
                    if not s.at_least(2):
                        dve.wait_ge(sa.stats, n.t + 1)
                        moments(sa, n, a_st, a_mv)
                if s.at_least(2) and in_range(s.back(2), NT):
                    b = s.back(2)
                    tb = b.t - BT if second else b.t
                    dve.wait_ge(kv_ps, b.t + 1)
                    dve.wait_ge(lg_sb, b.t + 1)
                    if b.at_least(2):
                        dve.wait_ge(st_ps, b.t - 1)
                    if in_range(n, NT):
                        dve.wait_ge(sa.stats, n.t + 1)
                    kv = a_kv[:, b.par, :]
                    dve.tensor_tensor(kv, bank[1 + b.par][:, :], bkv0_s[:, :], ALU.add).then_inc(kv_sb, 1)
                    if in_range(n, NT):
                        moments(sa, n, a_st, a_mv)
                    dve.max(a_top[:, b.par, :], a_lg[:, b.par, :]).then_inc(top_done, 1)
                    dve.wait_ge(kv_sb, b.t + 1)
                    dve.wait_ge(top_done, b.t + 1)
                    k4 = kv[:, 0:D].rearrange("p (r h j) -> p r h j", r=2, h=NH0)
                    t4 = [a_t[:, i, :].rearrange("p (r h j) -> p r h j", r=2, h=NH0) for i in range(2)]
                    cos = cosk_s[:, ds(tb * JR, JR)]
                    for r in range(2):
                        sin = sink_s[:, ds(tb * 2 * JR + r * JR, JR)]
                        dve.tensor_tensor(t4[0][:, r], k4[:, r], over_mid(cos, NH0), ALU.mult).then_inc(kprod, 1)
                        dve.tensor_tensor(t4[1][:, r], k4[:, 1 - r], over_mid(sin, NH0), ALU.mult).then_inc(kprod, 1)
                    dve.max_index(a_ti[:, b.par, :].bitcast(U32), a_top[:, b.par, :], a_lg[:, b.par, :]).then_inc(top_m, 1)
                    dve.wait_ge(kprod, 4 * (b.t + 1))
                    dve.tensor_tensor(a_kr[:, b.par, :], a_t[:, 0, :], a_t[:, 1, :], ALU.add).then_inc(krot, 1)
                    dve.tensor_copy(top_v[:, ds(b.t * TOPK, TOPK)], a_top[:, b.par, 0:TOPK]).then_inc(top_kept, 1)
                    dve.wait_ge(top_m, b.t + 1)
                    dve.tensor_copy(top_i[:, ds(b.t * TOPK, TOPK)], a_ti[:, b.par, 0:TOPK].bitcast(U32)).then_inc(top_kept, 1)

            stats(sa, Step(0, 0), a_x, a_st)
            dve.wait_ge(sa.stats, 1)
            moments(sa, Step(0, 0), a_st, a_mv)
            for t in range(4):
                step_a(Step(t // 2, t % 2))
            with dve.Fori(2, 9) as m:
                for par in range(2):
                    step_a(Step(m, par))
            step_a(Step(9, 0), second=True)
            for g in range(2):
                dve.wait_ge(st_ps, BT)
                last = dve.tensor_tensor(a_kvm[0][g], bank[3 + g][:, 0:P], headmask[:, :, :].rearrange("p a b -> p (a b)"),
                                         ALU.mult)
            last.then_inc(kvm_r, 1)
            step_a(Step(9, 1), second=True)
            with dve.Fori(10, NT // 2 - 1) as m:
                for par in range(2):
                    step_a(Step(m, par), second=True)
            for t in (30, 31, 32, 33):
                step_a(Step(t // 2, t % 2), second=True)
            for g in range(2):
                dve.wait_ge(st_ps, NT)
                last = dve.tensor_tensor(a_kvm[1][g], bank[3 + g][:, 0:P], headmask[:, :, :].rearrange("p a b -> p (a b)"),
                                         ALU.mult)
            last.then_inc(kvm_r, 1)

            dve.wait_ge(qrot, NT)
            dve.wait_ge(top_kept, TOPK * NT)
            tv, ti = (v[:, :].rearrange("p (t k) -> p t k", k=TOPK) for v in (top_v, top_i))
            for par in range(2):
                dve.wait_ge(sa.xn_out[par], 16 * (NT // 2))
            link(dve.tensor_tensor(top_d, tv[:, :, 1], tv[:, :, 0], ALU.subtract))
            dve.sem_inc(d_sb, 1)
            for k in range(TOPK):
                link(dve.tensor_tensor(m_k[k], over_last(iota_e[:, :], NT), over_mid(ti[:, :, k], E), ALU.is_equal))
            dve.tensor_tensor(small_mask.rearrange("p (e t) -> p e t", e=E), m_k[0], m_k[1], ALU.add).then_inc(mask_r, 1)
            dve.wait_ge(e_sb, 1)
            link(dve.tensor_scalar(top_w[:, 0, :], top_e, 1.0, None, ALU.add))
            link(dve.reciprocal(top_w[:, 0, :], top_w[:, 0, :]))
            link(dve.tensor_tensor(top_w[:, 1, :], top_w[:, 0, :], top_e, ALU.mult))
            for k in range(TOPK):
                link(dve.tensor_tensor(r_tmp[k], m_k[k], over_mid(top_w[:, k, :], E), ALU.mult))
            dve.tensor_tensor(gates.rearrange("p t e -> p e t"), r_tmp[0], r_tmp[1], ALU.add)\
               .then_inc(gates_r, 1)
            dve.wait_ge(rank_ps, 1)
            rank_v = bank[1][:, 0:E * NT].rearrange("p (e t) -> p e t", e=E)
            tot_v = bank[1][:, E * NT:2 * E * NT]
            link(dve.tensor_tensor_scan(incl.rearrange("p e t -> p (e t)"), not_first[:, :, :].rearrange("p e t -> p (e t)"),
                                        tot_v, 0.0, ALU.mult, ALU.add))
            link(dve.tensor_tensor(excl, incl, tot_v.rearrange("p (e t) -> p e t", e=E), ALU.subtract))
            link(dve.tensor_tensor(r_tmp[0], over_last(incl[:, :, NT - 1], NT), over_mid(iota_128m[:, :], E), ALU.is_gt))
            link(dve.tensor_reduce(n_tiles, r_tmp[0], AX, ALU.add))
            link(dve.tensor_tensor_scan(t_incl, one8[:, :], n_tiles, 0.0, ALU.mult, ALU.add))
            link(dve.tensor_tensor(t_excl, t_incl, n_tiles, ALU.subtract))
            link(dve.tensor_tensor(excl, excl, rank_v, ALU.add))
            link(dve.scalar_tensor_tensor(excl, over_last(t_excl, NT), float(P), excl, ALU.mult, ALU.add))
            for k in range(TOPK):
                link(dve.tensor_tensor(r_tmp[k], m_k[k], excl, ALU.mult))
                link(dve.tensor_reduce(slot_f[:, k, :], r_tmp[k].rearrange("p e t -> p t e"), AX, ALU.add))
            link(dve.tensor_copy(slot_i[:, 0, :], slot_f.rearrange("p k t -> p (k t)")))
            link(dve.tensor_scalar(slot_i[:, 1, :], slot_i[:, 0, :], 7, None, ALU.logical_shift_right))
            link(dve.tensor_scalar(slot_i[:, 0, :], slot_i[:, 0, :], P - 1, None, ALU.bitwise_and))
            link(dve.tensor_copy(slot_lh.rearrange("p a n -> p (a n)"), slot_i.rearrange("p a n -> p (a n)")))
            t1 = r_big[:, 0:ST0 * E].rearrange("p (j e) -> p j e", e=E)
            t2 = r_big[:, ST0 * E:2 * ST0 * E].rearrange("p (j e) -> p j e", e=E)
            link(dve.tensor_tensor(t1, over_last(iota_t[:, :], E), over_mid(t_incl, ST0), ALU.is_ge))
            link(dve.tensor_tensor(t2, over_last(iota_t[:, :], E), over_mid(t_excl, ST0), ALU.is_ge))
            link(dve.tensor_tensor(tile_1h[:, :].rearrange("p (j e) -> p j e", e=E), t2, t1, ALU.subtract))
            link(dve.tensor_reduce(te_f, t1, AX, ALU.add))
            link(dve.tensor_scalar(tile_e[:, :], te_f, float(E - 1), None, ALU.min))

            def step_b(s):
                for j in range(GB):
                    if j == 0 and s.at_least(2):
                        dve.wait_ge(inv_ps, s.t - 1)
                    for n in (2 * j, 2 * j + 1):
                        col = ds(GN * s.t + n, 1)
                        dve.tensor_scalar(hot_lo[:, s.par, n, :], iota_p[:, :], slot_lh[:, 0, col], None, ALU.is_equal)
                        last = dve.tensor_scalar(hot_hi[:, s.par, n, :], iota_t[:, :], slot_lh[:, 1, col],
                                                 number1[:, col], ALU.is_equal, ALU.mult)
                    if j == GB - 1:
                        last.then_inc(hot_r, 1)
                    if j == 0:
                        dve.wait_ge(xb_in[s.par], 16 * (s.half + 1))
                        if s.at_least(2):
                            dve.wait_ge(x1_out[s.par], 16 * s.half)
                    dve.wait_ge(ao_ps, GB * s.t + j + 1)
                    dve.tensor_tensor(b_x1[:, s.par, j, :], bank[attn_bank[j]][:, 0:D], b_xb[:, s.par, j, :], ALU.add)\
                       .then_inc(ao_sb, 1)

            dve.wait_ge(sa.xb, NT)
            step_b(Step(0, 0))
            step_b(Step(0, 1))
            with dve.Fori(1, SB // 2) as m:
                for par in range(2):
                    step_b(Step(m, par))

            dve.wait_ge(inv_ps, SB)
            link(dve.tensor_copy(inv_f, bank[0][:, 0:ST0]))
            link(dve.tensor_scalar(inv_z, inv_f, 0.0, BIG, ALU.is_equal, ALU.mult))
            link(dve.scalar_tensor_tensor(idx0[:, :], inv_f, -0.75, inv_z, ALU.add, ALU.add))
            end_stage(dve, 1)

            def step_c(s):
                if in_range(s, ST0):
                    e1 = dve.value_load(tile_e[0:1, ds(s.t, 1)], min_val=0, max_val=E - 1)
                    if s.at_least(2):
                        dve.wait_ge(hT_ps, s.t - 1)
                    dve.tensor_copy(c_w1[:, s.par, :, :].rearrange("p c n -> p (c n)").unsqueeze(1),
                                    r1[:, ds(e1, 1), 0:DC * H]).then_inc(w1_r, 1)
                    dve.wait_ge(xg_in[s.par], 16 * (s.half + 1))
                    dve.scalar_tensor_tensor(c_gt[:, s.par, :], c_xg[:, s.par, D:ROW], 1.0, tile_1h[:, ds(s.t * E, E)],
                                             ALU.mult, ALU.mult, accum_out=gate0[:, ds(s.t, 1)]).then_inc(gate_r, 1)
                if s.at_least(1) and in_range(s.back(1), ST0):
                    b = s.back(1)
                    dve.wait_ge(relu_sb, b.t + 1)
                    if b.at_least(2):
                        dve.wait_ge(y_ps, b.t - 1)
                    dve.tensor_tensor(c_hT[:, b.par, :, :].rearrange("p c n -> p (c n)"), c_r[:, b.par, :],
                                      c_r[:, b.par, :], ALU.mult).then_inc(hT_sb, 1)
                if s.at_least(2) and in_range(s.back(2), ST0):
                    b = s.back(2)
                    dve.wait_ge(y_ps, b.t + 1)
                    dve.wait_ge(gate_r, b.t + 1)
                    if b.at_least(2):
                        dve.wait_ge(y_out, 16 * (b.t - 1))
                    dve.tensor_scalar(c_y[:, b.par, :], bank[5 + b.par][:, 0:D], gate0[:, ds(b.t, 1)], None, ALU.mult)\
                       .then_inc(y_sb, 1)

            for t in range(4):
                step_c(Step(t // 2, t % 2))
            with dve.Fori(2, ST0 // 2) as m:
                for par in range(2):
                    step_c(Step(m, par))
            for t in (ST0, ST0 + 1):
                step_c(Step(t // 2, t % 2))
            end_stage(dve, 2)

            def step_d(s):
                if in_range(s, NT):
                    stats(sd, s, d_x, d_st)
                    if not s.at_least(2):
                        dve.wait_ge(sd.stats, s.t + 1)
                        moments(sd, s, d_st, d_mv)
                if s.at_least(2) and in_range(s.back(2), NT):
                    b = s.back(2)
                    dve.wait_ge(v1_ps, b.t + 1)
                    if in_range(s, NT):
                        dve.wait_ge(sd.stats, s.t + 1)
                    dve.tensor_tensor(r2[:, ds(b.t * D, D)], bank[3 + b.par][:, 0:D], bv1_s[:, :], ALU.add)\
                       .then_inc(v1_sb, 1)
                    if in_range(s, NT):
                        moments(sd, s, d_st, d_mv)
                    dve.wait_ge(sc_sb, b.t + 1)
                    dve.tensor_copy(sc_all[:, :, ds(b.t, 1)], d_sc[:, b.par, :].unsqueeze(2)).then_inc(sc_kept, 1)
                if in_range(s, NT):
                    normalise(sd, s, d_x, d_mv, d_sd, d_rs, d_xn)

            for t in range(4):
                step_d(Step(t // 2, t % 2))
            with dve.Fori(2, NT // 2) as m:
                for par in range(2):
                    step_d(Step(m, par))
            for t in (NT, NT + 1):
                step_d(Step(t // 2, t % 2))
            dve.wait_ge(sc_kept, NT)
            dve.tensor_reduce(pmax[:, :], sc_all[:, :, :], AX, ALU.max).then_inc(pm_r, 1)
            end_stage(dve, 3)

            def judge(r, bk, first=False):
                dve.wait_ge(cnt_ps, r + 1)
                count = bank[bk][:, D:D + E]
                if first:
                    dve.tensor_scalar(flip[:, :], count, CAP - 0.5, -1.0, ALU.is_lt, ALU.mult).then_inc(cnt_used, 1)
                else:
                    dve.tensor_scalar(got[:, :], count, CAP - 0.5, -1.0, ALU.is_ge, ALU.mult).then_inc(cnt_used, 1)
                    dve.wait_ge(cnt_used, r + 1)
                    dve.scalar_tensor_tensor(key[:, :], got[:, :], bit_i[:, ds(r, 1)], key[:, :],
                                             ALU.bitwise_and, ALU.bitwise_or).then_inc(key_r, 1)

            def propose(r, half, first=False):
                if not first:
                    dve.wait_ge(cnt_used, r)
                    dve.wait_ge(key_r, r)
                    dve.scalar_tensor_tensor(thr[:, :], key[:, :], bit_i[:, ds(r, 1)], flip[:, :],
                                             ALU.bitwise_or, ALU.bitwise_xor).then_inc(thr_r, 1)
                dve.wait_ge(thr_r, r + 1)
                dve.tensor_tensor(e_cmp[:, :, :], sc_all[:, :, :], over_last(thr[:, :].bitcast(F32), NT),
                                  ALU.is_ge).then_inc(cmp_r, 1)
                dve.wait_ge(cmp_r, r + 1)
                with nc.allow_low_precision(reason="counts up to 32 are exact in bfloat16"):
                    dve.tensor_reduce(e_part[:, half, :], e_cmp[:, :, :], AX, ALU.add).then_inc(part_r, 1)

            def step_e(s, search=False, first=False, last=False):
                if in_range(s, NT):
                    dve.wait_ge(s_ps, s.t + 1)
                    sv = banks47[:, :, 0:P].rearrange("p g (j k) -> p g j k", j=2)
                    dve.tensor_reduce(e_mx.rearrange("p (g j) -> p g j", g=4), sv, AX, ALU.max).then_inc(mx_r, 1)
                    dve.wait_ge(mx_r, s.t + 1)
                    if s.at_least(1):
                        dve.wait_ge(p_r, s.t)
                    dve.tensor_tensor(e_s.rearrange("p (g j) k -> p g j k", g=4), sv,
                                      e_mx.rearrange("p (g j) -> p g j", g=4).unsqueeze(3).broadcast_to([P, 4, 2, BLK]),
                                      ALU.subtract).then_inc(sub_r, 1)
                if search:
                    judge(2 * s.t, 3, first=first)
                    if first:
                        link(dve.memset(key[:, :], 0))
                        dve.sem_inc(key_r, 1)
                    propose(2 * s.t + 1, 1)
                if s.at_least(1) and in_range(s.back(1), NT):
                    b = s.back(1)
                    dve.wait_ge(o_ps, b.t + 1)
                    dve.reciprocal(e_rc[:, b.par, :], bank[1][:, D:D + NH1]).then_inc(rc_r, 1)
                    dve.wait_ge(rc_r, b.t + 1)
                    if b.at_least(2):
                        dve.wait_ge(oT_ps, b.t - 1)
                    dve.tensor_tensor(e_o[:, b.par, :].rearrange("p (h d) -> p h d", h=NH1),
                                      bank[1][:, 0:D].rearrange("p (h d) -> p h d", h=NH1),
                                      over_last(e_rc[:, b.par, :], DK), ALU.mult).then_inc(o_sb, 1)
                if search:
                    judge(2 * s.t + 1, 2)
                    if not last:
                        propose(2 * s.t + 2, 0)

            link(dve.memset(thr[:, :], 0))
            dve.sem_inc(thr_r, 1)
            propose(0, 0, first=True)
            step_e(Step(0, 0), search=True, first=True)
            for t in range(1, 4):
                step_e(Step(t // 2, t % 2), search=True)
            with dve.Fori(2, SR // 2 - 1) as m:
                for par in range(2):
                    step_e(Step(m, par), search=True)
            step_e(Step(SR // 2 - 1, 0), search=True)
            step_e(Step(SR // 2 - 1, 1), search=True, last=True)
            step_e(Step(SR // 2, 0))

            dve.wait_ge(key_r, NT)
            link(dve.tensor_tensor(thr[:, :], key[:, :], flip[:, :], ALU.bitwise_xor))
            tau = over_last(thr[:, :].bitcast(F32), NT)
            both = s_both.rearrange("p (k e t) -> p k e t", k=2, e=E)
            before = s_before.rearrange("p (k e t) -> p k e t", k=2, e=E)
            dve.tensor_tensor(both[:, 0], sc_all[:, :, :], tau, ALU.is_gt)
            link(dve.tensor_tensor(both[:, 1], sc_all[:, :, :], tau, ALU.is_equal))
            for k in range(2):
                last = dve.tensor_tensor_scan(s_in[k].rearrange("p e t -> p (e t)"),
                                              not_first[:, :, :].rearrange("p e t -> p (e t)"),
                                              s_both[:, k * E * NT:(k + 1) * E * NT], 0.0, ALU.mult, ALU.add)
            link(last)
            for k in range(2):
                dve.tensor_tensor(before[:, k], s_in[k], both[:, k], ALU.subtract)
            dve.tensor_copy(s_tot, s_in[0][:, :, NT - 1]).then_inc(both_r, 1)
            step_e(Step(SR // 2, 1))

            dve.wait_ge(rank1_ps, 1)
            for k in range(2):
                dve.tensor_copy(s_ex[k].rearrange("p e t -> p (e t)"), bank[3 - k][:, D:2 * D])
            link(dve.tensor_scalar(s_need, bank[1][:, 2 * D - E:2 * D], -1.0, float(CAP), ALU.mult, ALU.add))
            dve.sem_inc(rank1_used, 1)
            step_e(Step(SR // 2 + 1, 0))

            need = over_last(s_need, NT)
            link(dve.tensor_tensor(s_in[0], s_ex[1], need, ALU.is_lt))
            link(dve.tensor_tensor(s_in[0], s_in[0], both[:, 1], ALU.mult))
            dve.tensor_tensor(s_ex[1], s_ex[1], need, ALU.min)
            link(dve.tensor_tensor(s_in[0], s_in[0], both[:, 0], ALU.add))
            link(dve.tensor_tensor(s_ex[0], s_ex[0], s_ex[1], ALU.add))
            dve.wait_ge(ex_r, 1)
            link(dve.tensor_tensor(s_exp, s_exp, s_in[0], ALU.mult))
            dve.tensor_reduce(s_zp, s_exp, AX, ALU.add).then_inc(z_r, 1)
            step_e(Step(SR // 2 + 1, 1))

            link(dve.scalar_tensor_tensor(s_ex[0], s_ex[0], -BIG, s_in[0], ALU.add, ALU.mult))
            link(dve.tensor_scalar(s_ri[0], s_ex[0], BIG, None, ALU.add))
            link(dve.tensor_scalar(s_ri[1], s_ri[0], 4, None, ALU.logical_shift_right))
            link(dve.tensor_scalar(s_ri[0], s_ri[0], 15, None, ALU.bitwise_and))
            dve.tensor_copy(s_ex[1], s_ri[1])
            link(dve.tensor_copy(s_ex[0], s_ri[0]))
            iota32 = over_mid(iota_p[:, 0:32], E)
            iota16 = over_mid(iota_p[:, 0:16], E)

            def hot1(s):
                first = HT * s.t - HT * SH
                for k in range(HT):
                    c = ds(first + k, 1)
                    dve.tensor_tensor(hot1_hi[:, c, :].rearrange("p c (e k) -> p (c e) k", e=E), iota32,
                                      s_ex[1][:, :, c].broadcast_to([P, E, 32]), ALU.is_equal)
                    last = dve.tensor_tensor(hot1_lo[:, c, 1, :, :].rearrange("p c e m -> p (c e) m"), iota16,
                                             s_ex[0][:, :, c].broadcast_to([P, E, 16]), ALU.is_equal)
                last.then_inc(lo_r, 1)
                dve.wait_ge(lo_r, 2 * (s.t - SH) + 1)
                for k in range(HT):
                    c = ds(first + k, 1)
                    last = dve.tensor_scalar(hot1_lo[:, c, 0, :, :], hot1_lo[:, c, 1, :, :], pid0[:, :], None, ALU.mult)
                last.then_inc(lo_r, 1)
                dve.wait_ge(lo_r, 2 * (s.t - SH) + 2)
                for k in range(HT):
                    c = ds(first + k, 1)
                    last = dve.tensor_scalar(hot1_lo[:, c, 1, :, :], hot1_lo[:, c, 1, :, :], iota_t[:, c], None, ALU.mult)
                last.then_inc(hot1_r, 1)

            with dve.Fori(SH // 2, (SH + NT // HT) // 2) as m:
                for par in range(2):
                    step_e(Step(m, par))
                    hot1(Step(m, par))
            t = SH + NT // HT
            step_e(Step(t // 2, 0))

            dve.wait_ge(z_ps, 1)
            dve.reciprocal(rz[:, :], bank[1][:, 2 * D - E:2 * D]).then_inc(rz_r, 1)
            dve.wait_ge(inv1_ps, 1)
            for q in range(2):
                last = dve.tensor_copy(s_iv[q], bank[3][:, D + q * P:D + (q + 1) * P]
                                       .rearrange("p (k g n) -> p k g n", k=2, g=4))
            link(last)
            dve.sem_inc(inv1_used, 1)
            step_e(Step(t // 2, 1))
            for q in range(2):
                for g in range(4):
                    pq = slice(32 * g, 32 * g + 32)
                    last = dve.scalar_tensor_tensor(s_id[pq, q, :], s_iv[q][pq, 1, g, :], float(P),
                                                    s_iv[q][pq, 0, g, :], ALU.mult, ALU.add)
            link(last)
            for q in range(2):
                for g in range(4):
                    pq = slice(32 * g, 32 * g + 32)
                    for a in range(4):
                        last = dve.tensor_copy(idx1[32 * a:32 * a + 32, 4 * (4 * q + g):4 * (4 * q + g) + 4],
                                               s_id[pq, q, 4 * a:4 * a + 4])
            last.then_inc(idx1_r, 1)
            for t in range(SH + NT // HT + 2, NT + 1):
                step_e(Step(t // 2, t % 2))
            end_stage(dve, 4)

            def step_f(s, e):
                for hb in range(HC):
                    dve.wait_ge(g_r, HC * s.t + hb + 1)
                    if s.at_least(2):
                        dve.wait_ge(fy_ps, TE * (s.t - 1))
                    dve.tensor_tensor(f_h[:, s.par, hb, :], f_g[:, hb % 2, :], bank[2 * (hb % 2) + 1][:, :], ALU.mult)\
                       .then_inc(hh_r, 1)
                dve.wait_ge(fwe_r, s.t + 1)
                dve.tensor_scalar(f_wg[:, s.par, :], f_we[:, s.par, :], rz[:, ds(e, 1)], None, ALU.mult).then_inc(fwg_r, 1)
                dve.wait_ge(fwg_r, s.t + 1)
                if s.at_least(1):
                    dve.wait_ge(fy_out, 16 * TE * s.t)
                for i in range(TE):
                    dve.wait_ge(fy_ps, TE * s.t + i + 1)
                    dve.tensor_scalar(f_y[:, i, :], bank[6 + i % 2][:, 0:D], f_wg[:, s.par, i:i + 1], None, ALU.mult)\
                       .then_inc(fy_sb, 1)

            for t in range(2):
                step_f(Step(0, t), t)
            with dve.Fori(1, E // 2) as m:
                for par in range(2):
                    step_f(Step(m, par), 2 * m + par)

        @block.gpsimd
        def _(pool):
            chain = [0]

            def link(ins):
                chain[0] += 1
                ins.then_inc(pseq, 1)
                pool.wait_ge(pseq, chain[0])

            link(pool.memset(ident[:, :], 0.0))
            pool.affine_select(out=ident[:, :], in_=ident[:, :], compare_op=ALU.not_equal, fill=1.0, base=0,
                               pattern=[[-1, P]], channel_multiplier=1)
            pool.memset(eps_c[:, :], EPS)
            link(pool.memset(ones[:, :], 1.0))
            pool.affine_select(out=upper[:, :], in_=ones[:, :], compare_op=ALU.is_gt, fill=0.0, base=0,
                               pattern=[[1, P]], channel_multiplier=-1)
            link(pool.memset(headmask[:, :, :], 0.25))
            hm = headmask[:, :, :].rearrange("p r (h j) -> p r h j", h=8)
            link(pool.affine_select(out=hm, in_=hm, compare_op=ALU.is_ge, fill=0.0, base=0,
                                    pattern=[[0, 2], [-HD0, 8], [0, JR]], channel_multiplier=1))
            link(pool.affine_select(out=hm, in_=hm, compare_op=ALU.is_ge, fill=0.0, base=HD0 - 1,
                                    pattern=[[0, 2], [HD0, 8], [0, JR]], channel_multiplier=-1))
            pool.iota(iota_e[:, :], pattern=[[1, E]], base=0, channel_multiplier=0, allow_small_or_imprecise_dtypes=True)
            pool.iota(iota_p[:, :], pattern=[[1, P]], base=0, channel_multiplier=0, allow_small_or_imprecise_dtypes=True)
            pool.iota(iota_t[:, :], pattern=[[1, ST0]], base=0, channel_multiplier=0, allow_small_or_imprecise_dtypes=True)
            pool.iota(iota_128m[:, :], pattern=[[P, NT]], base=0, channel_multiplier=0, allow_small_or_imprecise_dtypes=True)
            pool.iota(pid1[:, :], pattern=[[0, 1]], base=1, channel_multiplier=1, allow_small_or_imprecise_dtypes=True)
            pool.iota(pid0[:, :], pattern=[[0, 1]], base=0, channel_multiplier=1, allow_small_or_imprecise_dtypes=True)
            pool.iota(number1[:, :], pattern=[[0, TOPK], [P, NT]], base=1, channel_multiplier=1,
                      allow_small_or_imprecise_dtypes=True)
            pool.memset(one8[:, :], 1.0)
            link(pool.memset(not_first[:, :, :], 1.0))
            link(pool.memset(not_first[:, :, 0:1], 0.0))
            for i in range(1, NT):
                last = pool.memset(bit_i[:, i:i + 1], 1 << (NT - 1 - i))
            link(last)
            pool.sem_inc(made, 1)
            last_row = pool.to_reg(N - 1)
            pool.wait_ge(consts, 16 * 7)

            def add_bias(z, s, xt, xb, bo):
                pool.wait_ge(z.x_in[s.par], 16 * (s.half + 1))
                if s.at_least(2):
                    pool.wait_ge(z.xb_out[s.par], 16 * s.half)
                pool.tensor_tensor(xb[:, s.par, :], xt[:, s.par, :], bo[:, :], ALU.add).then_inc(z.xb, 1)

            def step_a(s, second):
                if in_range(s, NT):
                    add_bias(sa, s, a_x, a_xb, bo0_s)
                if s.at_least(2) and in_range(s.back(2), NT):
                    b = s.back(2)
                    tb = b.t - BT if second else b.t
                    pool.wait_ge(q_sb, 2 * (b.t + 1))
                    q = a_q[:, b.par, :, :]
                    t = [a_pt[:, i, :].rearrange("p (r n) -> p r n", r=2) for i in range(2)]
                    cq = cosq_s[:, ds(tb * P, P)]
                    if not b.at_least(1):
                        pool.wait_ge(tables, 16 * 2)
                    if b.at_least(1):
                        pool.wait_ge(qrot, b.t)
                    for r in range(2):
                        pool.tensor_tensor(t[0][:, r, :], q[:, r, :], cq, ALU.mult)
                        last = pool.tensor_tensor(t[1][:, r, :], q[:, 1 - r, :], sinq_s[:, r, ds(tb * P, P)], ALU.mult)
                    last.then_inc(qprod, 1)
                    pool.wait_ge(qprod, b.t + 1)
                    pool.tensor_tensor(qrot_all[:, :, ds(b.t * P, P)], t[0], t[1], ALU.add).then_inc(qrot, 1)

            for t in range(4):
                step_a(Step(t // 2, t % 2), False)
            with pool.Fori(2, 9) as m:
                for par in range(2):
                    step_a(Step(m, par), False)
            with pool.Fori(9, NT // 2) as m:
                for par in range(2):
                    step_a(Step(m, par), True)
            for t in (32, 33):
                step_a(Step(t // 2, t % 2), True)
            end_stage(pool, 1)

            pool.memset(c_xg, 0.0).then_inc(xg_clear, 1)
            pool.wait_ge(xg_clear, 1)

            def gather(s):
                if s.at_least(2):
                    pool.wait_ge(xg_in[s.par], 16 * s.half)
                pool.tensor_copy(c_gi[:, s.par:s.par + 1], idx0[:, ds(s.t, 1)]).then_inc(gi_r, 1)
                pool.wait_ge(gi_r, s.t + 1)
                if s.at_least(2):
                    pool.wait_ge(cT_ps, s.t - 1)
                    pool.wait_ge(gate_r, s.t - 1)
                pool.nop(nofuse=True)
                pool.indirect_dma_start(c_xg[:, s.par, :], None, xg0_d[:, :],
                                        bass.IndirectOffsetOnAxis(c_gi[:, s.par:s.par + 1], 0),
                                        bounds_check=last_row, oob_is_err=False).then_inc(xg_in[s.par], 16)

            def scatter(s):
                if s.at_least(1):
                    pool.wait_ge(y_out, 16 * s.t)
                pool.tensor_copy(c_si[:, s.par:s.par + 1], idx0[:, ds(s.t, 1)]).then_inc(si_r, 1)
                pool.wait_ge(si_r, s.t + 1)
                pool.wait_ge(y_sb, s.t + 1)
                pool.nop(nofuse=True)
                pool.indirect_dma_start(x1_d[:, :], bass.IndirectOffsetOnAxis(c_si[:, s.par:s.par + 1], 0),
                                        c_y[:, s.par, :], None, bounds_check=last_row, oob_is_err=False,
                                        compute_op=ALU.add).then_inc(y_out, 16)

            for t in range(5):
                gather(Step(t // 2, t % 2))
            scatter(Step(0, 0))
            gather(Step(2, 1))
            with pool.Fori(3, ST0 // 2) as m:
                for par in range(2):
                    s = Step(m, par)
                    scatter(s.back(5))
                    gather(s)
            for t in range(ST0 - 5, ST0):
                scatter(Step(t // 2, t % 2))
            pool.wait_ge(y_out, 16 * ST0)
            end_stage(pool, 2)

            for t in range(2):
                add_bias(sd, Step(0, t), d_x, d_xb, bo1_s)
            with pool.Fori(1, NT // 2) as m:
                for par in range(2):
                    add_bias(sd, Step(m, par), d_x, d_xb, bo1_s)
            end_stage(pool, 3)

            for i in range(2):
                pool.memset(e_v[:, i], 0.0)
            link(pool.memset(e_one[:, :], 0.0))
            for i in range(2):
                link(pool.memset(e_one[BLK * i:BLK * i + BLK, i:i + 1], 1.0))
            link(pool.memset(onesf, 1.0))
            pool.sem_inc(vz, 1)
            pool.wait_ge(pm_r, 1)
            pool.partition_all_reduce(scmax[:, :], pmax[:, :], P, RMAX).then_inc(gmax_r, 1)
            pool.wait_ge(gmax_r, 1)
            pool.tensor_scalar(nscmax[:, :], scmax[:, :], -1.0, None, ALU.mult).then_inc(ngm_r, 1)

            def add_x(s):
                pool.wait_ge(y1_sb, s.t + 1)
                pool.wait_ge(xbl[s.par], 16 * (s.half + 1))
                pool.tensor_tensor(e_y[:, s.par, :], e_y[:, s.par, :], e_xb[:, s.par, :], ALU.add).then_inc(fin_r, 1)

            def gather1(s, e):
                if s.at_least(2):
                    pool.wait_ge(fT_ps, s.t - 1)
                    pool.wait_ge(fwe_r, s.t - 1)
                if s.at_least(1):
                    pool.wait_ge(fx_in[(s.back(1)).par], 16 * TE * (s.back(1).half + 1))
                pool.tensor_copy(f_gi[:, :], idx1[:, ds(e * TE, TE)]).then_inc(fgi_r, 1)
                pool.wait_ge(fgi_r, s.t + 1)
                for i in range(TE):
                    pool.nop(nofuse=True)
                    pool.indirect_dma_start(f_xg[:, s.par, i, :], None, xg1_d[:, :],
                                            bass.IndirectOffsetOnAxis(f_gi[:, i:i + 1], 0),
                                            bounds_check=last_row, oob_is_err=False).then_inc(fx_in[s.par], 16)

            with pool.Fori(0, NT // 2 - 2) as m:
                for par in range(2):
                    add_x(Step(m, par))
            pool.wait_ge(qkl[0], 16 * 9)
            pool.wait_ge(qkl[1], 16 * 8)
            pool.wait_ge(idx1_r, 1)
            gather1(Step(0, 0), 0)
            for t in range(NT - 4, NT):
                add_x(Step(t // 2, t % 2))
            end_stage(pool, 4)

            def scatter1(s, e):
                if s.at_least(1):
                    pool.wait_ge(fy_out, 16 * TE * s.t)
                pool.tensor_copy(f_si[:, :], idx1[:, ds(e * TE, TE)]).then_inc(fsi_r, 1)
                pool.wait_ge(fsi_r, s.t + 1)
                for i in range(TE):
                    pool.wait_ge(fy_sb, TE * s.t + i + 1)
                    pool.nop(nofuse=True)
                    pool.indirect_dma_start(out[:, :], bass.IndirectOffsetOnAxis(f_si[:, i:i + 1], 0),
                                            f_y[:, i, :], None, bounds_check=last_row, oob_is_err=False,
                                            compute_op=ALU.add).then_inc(fy_out, 16)

            gather1(Step(0, 1), 1)
            for t in (2, 3):
                gather1(Step(1, t - 2), t)
                scatter1(Step(0, t - 2), t - 2)
            with pool.Fori(2, E // 2) as m:
                for par in range(2):
                    s = Step(m, par)
                    gather1(s, 2 * m + par)
                    scatter1(s.back(2), 2 * m + par - 2)
            for t in (E - 2, E - 1):
                scatter1(Step(t // 2, t % 2), t)


def kernel(**inputs):
    import numpy as np
    import concourse.bacc as bacc
    from concourse.bass_utils import run_bass_kernel_spmd

    a = {k: np.asarray(v) for k, v in inputs.items()}

    pairs = np.arange(D).reshape(NH0 * JR, 2).T.reshape(-1)
    wq, wk, wv = (a["L0_attn_" + n] for n in ("Wq", "Wk", "Wv"))
    heads = np.arange(D).reshape(2, NH1 // 2, DK).transpose(1, 0, 2).reshape(-1)

    scale = np.arange(0, HD0, 2, dtype=np.float32)[:JR]
    with np.errstate(over="ignore"):
        freqs = np.float32(1.0) / np.power(np.float32(10000.0), scale)
    angles = np.arange(L, dtype=np.float32)[:, None] * freqs[None, :]
    cos = np.cos(angles.astype(np.float64)).astype(np.float32)
    sin = np.sin(angles.astype(np.float64)).astype(np.float32)
    signed = np.stack([-sin, sin], axis=1)
    cos_k = cos.reshape(BT, P, JR).transpose(1, 0, 2).reshape(P, BT * JR)
    sin_k = signed.reshape(BT, P, 2, JR).transpose(1, 0, 2, 3).reshape(P, BT * 2 * JR)
    cos_q = np.tile(cos.T, (NH0, 1))
    sin_q = np.tile(signed.transpose(2, 1, 0), (NH0, 1, 1)).reshape(P, 2 * L)

    arrays = {
        "x": a["L0_attn_x"].reshape(N, D),
        "wqkv0": np.concatenate([wq[:, pairs], wk[:, pairs], wv], axis=1),
        "bq0": a["L0_attn_bq"][pairs].reshape(DC, P).T,
        "bkv0": np.concatenate([a["L0_attn_bk"][pairs], a["L0_attn_bv"]]),
        "wo0": a["L0_attn_Wo"], "bo0": a["L0_attn_bo"],
        "rw0": a["L0_ffn_router_w"].T,
        "w1_0": a["L0_ffn_w1"], "w2_0": a["L0_ffn_w2"],
        "wqkv1": np.concatenate([a["L1_attn_Wq"], a["L1_attn_Wk"], a["L1_attn_Wv"]], axis=1),
        "bqk1": np.concatenate([a["L1_attn_bq"], a["L1_attn_bk"]]).reshape(2 * DC, P).T, "bv1": a["L1_attn_bv"],
        "wo1": a["L1_attn_Wo"][heads], "bo1": a["L1_attn_bo"],
        "wg1": a["L1_ffn_Wg"].T,
        "w13_1": np.concatenate([a["L1_ffn_W1"].transpose(0, 2, 1), a["L1_ffn_W3"].transpose(0, 2, 1)], axis=2),
        "w2_1": a["L1_ffn_W2"].transpose(0, 2, 1),
        "cos_q": cos_q, "sin_q": sin_q, "cos_k": cos_k, "sin_k": sin_k,
    }
    arrays = {k: np.ascontiguousarray(v) for k, v in arrays.items()}

    nc = bacc.Bacc("TRN2", target_bir_lowering=False, num_devices=1)
    args = [nc.dram_tensor("in_" + k, v.shape, mybir.dt.from_np(v.dtype), kind="ExternalInput").ap()
            for k, v in arrays.items()]
    args.append(nc.dram_tensor("out_x", (N, D), F32, kind="ExternalOutput").ap())
    two_layers(nc, *args)
    r = run_bass_kernel_spmd(nc, [{"in_" + k: v for k, v in arrays.items()}], core_ids=[0])
    return r.results[0]["out_x"].reshape(NB, L, D)
```

```python
import concourse.bass as bass
from concourse import mybir
from contextlib import ExitStack

F32 = mybir.dt.float32
BF16 = mybir.dt.bfloat16
F32R = mybir.dt.float32r
I32 = mybir.dt.int32
U32 = mybir.dt.uint32
ALU = mybir.AluOpType
ACT = mybir.ActivationFunctionType
AX = mybir.AxisListType.X

P = 128
N, D = 4096, 256
NB, L = 2, 2048
NT = N // P
BT = L // P
DC = D // P
E, H = 8, 512
HC = H // P
TOPK = 2
NH0, HD0 = 16, 16
JR = HD0 // 2
NH1, DK = 8, 32
BLK = 64
CAP = N // E
ST0 = TOPK * N // P + E
ROW = D + E
BIG = 8192.0
EPS = 1e-5
ds = bass.ds
RMAX = bass.bass_isa.ReduceOp.max


def over_last(ap, n):
    return ap.unsqueeze(2).broadcast_to([ap.shape[0], ap.shape[1], n])


def over_mid(ap, n):
    return ap.unsqueeze(1).broadcast_to([ap.shape[0], n, ap.shape[1]])


class Step:

    def __init__(self, half, par):
        self.half, self.par, self.t = half, par, 2 * half + par

    def back(self, k):
        q = self.par - k
        return Step(self.half + (q >> 1), q & 1)

    def at_least(self, k):
        return not isinstance(self.half, int) or self.t >= k


def in_range(s, n):
    return not isinstance(s.half, int) or 0 <= s.t < n


def two_layers(nc, x, wqkv0, bq0, bkv0, wo0, bo0, rw0, w1_0, w2_0,
               wqkv1, bqk1, bv1, wo1, bo1, wg1, w13_1, w2_1, cos_q, sin_q, cos_k, sin_k, out):
    xg0_d = nc.dram_tensor("rows_layer0", [N, ROW], F32).ap()
    xg1_d = nc.dram_tensor("rows_layer1", [N, ROW], F32).ap()
    xb_d = nc.dram_tensor("x_plus_bias", [N, D], F32).ap()
    x1_d = nc.dram_tensor("x_layer1", [N, D], F32).ap()
    xb1_d = nc.dram_tensor("x1_plus_bias", [N, D], F32).ap()

    def rows(dram, t, lo=0, hi=D):
        return dram[ds(t * P, P), lo:hi]

    ctx = ExitStack()
    with ctx:
        def sb(name, shape, dt=F32):
            return ctx.enter_context(nc.sbuf_tensor(name, shape, dt))

        def sb_twice(name, shape):
            with nc.sbuf_tensor(name, shape, F32) as plain:
                pass
            return plain, sb(name + "_split", shape, F32R)

        def sem(name):
            return ctx.enter_context(nc.semaphore(name))

        def sem2(name):
            return [sem(name + "_even"), sem(name + "_odd")]

        wqkv0_s = sb("wqkv0_s", [P, DC, 3 * D])
        wo0_s = sb("wo0_s", [P, DC, D])
        wqkv1_s = sb("wqkv1_s", [P, DC, 3 * D])
        wo1_s = sb("wo1_s", [P, DC, D])
        rw0_s = sb("rw0_s", [P, DC, E])
        wg1_s = sb("wg1_s", [P, DC, E])
        bq0_s = sb("bq0_s", [P, DC])
        bqk1_s = sb("bqk1_s", [P, 2 * DC])
        bkv0_s = sb("bkv0_s", [P, 2 * D])
        bv1_s = sb("bv1_s", [P, D])
        bo0_s = sb("bo0_s", [P, D])
        bo1_s = sb("bo1_s", [P, D])
        cosk_s = sb("cosk_s", [P, BT * JR])
        sink_s = sb("sink_s", [P, BT * 2 * JR])
        ident = sb("ident", [P, P])
        headmask = sb("headmask", [P, 2, P // 2])
        eps_c = sb("eps_c", [P, 1])
        upper = sb("upper", [P, P], BF16)
        ones = sb("ones", [P, P], BF16)
        iota_e = sb("iota_e", [P, E])
        iota_p = sb("iota_p", [P, P], BF16)
        iota_t = sb("iota_t", [P, ST0])
        iota_128m = sb("iota_128m", [P, NT])
        pid1 = sb("pid1", [P, 1])
        number1 = sb("number1", [P, TOPK * NT])
        not_first = sb("not_first", [P, E, NT], BF16)
        bit_i = sb("bit_i", [P, NT], I32)

        r1, r1s = sb_twice("r1", [P, E, 2 * DC * H])
        r2, r2s = sb_twice("r2", [P, NT * D])
        r3f, r3s = sb_twice("r3", [P, (NT * E * 64 + 3 * E * NT) // 2])
        rt = sb("rt", [P, 3 * L])
        r3 = r3f[:, :].bitcast(BF16)
        rw, rws = sb_twice("rw", [P, 6272])

        qk_all = r1[:, :, :].rearrange("p e n -> p (e n)").rearrange("p (m n) -> p m n", m=4)
        qrot_all = r2[:, :].rearrange("p (c n) -> p c n", c=DC)
        v_all = r2[:, :].rearrange("p (t n) -> p t n", t=NT)
        cosq_s = rt[:, 0:L]
        sinq_s = rt[:, L:3 * L].rearrange("p (r n) -> p r n", r=2)

        top_v = sb("top_v", [P, NT * TOPK])
        top_i = sb("top_i", [P, NT * TOPK])
        pid0 = sb("pid0", [P, 1])
        one8 = sb("one8", [P, E])
        GB = 4
        GN = TOPK * GB
        hot_lo = r3f[:, 0:2 * GN * P].rearrange("p (b n m) -> p b n m", b=2, n=GN)
        o = 2 * GN * P
        hot_hi = r3f[:, o:o + 2 * GN * ST0].rearrange("p (b n m) -> p b n m", b=2, n=GN)
        o += 2 * GN * ST0
        b_q = r3f[:, o:o + 2 * DC * GB * P].rearrange("p (b c n) -> p b c n", b=2, c=DC)
        o += 2 * DC * GB * P
        b_xb = r3f[:, o:o + 2 * GB * D].rearrange("p (b j n) -> p b j n", b=2, j=GB)
        hot1_hi = r3[:, 0:NT * E * 32].rearrange("p (c m) -> p c m", c=NT)
        hot1_lo = r3[:, NT * E * 32:NT * E * 64].rearrange("p (c k e m) -> p c k e m", c=NT, k=2, e=E)

        taken = [0]

        def scratch(shape, dt=F32, reset=False):
            if reset:
                taken[0] = 0
            n = 1
            for k in shape:
                n *= k
            words = n if dt != BF16 else n // 2
            v = rt[:, taken[0]:taken[0] + words]
            taken[0] += words
            assert taken[0] <= 3 * L
            v = v if dt == F32 else v.bitcast(dt)
            if len(shape) == 2:
                v = v.rearrange("p (a b) -> p a b", a=shape[0])
            elif len(shape) == 3:
                v = v.rearrange("p (a b c) -> p a b c", a=shape[0], b=shape[1])
            return v

        m_k = [scratch([E, NT], reset=True), scratch([E, NT])]
        r_tmp = [scratch([E, NT]), scratch([E, NT])]
        incl, excl = scratch([E, NT]), scratch([E, NT])
        m_all = [scratch([2, D]), scratch([2, D])]
        r_big = scratch([2 * ST0 * E])
        small_mask = scratch([E * NT], BF16)
        top_d, top_e, top_w = scratch([NT]), scratch([NT]), scratch([TOPK, NT])
        n_tiles, t_incl, t_excl = scratch([E]), scratch([E]), scratch([E])
        slot_f, slot_i, slot_lh = scratch([TOPK, NT]), scratch([2, TOPK * NT], I32), scratch([2, TOPK * NT])
        te_f, inv_f, inv_z = scratch([ST0]), scratch([ST0]), scratch([ST0])
        gates = scratch([NT, E])
        s_both = scratch([2 * E * NT], BF16, reset=True)
        s_in = [scratch([E, NT]), scratch([E, NT])]
        s_before = scratch([2 * E * NT], BF16)
        s_tot = scratch([E])
        s_ex = [scratch([E, NT]), scratch([E, NT])]
        s_exp = scratch([E, NT])
        s_ri = [scratch([E, NT], I32), scratch([E, NT], I32)]
        s_zp, s_need = scratch([E]), scratch([E])
        s_iv = [scratch([2, 4, 16]), scratch([2, 4, 16])]
        s_id = scratch([2, 16])
        onesf = scratch([P])
        idx0 = sb("idx0", [P, ST0], I32)
        idx1 = sb("idx1", [P, E * (CAP // P)], I32)
        tile_e = sb("tile_e", [P, ST0], I32)
        tile_1h = sb("tile_1h", [P, ST0 * E], BF16)
        gate0 = sb("gate0", [P, ST0])
        tail = r3[:, NT * E * 64:NT * E * 64 + 3 * E * NT]
        sc_all = tail[:, 0:2 * E * NT].bitcast(F32).rearrange("p (e t) -> p e t", e=E)
        e_cmp = tail[:, 2 * E * NT:3 * E * NT].rearrange("p (e t) -> p e t", e=E)

        used = [0]

        def work(shape, reset=False, split=False):
            if reset:
                used[0] = 0
            n = 1
            for k in shape:
                n *= k
            v = (rws if split else rw)[:, used[0]:used[0] + n]
            used[0] += n
            assert used[0] <= 6272, used[0]
            if len(shape) == 2:
                v = v.rearrange("p (a b) -> p a b", a=shape[0])
            elif len(shape) == 3:
                v = v.rearrange("p (a b c) -> p a b c", a=shape[0], b=shape[1])
            elif len(shape) == 4:
                v = v.rearrange("p (a b c d) -> p a b c d", a=shape[0], b=shape[1], c=shape[2])
            return v

        bank = [ctx.enter_context(nc.psum_tensor(f"bank{i}", [P, 512], F32)) for i in range(4)]
        banks47 = ctx.enter_context(nc.psum_tensor("banks47", [P, 4, 512], F32))
        bank += [banks47[:, i, :] for i in range(4)]

        consts = sem("consts_loaded")
        tables, tables_b = sem("rotary_tables_of_q_loaded"), sem("their_second_half_loaded")
        consts_b = sem("late_consts_loaded")
        made = sem("constants_made")
        w0_in = sem("experts0_loaded")
        stage_end = sem("stage_ended")
        seq = sem("vector_chain")
        pseq = sem("pool_chain")

        def end_stage(eng, n):
            eng.drain().then_inc(stage_end, 1)
            eng.wait_ge(stage_end, 5 * n)

        block = ctx.enter_context(nc.Block())

        a_x = work([2, D], reset=True)
        a_xn = work([2, D])
        a_xT = work([2, DC, P])
        a_kv = work([2, 2 * D])
        a_kr = work([2, D])
        a_t = work([2, D])
        a_q = work([2, DC, P])
        a_pt = work([2, D])
        a_xb = work([2, D])
        a_lg = work([2, E])
        a_st = work([2, 6])
        a_mv = work([2, 2])
        a_sd = work([2, 1])
        a_rs = work([2, 1])
        a_top = work([2, E])
        a_ti = work([2, E])
        kvm = work([NB, DC, P])
        a_kvm = [[kvm[:, b, g, :] for g in range(DC)] for b in range(NB)]

        b_x1 = work([2, GB, D], reset=True)

        class S:
            pass

        def ln_sems(z):
            s = S()
            s.x_in = sem2(f"x_loaded_{z}")
            s.stats, s.moments, s.std = sem(f"stats_{z}"), sem(f"moments_{z}"), sem(f"std_{z}")
            s.rstd, s.xn = sem(f"rstd_{z}"), sem(f"xn_ready_{z}")
            s.xn_out = sem2(f"xn_stored_{z}")
            s.xb, s.xb_out = sem(f"xb_ready_{z}"), sem2(f"xb_stored_{z}")
            s.xT_ps, s.xT = sem(f"xT_in_psum_{z}"), sem(f"xT_ready_{z}")
            return s

        sa, sd = ln_sems("a"), ln_sems("d")
        kv_ps, kv_sb, lg_ps, lg_sb = sem("kv_in_psum"), sem("kv_ready"), sem("logits_in_psum"), sem("logits_ready")
        q_ps, q_sb = sem("q_in_psum"), sem("q_ready")
        top_m, top_done, top_kept = sem("top_placed"), sem("top_found"), sem("top_kept")
        kprod, krot = sem("k_products"), sem("k_rotated")
        qprod, qrot = sem("q_products"), sem("q_rotated")
        st_ps = sem("ktv_in_psum")

        mask_r, rank_ps = sem("pair_mask_ready"), sem("ranks_in_psum")
        hot_r, inv_ps = sem("one_hots_ready"), sem("slots_in_psum")
        SB = NT // GB
        attn_bank = (2, 3, 4, 7)
        top_de = sem("top_diff_and_exp")
        gates_r, gates_out = sem("gates_ready"), sem("gates_stored")
        bounds_r = sem("slot_tile_bounds_ready")
        kvm_r, m_ps, m_sb = sem("ktv_masked"), sem("m_in_psum"), sem("m_ready")
        ql_in, xb_in = sem2("q_tile_loaded"), sem2("xb_tile_loaded")
        ao_ps, ao_sb, x1_out = sem("attn0_in_psum"), sem("attn0_added"), sem2("x1_stored")

        c_xg = work([2, ROW], reset=True)
        c_xT = work([2, DC, P])
        c_r = work([2, H])
        c_w1 = rt[:, 0:2 * DC * H].rearrange("p (b c n) -> p b c n", b=2, c=DC)
        c_sq = work([H])
        c_hi = work([2, HC, P], split=True)
        c_lo = work([2, HC, P], split=True)
        w2_hi = r2s[:, :].rearrange("p (e n) -> p e n", e=E)
        c_y = work([2, D])
        c_gt = work([2, E])
        c_gi = sb("c_gi", [P, 2], I32)
        c_si = sb("c_si", [P, 2], I32)
        xg_clear, gi_r, si_r, xg_in = sem("rows_cleared"), sem("gather_index"), sem("scatter_index"), sem2("rows_gathered")
        w1_r, cT_ps, cT_sb = sem("w1_copied"), sem("rows_T_in_psum"), sem("rows_T_ready")
        hT_ps, relu_sb, sq_r = sem("hT_in_psum"), sem("relu_ready"), sem("square_ready")
        hi_r, lo_c = sem("hidden_high_ready"), sem("hidden_low_ready")
        w2hi_r, w2lo_r = sem("w2_high_ready"), sem("w2_low_ready")
        y_ps, y_sb = sem("y_in_psum"), sem("y_ready")
        gate_r, y_out = sem("gate_ready"), sem("y_scattered")

        d_x = work([2, D], reset=True)
        d_xn = work([2, D])
        d_xT = work([2, DC, P])
        d_xb = work([2, D])
        d_sc = work([2, E])
        d_st = work([2, 6])
        d_mv = work([2, 2])
        d_sd = work([2, 1])
        d_rs = work([2, 1])
        qk1_ps, qk1_sb, v1_ps, v1_sb = sem("qk1_in_psum"), sem("qk1_ready"), sem("v1_in_psum"), sem("v1_ready")
        sc_ps, sc_sb, sc_kept, sc_out = sem("scores_in_psum"), sem("scores_ready"), sem("scores_kept"), sem2("scores_stored")

        NP = NH1 // 2
        e_y = work([2, D], reset=True)
        e_xb = work([2, D])
        e_o = work([2, D])
        e_oT = work([2, DC, P])
        e_mx = work([NH1])
        e_rc = work([2, NH1])
        work([16])
        e_qk = work([2, 4, P])
        VC = DK + 1
        e_v = work([2, 2, 2, NP * VC]).rearrange("p s b h (g d) -> p s b h g d", d=VC)
        e_s = work([NH1, BLK])
        e_p = work([2, NH1, BLK])
        e_pT = work([NP, P])
        e_part = sb("e_part", [P, 2, E], BF16)
        key_r, thr_r, cmp_r = sem("key_kept"), sem("threshold_ready"), sem("compared")
        key = sb("key", [P, E], I32)
        thr = sb("thr", [P, E], I32)
        flip = sb("flip", [P, E], I32)
        got = sb("got", [P, E], I32)
        scmax = sb("scmax", [P, E])
        nscmax = sb("nscmax", [P, E])
        pmax = sb("pmax", [P, E])
        vz = sem("v_spread_cleared")
        qkl, vl, xbl = sem2("qk_tile_loaded"), sem2("v_tile_loaded"), sem2("xb1_tile_loaded")
        s_ps, mx_r, sub_r, p_r, rc_r = (sem("att_in_psum"), sem("row_max"), sem("shifted"), sem("exp_ready"),
                                        sem("row_rcp"))
        pT_ps, pT_sb, o_ps, o_sb, oT_ps, oT_sb = (sem("pT_in_psum"), sem("pT_ready"), sem("o_in_psum"), sem("o_ready"),
                                                  sem("oT_in_psum"), sem("oT_ready"))
        y1_ps, y1_sb, fin_r, fin_out = sem("y1_in_psum"), sem("y1_ready"), sem("final_ready"), sem2("final_stored")
        part_r, cnt_ps, cnt_used = sem("counts_ready"), sem("counts_in_psum"), sem("counts_used")
        gmax = sem("score_maximum")
        ex_r, zsum = sem("score_exp"), sem("exp_sums")
        lo_r = sem("low_one_hots_ready")
        hot1_r = sem("one_hots1_ready")
        SR = NT // 2
        SH, HT = 20, 4
        rank1 = sem("ranks1")
        slots1 = sem("slots1")

        f1 = r1[:, :, :].rearrange("p e n -> p (e n)")
        TE = CAP // P
        f_xg = f1[:, 0:2 * TE * ROW].rearrange("p (b i n) -> p b i n", b=2, i=TE)
        o1 = 2 * TE * ROW
        f1s = r1s[:, :, :].rearrange("p e n -> p (e n)")
        f_xhi, f_xlo = (f1s[:, o:o + 2 * DC * CAP].rearrange("p (b c n) -> p b c n", b=2, c=DC)
                        for o in (o1, o1 + 2 * DC * CAP))
        o2 = o1 + 4 * DC * CAP
        f_g = f1[:, o2:o2 + 2 * CAP].rearrange("p (b n) -> p b n", b=2)
        o3 = o2 + 2 * CAP
        f_hhi, f_hlo = (f1s[:, o:o + 2 * HC * CAP].rearrange("p (b c n) -> p b c n", b=2, c=HC)
                        for o in (o3, o3 + 2 * HC * CAP))
        W13, W2 = 2 * DC * H, HC * D
        f_y = r2[:, 2 * (W13 + W2):2 * (W13 + W2) + TE * D].rearrange("p (i n) -> p i n", i=TE)
        f_h = r2[:, 2 * (W13 + W2) + TE * D:2 * (W13 + W2) + TE * D + 2 * CAP].rearrange("p (b n) -> p b n", b=2)
        f_w = [rt[:, (W13 + W2) * b:(W13 + W2) * (b + 1)] for b in range(2)]
        f_whi = [r2s[:, 0:W13 + W2], r3s[:, 0:W13 + W2]]
        f_wlo = [r2s[:, W13 + W2:2 * (W13 + W2)], r3s[:, W13 + W2:2 * (W13 + W2)]]
        f_gi = sb("f_gi", [P, TE], I32)
        f_si = sb("f_si", [P, TE], I32)
        f_we = sb("f_we", [P, 2, TE])
        f_wg = sb("f_wg", [P, 2, TE])
        rz = sb("rz", [P, E])
        table_warm = sb("table_warm", [P, 1])
        fw13_in, fw2_in = sem2("w13_loaded"), sem2("w2_loaded")
        whi_r, wlo_r = sem("w13_high_ready"), sem("w13_low_ready")
        fgi_r, fsi_r, fx_in = sem("gather1_index"), sem("scatter1_index"), sem2("rows1_gathered")
        fT_ps, xhi_r, xlo_r, h13_ps, g_r = (sem("rows1_T_in_psum"), sem("rows1_high_ready"), sem("rows1_low_ready"),
                                            sem("h13_in_psum"), sem("silu_ready"))
        h1_r, hhi_r, hlo_r = sem("hidden1_ready"), sem("hidden1_high_ready"), sem("hidden1_low_ready")
        fy_ps, fy_sb, fwe_r, fwg_r, fy_out = (sem("y1e_in_psum"), sem("y1e_ready"), sem("weight_exp"),
                                              sem("weight_ready"), sem("y1e_scattered"))

        @block.sync
        def _(sp):
            def load_x(z, s, src, dst):
                sp.dma_start(dst[:, s.par, :], rows(src, s.t)).then_inc(z.x_in[s.par], 16)

            load_x(sa, Step(0, 0), x, a_x)
            load_x(sa, Step(0, 1), x, a_x)
            for dst, src in ((wqkv0_s[:, :, :], wqkv0.rearrange("(c p) n -> p c n", p=P)),
                             (rw0_s[:, :, :], rw0.rearrange("(c p) n -> p c n", p=P)),
                             (bq0_s[:, :], bq0[:, :]),
                             (bkv0_s[:, :], bkv0.partition_broadcast(P)),
                             (bo0_s[:, :], bo0.partition_broadcast(P)),
                             (cosk_s[:, :], cos_k[:, :]),
                             (sink_s[:, :], sin_k[:, :])):
                sp.dma_start(dst, src).then_inc(consts, 16)

            def step_a(s, more=True):
                sp.wait_ge(sa.xn, s.t + 1)
                sp.dma_start(rows(xg0_d, s.t), a_xn[:, s.par, :]).then_inc(sa.xn_out[s.par], 16)
                sp.wait_ge(sa.xb, s.t + 1)
                sp.dma_start(rows(xb_d, s.t), a_xb[:, s.par, :]).then_inc(sa.xb_out[s.par], 16)
                if more:
                    load_x(sa, Step(s.half + 1, s.par), x, a_x)

            with sp.Fori(0, E) as m:
                for par in range(2):
                    step_a(Step(m, par))
                sp.dma_start(r1[:, ds(m, 1), 0:DC * H].rearrange("p e (c n) -> p (e c) n", c=DC),
                             w1_0[ds(m, 1)].rearrange("e (c p) n -> p (e c) n", p=P)).then_inc(w0_in, 16)
                sp.dma_start(r1[:, ds(m, 1), DC * H:2 * DC * H].rearrange("p e (c n) -> p (e c) n", c=HC),
                             w2_0[ds(m, 1)].rearrange("e (c p) n -> p (e c) n", p=P)).then_inc(w0_in, 16)
            with sp.Fori(E, NT // 2 - 1) as m:
                for par in range(2):
                    step_a(Step(m, par))
            for par in range(2):
                step_a(Step(NT // 2 - 1, par), more=False)

            def group(s):
                return s.par * L + s.half * GB * P

            def load_q(s):
                sp.dma_start(b_q[:, s.par, :, :], qrot_all[:, :, ds(group(s), GB * P)]).then_inc(ql_in[s.par], 16)

            def load_xb(s):
                sp.dma_start(b_xb[:, s.par, :, :], xb_d[ds(group(s), GB * P), :].rearrange("(j p) n -> p j n", p=P))\
                  .then_inc(xb_in[s.par], 16)

            sp.wait_ge(qrot, NT)
            for par in range(2):
                load_q(Step(0, par))
            for par in range(2):
                sp.wait_ge(sa.xb_out[par], 16 * (NT // 2))
            for par in range(2):
                load_xb(Step(0, par))
            for par in range(2):
                sp.wait_ge(sa.xn_out[par], 16 * (NT // 2))
            sp.wait_ge(gates_r, 1)
            sp.dma_start(xg0_d.rearrange("(t p) n -> p t n", p=P)[:, :, D:ROW], gates).then_inc(gates_out, 16)

            def step_b(s, more=True):
                sp.wait_ge(ao_sb, GB * (s.t + 1))
                sp.dma_start(x1_d[ds(group(s), GB * P), :].rearrange("(j p) n -> p j n", p=P), b_x1[:, s.par, :, :])\
                  .then_inc(x1_out[s.par], 16)
                if more:
                    load_q(Step(s.half + 1, s.par))
                    load_xb(Step(s.half + 1, s.par))

            with sp.Fori(0, SB // 2 - 1) as m:
                for par in range(2):
                    step_b(Step(m, par))
            for par in range(2):
                step_b(Step(SB // 2 - 1, par), more=False)
            for par in range(2):
                sp.wait_ge(x1_out[par], 16 * (SB // 2))
            sp.wait_ge(gates_out, 16)
            end_stage(sp, 1)

            end_stage(sp, 2)

            for par in range(2):
                load_x(sd, Step(0, par), x1_d, d_x)

            def step_d(s, more=True):
                sp.wait_ge(sd.xn, s.t + 1)
                sp.dma_start(rows(xg1_d, s.t), d_xn[:, s.par, :]).then_inc(sd.xn_out[s.par], 16)
                sp.wait_ge(sd.xb, s.t + 1)
                sp.dma_start(rows(xb1_d, s.t), d_xb[:, s.par, :]).then_inc(sd.xb_out[s.par], 16)
                if more:
                    load_x(sd, Step(s.half + 1, s.par), x1_d, d_x)
                if s.at_least(1):
                    b = s.back(1)
                    sp.wait_ge(sc_sb, b.t + 1)
                    sp.dma_start(rows(xg1_d, b.t, D, ROW), d_sc[:, b.par, :]).then_inc(sc_out[b.par], 16)

            def load_qk(s):
                if s.at_least(2):
                    sp.wait_ge(s_ps, s.t - 1)
                sp.dma_start(e_qk[:, s.par, :, :], qk_all[:, :, ds(s.t * P, P)]).then_inc(qkl[s.par], 16)

            def load_v(s):
                if s.at_least(2):
                    sp.wait_ge(o_ps, s.t - 1)
                for b in range(2):
                    for hp in range(2):
                        sp.dma_start(e_v[BLK * hp:BLK * hp + BLK, s.par, b, hp, :, 0:DK],
                                     r2[BLK * b:BLK * b + BLK, ds(s.t * D + P * hp, P)]
                                     .rearrange("p (g d) -> p g d", d=DK)).then_inc(vl[s.par], 16)

            step_d(Step(0, 0))
            step_d(Step(0, 1))
            with sp.Fori(1, NT // 2 - 1) as m:
                for par in range(2):
                    step_d(Step(m, par))
            sp.wait_ge(qk1_sb, 4 * 2)
            sp.wait_ge(v1_sb, 2)
            sp.wait_ge(vz, 1)
            for par in range(2):
                load_qk(Step(0, par))
                load_v(Step(0, par))
            for par in range(2):
                step_d(Step(NT // 2 - 1, par), more=False)
            sp.wait_ge(sc_sb, NT)
            sp.dma_start(rows(xg1_d, NT - 1, D, ROW), d_sc[:, 1, :]).then_inc(sc_out[1], 16)
            for par in range(2):
                sp.wait_ge(sd.xn_out[par], 16 * (NT // 2))
                sp.wait_ge(sd.xb_out[par], 16 * (NT // 2))
                sp.wait_ge(sc_out[par], 16 * (NT // 2))
            end_stage(sp, 3)

            def load_w13(s):
                sp.dma_start(f_w[s.par][:, 0:W13].rearrange("p (c n) -> p c n", c=DC),
                             w13_1[ds(s.t, 1)].rearrange("o (c p) n -> p (o c) n", p=P)).then_inc(fw13_in[s.par], 16)

            def load_w2(s):
                sp.dma_start(f_w[s.par][:, W13:W13 + W2].rearrange("p (c n) -> p c n", c=HC),
                             w2_1[ds(s.t, 1)].rearrange("o (c p) n -> p (o c) n", p=P)).then_inc(fw2_in[s.par], 16)

            def load_xb1(s):
                sp.dma_start(e_xb[:, s.par, :], rows(xb1_d, s.t)).then_inc(xbl[s.par], 16)

            def store_e(s, more=True):
                sp.wait_ge(fin_r, s.t + 1)
                sp.dma_start(rows(out, s.t), e_y[:, s.par, :]).then_inc(fin_out[s.par], 16)
                if more:
                    load_xb1(Step(s.half + 1, s.par))

            for par in range(2):
                load_xb1(Step(0, par))
            for t in (2, 3):
                load_qk(Step(1, t - 2))
                if t == 3:
                    load_v(Step(1, 0))
            with sp.Fori(2, NT // 2) as m:
                for par in range(2):
                    s = Step(m, par)
                    load_qk(s)
                    load_v(s.back(1))
                    store_e(s.back(4))
            load_v(Step(NT // 2 - 1, 1))
            for t in range(NT - 4, NT):
                store_e(Step(t // 2, t % 2), more=t < NT - 2)
                if t == NT - 3:
                    sp.wait_ge(slots1, 3)
                    load_w13(Step(0, 0))
            load_w2(Step(0, 0))
            load_w13(Step(0, 1))
            load_w2(Step(0, 1))
            for par in range(2):
                sp.wait_ge(fin_out[par], 16 * (NT // 2))
            end_stage(sp, 4)

            with sp.Fori(1, E // 2) as m:
                for par in range(2):
                    s = Step(m, par)
                    sp.wait_ge(wlo_r, DC * (s.t - 1))
                    load_w13(s)
                    sp.wait_ge(w2lo_r, E + s.t - 1)
                    load_w2(s)
            sp.wait_ge(fy_out, 16 * TE * E)

        @block.tensor
        def _(pe):
            def transpose_x(z, s, xn, n=NT):
                pe.wait_ge(z.xn, s.t + 1)
                if s.at_least(1):
                    pe.wait_ge(z.xT, s.t)
                for c in range(DC):
                    last = pe.transpose(bank[0][:, c * P:(c + 1) * P], xn[:, s.par, c * P:(c + 1) * P], ident[:, :])
                last.then_inc(z.xT_ps, 1)

            pe.wait_ge(made, 1)

            def step_a(s, first=False):
                if in_range(s.back(1), NT) and s.at_least(1):
                    b = s.back(1)
                    xT = a_xT[:, b.par, :, :]
                    pe.wait_ge(sa.xT, b.t + 1)
                    if b.at_least(2):
                        pe.wait_ge(kv_sb, b.t - 1)
                    if not b.at_least(1):
                        pe.wait_ge(consts, 16 * 7)
                    for c in range(DC):
                        last = pe.matmul(bank[1 + b.par][:, :], xT[:, c, :], wqkv0_s[:, c, D:3 * D],
                                         start=c == 0, stop=c == DC - 1)
                    last.then_inc(kv_ps, 1)
                if in_range(s, NT):
                    transpose_x(sa, s, a_xn)
                if in_range(s.back(1), NT) and s.at_least(1):
                    if b.at_least(2):
                        pe.wait_ge(q_sb, 2 * (b.t - 1))
                    for r in range(DC):
                        for c in range(DC):
                            last = pe.matmul(bank[5 + b.par][:, r * P:(r + 1) * P], wqkv0_s[:, c, r * P:(r + 1) * P],
                                             xT[:, c, :], start=c == 0, stop=c == DC - 1)
                    last.then_inc(q_ps, 1)
                    if b.at_least(1):
                        pe.wait_ge(lg_sb, b.t)
                    for c in range(DC):
                        last = pe.matmul(bank[7][:, 0:E], xT[:, c, :], rw0_s[:, c, :], start=c == 0, stop=c == DC - 1)
                    last.then_inc(lg_ps, 1)
                if s.at_least(3) and in_range(s.back(3), NT):
                    b = s.back(3)
                    start = isinstance(b.half, int) and b.t % BT == 0
                    stop = isinstance(b.half, int) and b.t % BT == BT - 1
                    pe.wait_ge(krot, b.t + 1)
                    if start and b.t:
                        pe.wait_ge(kvm_r, 1)
                    kr = a_kr[:, b.par, :].rearrange("p (r h) -> p r h", r=2)
                    for g in range(2):
                        last = pe.matmul(bank[3 + g][:, 0:P], a_kv[:, b.par, D + g * P:D + (g + 1) * P],
                                         kr[:, :, g * 64:(g + 1) * 64], start=start, stop=stop)
                    last.then_inc(st_ps, 1)

            for t in range(4):
                step_a(Step(t // 2, t % 2))
            with pe.Fori(2, 9) as m:
                for par in range(2):
                    step_a(Step(m, par))
            for t in (18, 19):
                step_a(Step(t // 2, t % 2))
            with pe.Fori(10, NT // 2) as m:
                for par in range(2):
                    step_a(Step(m, par))
            for t in (32, 33, 34):
                step_a(Step(t // 2, t % 2))

            pe.wait_ge(consts_b, 16 * 7)
            pe.wait_ge(mask_r, 1)
            pe.wait_ge(kv_sb, NT)
            pe.matmul(bank[1][:, 0:E * NT], upper[:, :], small_mask, start=True, stop=True)
            pe.matmul(bank[1][:, E * NT:2 * E * NT], ones[:, :], small_mask, start=True, stop=True).then_inc(rank_ps, 1)
            pe.wait_ge(q_sb, 2 * NT)

            for b in range(NB):
                pe.wait_ge(kvm_r, b + 1)
                for r in range(2):
                    for g in range(2):
                        last = pe.matmul(bank[5 + b][64 * g:64 * g + 64, r * D:(r + 1) * D],
                                         a_kvm[b][g][:, r * 64:(r + 1) * 64], wo0_s[:, g, :], start=True, stop=True)
                last.then_inc(m_ps, 1)

            def invert(s, start=False, stop=False):
                pe.wait_ge(hot_r, s.t + 1)
                for n in range(GN):
                    last = pe.matmul(bank[0][:, 0:ST0], hot_lo[:, s.par, n, :], hot_hi[:, s.par, n, :],
                                     start=start and n == 0, stop=stop and n == GN - 1)
                last.then_inc(inv_ps, 1)

            def step_b(s):
                pe.wait_ge(ql_in[s.par], 16 * (s.half + 1))
                for j in range(GB):
                    if s.at_least(1):
                        pe.wait_ge(ao_sb, GB * (s.t - 1) + j + 1)
                    for r in range(2):
                        last = pe.matmul(bank[attn_bank[j]][:, 0:D], b_q[:, s.par, r, j * P:(j + 1) * P],
                                         m_all[s.par][:, r, :], start=r == 0, stop=r == 1)
                    last.then_inc(ao_ps, 1)
                if s.at_least(1):
                    b = s.back(1)
                    invert(b, start=isinstance(b.half, int) and b.t == 0)

            pe.wait_ge(m_sb, NB)
            step_b(Step(0, 0))
            step_b(Step(0, 1))
            with pe.Fori(1, SB // 2) as m:
                for par in range(2):
                    step_b(Step(m, par))
            invert(Step(SB // 2 - 1, 1), stop=True)
            pe.wait_ge(w0_in, 16 * 2 * E)
            end_stage(pe, 1)

            def step_c(s):
                if in_range(s, ST0):
                    pe.wait_ge(xg_in[s.par], 16 * (s.half + 1))
                    if s.at_least(2):
                        pe.wait_ge(cT_sb, s.t - 1)
                    for c in range(DC):
                        last = pe.transpose(bank[(0, 3)[s.par]][:, c * P:(c + 1) * P], c_xg[:, s.par, c * P:(c + 1) * P],
                                            ident[:, :])
                    last.then_inc(cT_ps, 1)
                if s.at_least(1) and in_range(s.back(1), ST0):
                    b = s.back(1)
                    pe.wait_ge(w1_r, b.t + 1)
                    pe.wait_ge(cT_sb, b.t + 1)
                    if b.at_least(2):
                        pe.wait_ge(relu_sb, b.t - 1)
                    for k in range(HC):
                        for c in range(DC):
                            last = pe.matmul(bank[1 + b.par][:, k * P:(k + 1) * P], c_w1[:, b.par, c, k * P:(k + 1) * P],
                                             c_xT[:, b.par, c, :], start=c == 0, stop=c == DC - 1)
                    last.then_inc(hT_ps, 1)
                if s.at_least(2) and in_range(s.back(2), ST0):
                    b = s.back(2)
                    e2 = pe.value_load(tile_e[0:1, ds(b.t, 1)], min_val=0, max_val=E - 1)
                    pe.wait_ge(hi_r, b.t + 1)
                    pe.wait_ge(lo_c, b.t + 1)
                    if not b.at_least(1):
                        pe.wait_ge(w2lo_r, E)
                    if b.at_least(2):
                        pe.wait_ge(y_sb, b.t - 1)
                    n = 0
                    for h, w, o in ((c_hi, w2_hi, 0), (c_lo, w2_hi, 0), (c_hi, r1s, DC * H)):
                        for c in range(HC):
                            last = pe.matmul(bank[5 + b.par][:, 0:D], h[:, b.par, c, :],
                                             w[:, ds(e2, 1), o + c * D:o + (c + 1) * D],
                                             start=n == 0, stop=n == 3 * HC - 1)
                            n += 1
                    last.then_inc(y_ps, 1)

            for t in range(4):
                step_c(Step(t // 2, t % 2))
            with pe.Fori(2, ST0 // 2) as m:
                for par in range(2):
                    step_c(Step(m, par))
            for t in (ST0, ST0 + 1):
                step_c(Step(t // 2, t % 2))
            end_stage(pe, 2)

            def step_d(s):
                if s.at_least(1) and in_range(s.back(1), NT):
                    b = s.back(1)
                    xT = d_xT[:, b.par, :, :]
                    pe.wait_ge(sd.xT, b.t + 1)
                    if b.at_least(2):
                        pe.wait_ge(qk1_sb, 4 * (b.t - 1))
                    for j in range(2 * DC):
                        for c in range(DC):
                            last = pe.matmul(bank[1 + b.par][:, j * P:(j + 1) * P], wqkv1_s[:, c, j * P:(j + 1) * P],
                                             xT[:, c, :], start=c == 0, stop=c == DC - 1)
                    last.then_inc(qk1_ps, 1)
                if in_range(s, NT):
                    transpose_x(sd, s, d_xn)
                if s.at_least(1) and in_range(s.back(1), NT):
                    if b.at_least(2):
                        pe.wait_ge(v1_sb, b.t - 1)
                    for c in range(DC):
                        last = pe.matmul(bank[3 + b.par][:, 0:D], xT[:, c, :], wqkv1_s[:, c, 2 * D:3 * D],
                                         start=c == 0, stop=c == DC - 1)
                    last.then_inc(v1_ps, 1)
                    if b.at_least(1):
                        pe.wait_ge(sc_sb, b.t)
                    for c in range(DC):
                        last = pe.matmul(bank[5][:, 0:E], xT[:, c, :], wg1_s[:, c, :], start=c == 0, stop=c == DC - 1)
                    last.then_inc(sc_ps, 1)

            for t in range(4):
                step_d(Step(t // 2, t % 2))
            with pe.Fori(2, NT // 2) as m:
                for par in range(2):
                    step_d(Step(m, par))
            step_d(Step(NT // 2, 0))
            end_stage(pe, 3)


            def count(s, r, bk):
                pe.wait_ge(part_r, 2 * s.t + r + 1)
                pe.matmul(bank[bk][:, D:D + E], ones[:, :], e_part[:, r, :], start=True, stop=True).then_inc(cnt_ps, 1)

            def step_e(s, search=False, copied=None):
                if in_range(s, NT):
                    pe.wait_ge(qkl[s.par], 16 * (s.half + 1))
                    if s.at_least(1):
                        pe.wait_ge(sub_r, s.t)
                    for j in range(2):
                        for b in range(2):
                            for g in range(4):
                                last = pe.matmul(banks47[BLK * b:BLK * b + BLK, g, BLK * j:BLK * j + BLK],
                                                 e_qk[DK * g:DK * g + DK, s.par, j, BLK * b:BLK * b + BLK],
                                                 e_qk[DK * g:DK * g + DK, s.par, DC + j, BLK * b:BLK * b + BLK],
                                                 start=True, stop=True, tile_position=(DK * g, BLK * b))
                    last.then_inc(s_ps, 1)
                if copied is not None:
                    pe.wait_ge(copied, 3 if copied is rank1 else 2)
                if s.at_least(3) and in_range(s.back(3), NT):
                    b = s.back(3)
                    pe.wait_ge(oT_sb, b.t + 1)
                    if b.at_least(1):
                        pe.wait_ge(y1_sb, b.t)
                    if search or (isinstance(s.half, int) and s.t == SR):
                        pe.wait_ge(cnt_used, 2 * s.t - 1)
                    for c in range(DC):
                        last = pe.matmul(bank[3][:, 0:D], e_oT[:, b.par, c, :], wo1_s[:, c, :],
                                         start=c == 0, stop=c == DC - 1)
                    last.then_inc(y1_ps, 1)
                if s.at_least(1) and in_range(s.back(1), NT):
                    b = s.back(1)
                    pe.wait_ge(p_r, b.t + 1)
                    if b.at_least(1):
                        pe.wait_ge(pT_sb, b.t)
                    for g in range(NP):
                        last = pe.transpose(bank[0][:, g * P:(g + 1) * P],
                                            e_p[:, b.par, 2 * g:2 * g + 2, :], ident[:, :])
                    last.then_inc(pT_ps, 1)
                if search:
                    if s.at_least(3):
                        pe.wait_ge(y1_sb, s.t - 2)
                    count(s, 0, 3)
                if s.at_least(2) and in_range(s.back(2), NT):
                    b = s.back(2)
                    pe.wait_ge(o_sb, b.t + 1)
                    if b.at_least(1):
                        pe.wait_ge(oT_sb, b.t)
                    if search or (isinstance(s.half, int) and s.t == SR):
                        pe.wait_ge(cnt_used, 2 * s.t)
                    for c in range(DC):
                        last = pe.transpose(bank[2][:, c * P:(c + 1) * P], e_o[:, b.par, c * P:(c + 1) * P], ident[:, :])
                    last.then_inc(oT_ps, 1)
                if s.at_least(1) and in_range(s.back(1), NT):
                    b = s.back(1)
                    pe.wait_ge(vl[b.par], 64 * (b.half + 1))
                    pe.wait_ge(pT_sb, b.t + 1)
                    if b.at_least(1):
                        pe.wait_ge(o_sb, b.t)
                    for k in range(2):
                        for g in range(NP):
                            rows_k = slice(BLK * k, BLK * k + BLK)
                            last = pe.matmul(bank[1][rows_k, 2 * VC * g:2 * VC * (g + 1)], e_pT[:, g, rows_k],
                                             e_v[:, b.par, k, :, g, :], start=True, stop=True)
                    last.then_inc(o_ps, 1)
                if search:
                    if s.at_least(2):
                        pe.wait_ge(oT_sb, s.t - 1)
                    count(s, 1, 2)

            def free_banks(t):
                pe.wait_ge(o_sb, t)
                pe.wait_ge(oT_sb, t - 1)
                pe.wait_ge(y1_sb, t - 2)

            for t in range(4):
                step_e(Step(t // 2, t % 2), search=True)
            with pe.Fori(2, SR // 2) as m:
                for par in range(2):
                    step_e(Step(m, par), search=True)
            step_e(Step(SR // 2, 0))
            pe.wait_ge(rank1, 1)
            free_banks(SR)
            for k in range(2):
                half = slice(k * E * NT, (k + 1) * E * NT)
                pe.matmul(bank[3 - k][:, D:2 * D], upper[:, :], s_both[:, half], start=True, stop=False)
                pe.matmul(bank[3 - k][:, D:2 * D], ones[:, :], s_before[:, half], start=False, stop=True)
            pe.matmul(bank[1][:, 2 * D - E:2 * D], onesf, s_tot, start=True, stop=True).then_inc(rank1, 1)
            step_e(Step(SR // 2, 1), copied=rank1)
            step_e(Step(SR // 2 + 1, 0))
            step_e(Step(SR // 2 + 1, 1))
            with pe.Fori(SH // 2, (SH + NT // HT) // 2) as m:
                for par in range(2):
                    step_e(Step(m, par))
            t = SH + NT // HT
            step_e(Step(t // 2, 0))
            pe.wait_ge(zsum, 1)
            pe.wait_ge(hot1_r, NT // HT)
            free_banks(t)
            pe.matmul(bank[1][:, 2 * D - E:2 * D], onesf, s_zp, start=True, stop=True).then_inc(zsum, 1)
            for q in range(2):
                for c in range(NT):
                    last = pe.matmul(bank[3][:, D + q * P:D + (q + 1) * P], hot1_hi[:, c, q * P:(q + 1) * P],
                                     hot1_lo[:, c, :, q * 4:(q + 1) * 4, :],
                                     start=c == 0, stop=c == NT - 1)
            last.then_inc(slots1, 1)
            step_e(Step(t // 2, 1), copied=slots1)
            for t in range(SH + NT // HT + 2, NT + 3):
                step_e(Step(t // 2, t % 2))
            end_stage(pe, 4)

            def transpose_f(s):
                pe.wait_ge(fx_in[s.par], 16 * TE * (s.half + 1))
                if s.at_least(1):
                    pe.wait_ge(xlo_r, DC * s.t)
                for c in range(DC):
                    for i in range(TE):
                        last = pe.transpose(bank[4 + c][:, i * P:(i + 1) * P],
                                            f_xg[:, s.par, i, c * P:(c + 1) * P], ident[:, :])
                last.then_inc(fT_ps, 1)

            def hidden(s):
                pe.wait_ge(wlo_r, DC * (s.t + 1))
                pe.wait_ge(xlo_r, DC * (s.t + 1))
                whi, wlo = f_whi[s.par], f_wlo[s.par]
                for hb in range(HC):
                    if hb >= 2 or s.at_least(1):
                        pe.wait_ge(h1_r, HC * s.t + hb - 1)
                    for k in range(2):
                        n = 0
                        for c in range(DC):
                            o = c * 2 * H + k * H + hb * P
                            for w, x in ((whi, f_xhi), (whi, f_xlo), (wlo, f_xhi)):
                                last = pe.matmul(bank[2 * (hb % 2) + k][:, :], w[:, o:o + P],
                                                 x[:, s.par, c, :], start=n == 0, stop=n == 3 * DC - 1)
                                n += 1
                    last.then_inc(h13_ps, 1)

            def result(s):
                pe.wait_ge(w2lo_r, E + s.t + 1)
                pe.wait_ge(hlo_r, HC * (s.t + 1))
                for i in range(TE):
                    if i >= 2 or s.at_least(1):
                        pe.wait_ge(fy_sb, TE * s.t + i - 1)
                    n = 0
                    for c in range(HC):
                        o = W13 + c * D
                        for h, w in ((f_hhi, f_whi), (f_hhi, f_wlo), (f_hlo, f_whi)):
                            last = pe.matmul(bank[6 + i % 2][:, 0:D], h[:, s.par, c, i * P:(i + 1) * P],
                                             w[s.par][:, o:o + D], start=n == 0, stop=n == 3 * HC - 1)
                            n += 1
                    last.then_inc(fy_ps, 1)

            def step_f(s, more=True):
                hidden(s)
                if more:
                    transpose_f(s.back(-1))
                if s.at_least(1):
                    result(s.back(1))

            transpose_f(Step(0, 0))
            step_f(Step(0, 0))
            step_f(Step(0, 1))
            with pe.Fori(1, E // 2 - 1) as m:
                for par in range(2):
                    step_f(Step(m, par))
            step_f(Step(E // 2 - 1, 0))
            step_f(Step(E // 2 - 1, 1), more=False)
            result(Step(E // 2 - 1, 1))

        @block.scalar
        def _(act):
            def sqrt_and_copy(z, s, mv, sdv, xT):
                act.wait_ge(z.moments, s.t + 1)
                act.activation(sdv[:, s.par, :], mv[:, s.par, 1:2], ACT.Sqrt, bias=eps_c[:, :]).then_inc(z.std, 1)

            def copy_xT(z, s, xT, users):
                act.wait_ge(z.xT_ps, s.t + 1)
                for u, n in users:
                    if s.at_least(2):
                        act.wait_ge(u, n * (s.t - 1))
                act.activation(xT[:, s.par, :, :], bank[0][:, 0:D], ACT.Copy).then_inc(z.xT, 1)

            act.wait_ge(made, 1)

            def step_a(s):
                if in_range(s, NT):
                    sqrt_and_copy(sa, s, a_mv, a_sd, a_xT)
                    copy_xT(sa, s, a_xT, [(lg_ps, 1)])
                if s.at_least(1) and in_range(s.back(1), NT):
                    b = s.back(1)
                    act.wait_ge(q_ps, b.t + 1)
                    if b.at_least(2):
                        act.wait_ge(qprod, b.t - 1)
                    for r in range(DC):
                        act.activation(a_q[:, b.par, r, :], bank[5 + b.par][:, r * P:(r + 1) * P], ACT.Identity,
                                       bias=bq0_s[:, r:r + 1]).then_inc(q_sb, 1)
                    act.wait_ge(lg_ps, b.t + 1)
                    if b.at_least(2):
                        act.wait_ge(top_m, b.t - 1)
                    act.activation(a_lg[:, b.par, :], bank[7][:, 0:E], ACT.Copy).then_inc(lg_sb, 1)

            step_a(Step(0, 0))
            act.wait_ge(consts, 16 * 7)
            for half, loaded in ((slice(0, L // 2), tables), (slice(L // 2, L), tables_b)):
                act.dma_start(cosq_s[:, half], cos_q[:, half]).then_inc(loaded, 16)
                act.dma_start(sinq_s[:, :, half], sin_q.rearrange("p (r n) -> p r n", r=2)[:, :, half]).then_inc(loaded, 16)
            for dst, src in ((wo0_s[:, :, :], wo0.rearrange("(c p) n -> p c n", p=P)),
                             (wqkv1_s[:, :, :], wqkv1.rearrange("(c p) n -> p c n", p=P)),
                             (wo1_s[:, :, :], wo1.rearrange("(c p) n -> p c n", p=P)),
                             (wg1_s[:, :, :], wg1.rearrange("(c p) n -> p c n", p=P)),
                             (bqk1_s[:, :], bqk1[:, :]),
                             (bv1_s[:, :], bv1.partition_broadcast(P)),
                             (bo1_s[:, :], bo1.partition_broadcast(P))):
                act.dma_start(dst, src).then_inc(consts_b, 16)
            for t in range(1, 4):
                step_a(Step(t // 2, t % 2))
            with act.Fori(2, NT // 2) as m:
                for par in range(2):
                    step_a(Step(m, par))
            step_a(Step(NT // 2, 0))

            act.wait_ge(top_de, 1)
            act.activation(top_e, top_d, ACT.Exp).then_inc(top_de, 1)
            for b in range(NB):
                act.wait_ge(m_ps, b + 1)
                act.activation(m_all[b], bank[5 + b][:, :], ACT.Copy).then_inc(m_sb, 1)
            act.wait_ge(w0_in, 16 * 2 * E)
            for par in range(2):
                act.wait_ge(ql_in[par], 16 * (SB // 2))
            for e in range(E):
                act.activation(w2_hi[:, e, :], r1[:, e, DC * H:2 * DC * H], ACT.Copy).then_inc(w2hi_r, 1)
            end_stage(act, 1)

            def step_c(s):
                if in_range(s, ST0):
                    act.wait_ge(cT_ps, s.t + 1)
                    if s.at_least(2):
                        act.wait_ge(hT_ps, s.t - 1)
                    act.activation(c_xT[:, s.par, :, :], bank[(0, 3)[s.par]][:, 0:D], ACT.Copy).then_inc(cT_sb, 1)
                if s.at_least(1) and in_range(s.back(1), ST0):
                    b = s.back(1)
                    act.wait_ge(hT_ps, b.t + 1)
                    if b.at_least(2):
                        act.wait_ge(sq_r, b.t - 1)
                    act.activation(c_r[:, b.par, :], bank[1 + b.par][:, :], ACT.Relu).then_inc(relu_sb, 1)
                    act.wait_ge(sq_r, b.t + 1)
                    if b.at_least(2):
                        act.wait_ge(y_ps, b.t - 1)
                    act.activation(c_hi[:, b.par, :, :].rearrange("p c n -> p (c n)"), c_sq[:],
                                   ACT.Copy).then_inc(hi_r, 1)

            for t in range(4):
                step_c(Step(t // 2, t % 2))
            with act.Fori(2, ST0 // 2) as m:
                for par in range(2):
                    step_c(Step(m, par))
            step_c(Step(ST0 // 2, 0))
            end_stage(act, 2)

            def step_d(s):
                if in_range(s, NT):
                    sqrt_and_copy(sd, s, d_mv, d_sd, d_xT)
                    copy_xT(sd, s, d_xT, [(sc_ps, 1)])
                if s.at_least(1) and in_range(s.back(1), NT):
                    b = s.back(1)
                    act.wait_ge(qk1_ps, b.t + 1)
                    for j in range(2 * DC):
                        act.activation(qk_all[:, j, ds(b.t * P, P)], bank[1 + b.par][:, j * P:(j + 1) * P],
                                       ACT.Identity, bias=bqk1_s[:, j:j + 1]).then_inc(qk1_sb, 1)
                    act.wait_ge(sc_ps, b.t + 1)
                    if b.at_least(2):
                        act.wait_ge(sc_kept, b.t - 1)
                        act.wait_ge(sc_out[b.par], 16 * b.half)
                    act.activation(d_sc[:, b.par, :], bank[5][:, 0:E], ACT.Copy).then_inc(sc_sb, 1)

            for t in range(4):
                step_d(Step(t // 2, t % 2))
            with act.Fori(2, NT // 2) as m:
                for par in range(2):
                    step_d(Step(m, par))
            step_d(Step(NT // 2, 0))
            end_stage(act, 3)

            def step_e(s):
                if s.at_least(3) and in_range(s.back(3), NT):
                    b = s.back(3)
                    act.wait_ge(y1_ps, b.t + 1)
                    if b.at_least(2):
                        act.wait_ge(fin_out[b.par], 16 * b.half)
                    act.activation(e_y[:, b.par, :], bank[3][:, 0:D], ACT.Copy).then_inc(y1_sb, 1)
                if s.at_least(1) and in_range(s.back(1), NT):
                    b = s.back(1)
                    act.wait_ge(pT_ps, b.t + 1)
                    if b.at_least(1):
                        act.wait_ge(o_ps, b.t)
                    act.activation(e_pT[:, :, :], bank[0][:, :], ACT.Copy).then_inc(pT_sb, 1)
                if s.at_least(2) and in_range(s.back(2), NT):
                    b = s.back(2)
                    act.wait_ge(oT_ps, b.t + 1)
                    if b.at_least(2):
                        act.wait_ge(y1_ps, b.t - 1)
                    act.activation(e_oT[:, b.par, :, :], bank[2][:, 0:D], ACT.Copy).then_inc(oT_sb, 1)
                if in_range(s, NT):
                    act.wait_ge(sub_r, s.t + 1)
                    if s.at_least(2):
                        act.wait_ge(pT_ps, s.t - 1)
                    act.activation(e_p[:, s.par, :, :], e_s[:, :, :], ACT.Exp, scale=DK ** -0.5).then_inc(p_r, 1)

            act.activation(table_warm[:, :], eps_c[:, :], ACT.Exp)
            for t in range(6):
                step_e(Step(t // 2, t % 2))
            with act.Fori(3, SR // 2) as m:
                for par in range(2):
                    step_e(Step(m, par))
            act.wait_ge(gmax, 3)
            for e in range(E):
                last = act.activation(s_exp[:, e, :], sc_all[:, e, :], ACT.Exp, bias=nscmax[:, e:e + 1])
            last.then_inc(ex_r, 1)
            with act.Fori(SR // 2, NT // 2) as m:
                for par in range(2):
                    step_e(Step(m, par))
            for t in (NT, NT + 1, NT + 2):
                step_e(Step(t // 2, t % 2))
            end_stage(act, 4)

            def high_x(s):
                act.wait_ge(fT_ps, s.t + 1)
                if s.at_least(2):
                    act.wait_ge(h13_ps, HC * (s.t - 1))
                for c in range(DC):
                    act.activation(f_xhi[:, s.par, c, :], bank[4 + c][:, :], ACT.Copy).then_inc(xhi_r, 1)

            def high_w13(s, c):
                if c == 0:
                    act.wait_ge(fw13_in[s.par], 16 * (s.half + 1))
                    if s.at_least(2):
                        act.wait_ge(h13_ps, HC * (s.t - 1))
                act.activation(f_whi[s.par][:, c * 2 * H:(c + 1) * 2 * H],
                               f_w[s.par][:, c * 2 * H:(c + 1) * 2 * H], ACT.Copy).then_inc(whi_r, 1)

            def high_w2(s):
                act.wait_ge(fw2_in[s.par], 16 * (s.half + 1))
                if s.at_least(2):
                    act.wait_ge(fy_ps, TE * (s.t - 1))
                act.activation(f_whi[s.par][:, W13:W13 + W2], f_w[s.par][:, W13:W13 + W2], ACT.Copy)\
                   .then_inc(w2hi_r, 1)

            def step_f(s, e, more=True):
                for hb in range(HC):
                    act.wait_ge(h13_ps, HC * s.t + hb + 1)
                    if hb >= 2 or s.at_least(1):
                        act.wait_ge(h1_r, HC * s.t + hb - 1)
                    act.activation(f_g[:, hb % 2, :], bank[2 * (hb % 2)][:, :], ACT.Silu).then_inc(g_r, 1)
                    if hb < DC and more:
                        high_w13(s.back(-1), hb)
                    elif hb == DC:
                        high_w2(s)
                    act.wait_ge(h1_r, HC * s.t + hb + 1)
                    if hb == 0 and s.at_least(2):
                        act.wait_ge(fy_ps, TE * (s.t - 1))
                    act.activation(f_hhi[:, s.par, hb, :], f_h[:, hb % 2, :], ACT.Copy).then_inc(hhi_r, 1)
                if more:
                    high_x(s.back(-1))
                act.wait_ge(fx_in[s.par], 16 * TE * (s.half + 1))
                if s.at_least(2):
                    act.wait_ge(fwg_r, s.t - 1)
                act.activation(f_we[:, s.par, :].unsqueeze(2), f_xg[:, s.par, :, ds(D + e, 1)], ACT.Exp,
                               bias=nscmax[:, ds(e, 1)]).then_inc(fwe_r, 1)
                act.activation(table_warm[:, :], eps_c[:, :], ACT.Silu)

            for c in range(DC):
                high_w13(Step(0, 0), c)
            high_x(Step(0, 0))
            act.activation(table_warm[:, :], eps_c[:, :], ACT.Silu)
            step_f(Step(0, 0), 0)
            step_f(Step(0, 1), 1)
            with act.Fori(1, E // 2 - 1) as m:
                for par in range(2):
                    step_f(Step(m, par), 2 * m + par)
            step_f(Step(E // 2 - 1, 0), E - 2)
            step_f(Step(E // 2 - 1, 1), E - 1, more=False)

        @block.vector
        def _(dve):
            chain = [0]

            def link(ins):
                chain[0] += 1
                ins.then_inc(seq, 1)
                dve.wait_ge(seq, chain[0])

            def stats(z, s, xt, st):
                dve.wait_ge(z.x_in[s.par], 16 * (s.half + 1))
                dve.bn_stats(st[:, s.par, :], xt[:, s.par, :]).then_inc(z.stats, 1)

            def moments(z, s, st, mv):
                dve.bn_aggr(mv[:, s.par, :], st[:, s.par, :]).then_inc(z.moments, 1)

            def normalise(z, s, xt, mv, sdv, rs, xn):
                dve.wait_ge(z.std, s.t + 1)
                dve.reciprocal(rs[:, s.par, :], sdv[:, s.par, :]).then_inc(z.rstd, 1)
                dve.wait_ge(z.rstd, s.t + 1)
                if s.at_least(2):
                    dve.wait_ge(z.xT_ps, s.t - 1)
                    dve.wait_ge(z.xn_out[s.par], 16 * s.half)
                dve.tensor_scalar(xn[:, s.par, :], xt[:, s.par, :], mv[:, s.par, 0:1], rs[:, s.par, :],
                                  ALU.subtract, ALU.mult).then_inc(z.xn, 1)

            dve.wait_ge(made, 1)

            def step_a(s, second=False):
                if in_range(s, NT):
                    normalise(sa, s, a_x, a_mv, a_sd, a_rs, a_xn)
                n = s.back(-1)
                if in_range(n, NT):
                    stats(sa, n, a_x, a_st)
                    if not s.at_least(2):
                        dve.wait_ge(sa.stats, n.t + 1)
                        moments(sa, n, a_st, a_mv)
                if s.at_least(2) and in_range(s.back(2), NT):
                    b = s.back(2)
                    tb = b.t - BT if second else b.t
                    if not b.at_least(1):
                        dve.wait_ge(consts, 16 * 7)
                    dve.wait_ge(kv_ps, b.t + 1)
                    dve.wait_ge(lg_sb, b.t + 1)
                    if b.at_least(2):
                        dve.wait_ge(st_ps, b.t - 1)
                    if in_range(n, NT):
                        dve.wait_ge(sa.stats, n.t + 1)
                    kv = a_kv[:, b.par, :]
                    dve.tensor_tensor(kv, bank[1 + b.par][:, :], bkv0_s[:, :], ALU.add).then_inc(kv_sb, 1)
                    if in_range(n, NT):
                        moments(sa, n, a_st, a_mv)
                    dve.max(a_top[:, b.par, :], a_lg[:, b.par, :]).then_inc(top_done, 1)
                    dve.wait_ge(kv_sb, b.t + 1)
                    dve.wait_ge(top_done, b.t + 1)
                    k4 = kv[:, 0:D].rearrange("p (r h j) -> p r h j", r=2, h=NH0)
                    t4 = [a_t[:, i, :].rearrange("p (r h j) -> p r h j", r=2, h=NH0) for i in range(2)]
                    cos = cosk_s[:, ds(tb * JR, JR)]
                    for r in range(2):
                        sin = sink_s[:, ds(tb * 2 * JR + r * JR, JR)]
                        dve.tensor_tensor(t4[0][:, r], k4[:, r], over_mid(cos, NH0), ALU.mult).then_inc(kprod, 1)
                        dve.tensor_tensor(t4[1][:, r], k4[:, 1 - r], over_mid(sin, NH0), ALU.mult).then_inc(kprod, 1)
                    dve.max_index(a_ti[:, b.par, :].bitcast(U32), a_top[:, b.par, :], a_lg[:, b.par, :]).then_inc(top_m, 1)
                    dve.wait_ge(kprod, 4 * (b.t + 1))
                    dve.tensor_tensor(a_kr[:, b.par, :], a_t[:, 0, :], a_t[:, 1, :], ALU.add).then_inc(krot, 1)
                    dve.tensor_copy(top_v[:, ds(b.t * TOPK, TOPK)], a_top[:, b.par, 0:TOPK]).then_inc(top_kept, 1)
                    dve.wait_ge(top_m, b.t + 1)
                    dve.tensor_copy(top_i[:, ds(b.t * TOPK, TOPK)], a_ti[:, b.par, 0:TOPK].bitcast(U32)).then_inc(top_kept, 1)

            stats(sa, Step(0, 0), a_x, a_st)
            dve.wait_ge(sa.stats, 1)
            moments(sa, Step(0, 0), a_st, a_mv)
            for t in range(4):
                step_a(Step(t // 2, t % 2))
            with dve.Fori(2, 9) as m:
                for par in range(2):
                    step_a(Step(m, par))
            step_a(Step(9, 0), second=True)
            for g in range(2):
                dve.wait_ge(st_ps, BT)
                last = dve.tensor_tensor(a_kvm[0][g], bank[3 + g][:, 0:P], headmask[:, :, :].rearrange("p a b -> p (a b)"),
                                         ALU.mult)
            last.then_inc(kvm_r, 1)
            step_a(Step(9, 1), second=True)
            with dve.Fori(10, NT // 2 - 1) as m:
                for par in range(2):
                    step_a(Step(m, par), second=True)
            for t in (30, 31, 32, 33):
                step_a(Step(t // 2, t % 2), second=True)
            for g in range(2):
                dve.wait_ge(st_ps, NT)
                last = dve.tensor_tensor(a_kvm[1][g], bank[3 + g][:, 0:P], headmask[:, :, :].rearrange("p a b -> p (a b)"),
                                         ALU.mult)
            last.then_inc(kvm_r, 1)

            dve.wait_ge(qrot, NT)
            dve.wait_ge(top_kept, TOPK * NT)
            tv, ti = (v[:, :].rearrange("p (t k) -> p t k", k=TOPK) for v in (top_v, top_i))
            for par in range(2):
                dve.wait_ge(sa.xn_out[par], 16 * (NT // 2))
            link(dve.tensor_tensor(top_d, tv[:, :, 1], tv[:, :, 0], ALU.subtract))
            dve.sem_inc(top_de, 1)
            for k in range(TOPK):
                link(dve.tensor_tensor(m_k[k], over_last(iota_e[:, :], NT), over_mid(ti[:, :, k], E), ALU.is_equal))
            dve.tensor_tensor(small_mask.rearrange("p (e t) -> p e t", e=E), m_k[0], m_k[1], ALU.add).then_inc(mask_r, 1)
            dve.wait_ge(top_de, 2)
            link(dve.tensor_scalar(top_w[:, 0, :], top_e, 1.0, None, ALU.add))
            link(dve.reciprocal(top_w[:, 0, :], top_w[:, 0, :]))
            link(dve.tensor_tensor(top_w[:, 1, :], top_w[:, 0, :], top_e, ALU.mult))
            for k in range(TOPK):
                link(dve.tensor_tensor(r_tmp[k], m_k[k], over_mid(top_w[:, k, :], E), ALU.mult))
            dve.tensor_tensor(gates.rearrange("p t e -> p e t"), r_tmp[0], r_tmp[1], ALU.add)\
               .then_inc(gates_r, 1)
            dve.wait_ge(rank_ps, 1)
            rank_v = bank[1][:, 0:E * NT].rearrange("p (e t) -> p e t", e=E)
            tot_v = bank[1][:, E * NT:2 * E * NT]
            link(dve.tensor_tensor_scan(incl.rearrange("p e t -> p (e t)"), not_first[:, :, :].rearrange("p e t -> p (e t)"),
                                        tot_v, 0.0, ALU.mult, ALU.add))
            link(dve.tensor_tensor(excl, incl, tot_v.rearrange("p (e t) -> p e t", e=E), ALU.subtract))
            link(dve.tensor_tensor(r_tmp[0], over_last(incl[:, :, NT - 1], NT), over_mid(iota_128m[:, :], E), ALU.is_gt))
            link(dve.tensor_reduce(n_tiles, r_tmp[0], AX, ALU.add))
            link(dve.tensor_tensor_scan(t_incl, one8[:, :], n_tiles, 0.0, ALU.mult, ALU.add))
            link(dve.tensor_tensor(t_excl, t_incl, n_tiles, ALU.subtract))
            dve.sem_inc(bounds_r, 1)
            link(dve.tensor_tensor(excl, excl, rank_v, ALU.add))
            link(dve.scalar_tensor_tensor(excl, over_last(t_excl, NT), float(P), excl, ALU.mult, ALU.add))
            for k in range(TOPK):
                link(dve.tensor_tensor(r_tmp[k], m_k[k], excl, ALU.mult))
                link(dve.tensor_reduce(slot_f[:, k, :], r_tmp[k].rearrange("p e t -> p t e"), AX, ALU.add))
            link(dve.tensor_copy(slot_i[:, 0, :], slot_f.rearrange("p k t -> p (k t)")))
            link(dve.tensor_scalar(slot_i[:, 1, :], slot_i[:, 0, :], 7, None, ALU.logical_shift_right))
            link(dve.tensor_scalar(slot_i[:, 0, :], slot_i[:, 0, :], P - 1, None, ALU.bitwise_and))
            link(dve.tensor_copy(slot_lh.rearrange("p a n -> p (a n)"), slot_i.rearrange("p a n -> p (a n)")))
            def step_b(s):
                for j in range(GB):
                    if j == 0 and s.at_least(2):
                        dve.wait_ge(inv_ps, s.t - 1)
                    for n in (2 * j, 2 * j + 1):
                        col = ds(GN * s.t + n, 1)
                        dve.tensor_scalar(hot_lo[:, s.par, n, :], iota_p[:, :], slot_lh[:, 0, col], None, ALU.is_equal)
                        last = dve.tensor_scalar(hot_hi[:, s.par, n, :], iota_t[:, :], slot_lh[:, 1, col],
                                                 number1[:, col], ALU.is_equal, ALU.mult)
                    if j == GB - 1:
                        last.then_inc(hot_r, 1)
                    if j == 0:
                        dve.wait_ge(xb_in[s.par], 16 * (s.half + 1))
                        if s.at_least(2):
                            dve.wait_ge(x1_out[s.par], 16 * s.half)
                    dve.wait_ge(ao_ps, GB * s.t + j + 1)
                    dve.tensor_tensor(b_x1[:, s.par, j, :], bank[attn_bank[j]][:, 0:D], b_xb[:, s.par, j, :], ALU.add)\
                       .then_inc(ao_sb, 1)

            dve.wait_ge(sa.xb, NT)
            step_b(Step(0, 0))
            step_b(Step(0, 1))
            with dve.Fori(1, SB // 2) as m:
                for par in range(2):
                    step_b(Step(m, par))

            def low_w2_0(lo, hi):
                for e in range(lo, hi):
                    dve.wait_ge(w2hi_r, e + 1)
                    dve.tensor_tensor(r1s[:, e, DC * H:2 * DC * H], r1[:, e, DC * H:2 * DC * H],
                                      w2_hi[:, e, :].bitcast(F32), ALU.subtract).then_inc(w2lo_r, 1)

            low_w2_0(0, 2)
            dve.wait_ge(inv_ps, SB)
            link(dve.tensor_copy(inv_f, bank[0][:, 0:ST0]))
            link(dve.tensor_scalar(inv_z, inv_f, 0.0, BIG, ALU.is_equal, ALU.mult))
            link(dve.scalar_tensor_tensor(idx0[:, :], inv_f, -0.75, inv_z, ALU.add, ALU.add))
            end_stage(dve, 1)

            def step_c(s):
                if in_range(s, ST0):
                    e1 = dve.value_load(tile_e[0:1, ds(s.t, 1)], min_val=0, max_val=E - 1)
                    if s.at_least(2):
                        dve.wait_ge(hT_ps, s.t - 1)
                    dve.tensor_copy(c_w1[:, s.par, :, :].rearrange("p c n -> p (c n)").unsqueeze(1),
                                    r1[:, ds(e1, 1), 0:DC * H]).then_inc(w1_r, 1)
                    dve.wait_ge(xg_in[s.par], 16 * (s.half + 1))
                    dve.scalar_tensor_tensor(c_gt[:, s.par, :], c_xg[:, s.par, D:ROW], 1.0, tile_1h[:, ds(s.t * E, E)],
                                             ALU.mult, ALU.mult, accum_out=gate0[:, ds(s.t, 1)]).then_inc(gate_r, 1)
                if s.at_least(1) and in_range(s.back(1), ST0):
                    b = s.back(1)
                    dve.wait_ge(relu_sb, b.t + 1)
                    if b.at_least(1):
                        dve.wait_ge(lo_c, b.t)
                    dve.tensor_tensor(c_sq[:], c_r[:, b.par, :], c_r[:, b.par, :], ALU.mult).then_inc(sq_r, 1)
                    dve.wait_ge(hi_r, b.t + 1)
                    if b.at_least(2):
                        dve.wait_ge(y_ps, b.t - 1)
                    dve.tensor_tensor(c_lo[:, b.par, :, :].rearrange("p c n -> p (c n)"), c_sq[:],
                                      c_hi[:, b.par, :, :].rearrange("p c n -> p (c n)").bitcast(F32), ALU.subtract).then_inc(lo_c, 1)
                if s.at_least(2) and in_range(s.back(2), ST0):
                    b = s.back(2)
                    dve.wait_ge(y_ps, b.t + 1)
                    dve.wait_ge(gate_r, b.t + 1)
                    if b.at_least(2):
                        dve.wait_ge(y_out, 16 * (b.t - 1))
                    dve.tensor_scalar(c_y[:, b.par, :], bank[5 + b.par][:, 0:D], gate0[:, ds(b.t, 1)], None, ALU.mult)\
                       .then_inc(y_sb, 1)

            low_w2_0(2, 4)
            step_c(Step(0, 0))
            low_w2_0(4, 6)
            step_c(Step(0, 1))
            low_w2_0(6, 8)
            for t in range(2, 4):
                step_c(Step(t // 2, t % 2))
            with dve.Fori(2, ST0 // 2) as m:
                for par in range(2):
                    step_c(Step(m, par))
            for t in (ST0, ST0 + 1):
                step_c(Step(t // 2, t % 2))
            end_stage(dve, 2)

            def step_d(s):
                if in_range(s, NT):
                    stats(sd, s, d_x, d_st)
                    if not s.at_least(2):
                        dve.wait_ge(sd.stats, s.t + 1)
                        moments(sd, s, d_st, d_mv)
                if s.at_least(2) and in_range(s.back(2), NT):
                    b = s.back(2)
                    dve.wait_ge(v1_ps, b.t + 1)
                    if in_range(s, NT):
                        dve.wait_ge(sd.stats, s.t + 1)
                    dve.tensor_tensor(r2[:, ds(b.t * D, D)], bank[3 + b.par][:, 0:D], bv1_s[:, :], ALU.add)\
                       .then_inc(v1_sb, 1)
                    if in_range(s, NT):
                        moments(sd, s, d_st, d_mv)
                    dve.wait_ge(sc_sb, b.t + 1)
                    dve.tensor_copy(sc_all[:, :, ds(b.t, 1)], d_sc[:, b.par, :].unsqueeze(2)).then_inc(sc_kept, 1)
                if in_range(s, NT):
                    normalise(sd, s, d_x, d_mv, d_sd, d_rs, d_xn)

            for t in range(4):
                step_d(Step(t // 2, t % 2))
            with dve.Fori(2, NT // 2) as m:
                for par in range(2):
                    step_d(Step(m, par))
            for t in (NT, NT + 1):
                step_d(Step(t // 2, t % 2))
            dve.wait_ge(sc_kept, NT)
            dve.tensor_reduce(pmax[:, :], sc_all[:, :, :], AX, ALU.max).then_inc(gmax, 1)
            end_stage(dve, 3)

            def judge(r, bk, first=False):
                dve.wait_ge(cnt_ps, r + 1)
                count = bank[bk][:, D:D + E]
                if first:
                    dve.tensor_scalar(flip[:, :], count, CAP - 0.5, -1.0, ALU.is_lt, ALU.mult).then_inc(cnt_used, 1)
                else:
                    dve.tensor_scalar(got[:, :], count, CAP - 0.5, -1.0, ALU.is_ge, ALU.mult).then_inc(cnt_used, 1)
                    dve.wait_ge(cnt_used, r + 1)
                    dve.scalar_tensor_tensor(key[:, :], got[:, :], bit_i[:, ds(r, 1)], key[:, :],
                                             ALU.bitwise_and, ALU.bitwise_or).then_inc(key_r, 1)

            def propose(r, half, first=False):
                if not first:
                    dve.wait_ge(cnt_used, r)
                    dve.wait_ge(key_r, r)
                    dve.scalar_tensor_tensor(thr[:, :], key[:, :], bit_i[:, ds(r, 1)], flip[:, :],
                                             ALU.bitwise_or, ALU.bitwise_xor).then_inc(thr_r, 1)
                dve.wait_ge(thr_r, r + 1)
                dve.tensor_tensor(e_cmp[:, :, :], sc_all[:, :, :], over_last(thr[:, :].bitcast(F32), NT),
                                  ALU.is_ge).then_inc(cmp_r, 1)
                dve.wait_ge(cmp_r, r + 1)
                with nc.allow_low_precision(reason="counts up to 32 are exact in bfloat16"):
                    dve.tensor_reduce(e_part[:, half, :], e_cmp[:, :, :], AX, ALU.add).then_inc(part_r, 1)

            def step_e(s, search=False, first=False, last=False, between=None):
                if in_range(s, NT):
                    dve.wait_ge(s_ps, s.t + 1)
                    sv = banks47[:, :, 0:P].rearrange("p g (j k) -> p g j k", j=2)
                    dve.tensor_reduce(e_mx.rearrange("p (g j) -> p g j", g=4), sv, AX, ALU.max).then_inc(mx_r, 1)
                    dve.wait_ge(mx_r, s.t + 1)
                    if s.at_least(1):
                        dve.wait_ge(p_r, s.t)
                    dve.tensor_tensor(e_s.rearrange("p (g j) k -> p g j k", g=4), sv,
                                      e_mx.rearrange("p (g j) -> p g j", g=4).unsqueeze(3).broadcast_to([P, 4, 2, BLK]),
                                      ALU.subtract).then_inc(sub_r, 1)
                if search:
                    judge(2 * s.t, 3, first=first)
                    if first:
                        link(dve.memset(key[:, :], 0))
                        dve.sem_inc(key_r, 1)
                    propose(2 * s.t + 1, 1)
                if between is not None:
                    between(s)
                if s.at_least(1) and in_range(s.back(1), NT):
                    b = s.back(1)
                    dve.wait_ge(o_ps, b.t + 1)
                    o_v = bank[1][:, 0:NH1 * VC].rearrange("p (h d) -> p h d", d=VC)
                    dve.reciprocal(e_rc[:, b.par, :].unsqueeze(2), o_v[:, :, DK:VC]).then_inc(rc_r, 1)
                    dve.wait_ge(rc_r, b.t + 1)
                    if b.at_least(2):
                        dve.wait_ge(oT_ps, b.t - 1)
                    dve.tensor_tensor(e_o[:, b.par, :].rearrange("p (h d) -> p h d", h=NH1),
                                      o_v[:, :, 0:DK],
                                      over_last(e_rc[:, b.par, :], DK), ALU.mult).then_inc(o_sb, 1)
                if search:
                    judge(2 * s.t + 1, 2)
                    if not last:
                        propose(2 * s.t + 2, 0)

            link(dve.memset(thr[:, :], 0))
            dve.sem_inc(thr_r, 1)
            propose(0, 0, first=True)
            step_e(Step(0, 0), search=True, first=True)
            for t in range(1, 4):
                step_e(Step(t // 2, t % 2), search=True)
            with dve.Fori(2, SR // 2 - 1) as m:
                for par in range(2):
                    step_e(Step(m, par), search=True)
            step_e(Step(SR // 2 - 1, 0), search=True)
            step_e(Step(SR // 2 - 1, 1), search=True, last=True)
            tau = over_last(thr[:, :].bitcast(F32), NT)
            both = s_both.rearrange("p (k e t) -> p k e t", k=2, e=E)
            before = s_before.rearrange("p (k e t) -> p k e t", k=2, e=E)

            def mark_selected(s):
                dve.wait_ge(key_r, NT)
                link(dve.tensor_tensor(thr[:, :], key[:, :], flip[:, :], ALU.bitwise_xor))
                dve.tensor_tensor(both[:, 0], sc_all[:, :, :], tau, ALU.is_gt)
                link(dve.tensor_tensor(both[:, 1], sc_all[:, :, :], tau, ALU.is_equal))
                for k in range(2):
                    last = dve.tensor_tensor_scan(s_in[k].rearrange("p e t -> p (e t)"),
                                                  not_first[:, :, :].rearrange("p e t -> p (e t)"),
                                                  s_both[:, k * E * NT:(k + 1) * E * NT], 0.0, ALU.mult, ALU.add)
                link(last)
                for k in range(2):
                    dve.tensor_tensor(before[:, k], s_in[k], both[:, k], ALU.subtract)
                dve.tensor_copy(s_tot, s_in[0][:, :, NT - 1]).then_inc(rank1, 1)

            step_e(Step(SR // 2, 0), between=mark_selected)

            dve.wait_ge(rank1, 2)
            for k in range(2):
                dve.tensor_copy(s_ex[k].rearrange("p e t -> p (e t)"), bank[3 - k][:, D:2 * D])
            link(dve.tensor_scalar(s_need, bank[1][:, 2 * D - E:2 * D], -1.0, float(CAP), ALU.mult, ALU.add))
            dve.sem_inc(rank1, 1)

            def rank_selected(s):
                need = over_last(s_need, NT)
                link(dve.tensor_tensor(s_in[0], s_ex[1], need, ALU.is_lt))
                link(dve.tensor_tensor(s_in[0], s_in[0], both[:, 1], ALU.mult))
                dve.tensor_tensor(s_ex[1], s_ex[1], need, ALU.min)
                link(dve.tensor_tensor(s_in[0], s_in[0], both[:, 0], ALU.add))
                link(dve.tensor_tensor(s_ex[0], s_ex[0], s_ex[1], ALU.add))
                dve.wait_ge(ex_r, 1)
                link(dve.tensor_tensor(s_exp, s_exp, s_in[0], ALU.mult))
                dve.tensor_reduce(s_zp, s_exp, AX, ALU.add).then_inc(zsum, 1)

            def split_rank(s):
                link(dve.scalar_tensor_tensor(s_ex[0], s_ex[0], -BIG, s_in[0], ALU.add, ALU.mult))
                link(dve.tensor_scalar(s_ri[0], s_ex[0], BIG, None, ALU.add))
                link(dve.tensor_scalar(s_ri[1], s_ri[0], 4, None, ALU.logical_shift_right))
                link(dve.tensor_scalar(s_ri[0], s_ri[0], 15, None, ALU.bitwise_and))
                dve.tensor_copy(s_ex[1], s_ri[1])
                link(dve.tensor_copy(s_ex[0], s_ri[0]))

            step_e(Step(SR // 2, 1), between=rank_selected)
            step_e(Step(SR // 2 + 1, 0), between=split_rank)
            step_e(Step(SR // 2 + 1, 1))
            iota32 = over_mid(iota_p[:, 0:32], E)
            iota16 = over_mid(iota_p[:, 0:16], E)

            def hot1(s):
                first = HT * s.t - HT * SH
                for k in range(HT):
                    c = ds(first + k, 1)
                    dve.tensor_tensor(hot1_hi[:, c, :].rearrange("p c (e k) -> p (c e) k", e=E), iota32,
                                      s_ex[1][:, :, c].broadcast_to([P, E, 32]), ALU.is_equal)
                    last = dve.tensor_tensor(hot1_lo[:, c, 1, :, :].rearrange("p c e m -> p (c e) m"), iota16,
                                             s_ex[0][:, :, c].broadcast_to([P, E, 16]), ALU.is_equal)
                last.then_inc(lo_r, 1)
                dve.wait_ge(lo_r, 2 * (s.t - SH) + 1)
                for k in range(HT):
                    c = ds(first + k, 1)
                    last = dve.tensor_scalar(hot1_lo[:, c, 0, :, :], hot1_lo[:, c, 1, :, :], pid0[:, :], None, ALU.mult)
                last.then_inc(lo_r, 1)
                dve.wait_ge(lo_r, 2 * (s.t - SH) + 2)
                for k in range(HT):
                    c = ds(first + k, 1)
                    last = dve.tensor_scalar(hot1_lo[:, c, 1, :, :], hot1_lo[:, c, 1, :, :], iota_t[:, c], None, ALU.mult)
                last.then_inc(hot1_r, 1)

            with dve.Fori(SH // 2, (SH + NT // HT) // 2) as m:
                for par in range(2):
                    step_e(Step(m, par), between=hot1)
            t = SH + NT // HT
            step_e(Step(t // 2, 0))

            dve.wait_ge(zsum, 2)
            dve.reciprocal(rz[:, :], bank[1][:, 2 * D - E:2 * D])
            dve.wait_ge(slots1, 1)
            for q in range(2):
                last = dve.tensor_copy(s_iv[q], bank[3][:, D + q * P:D + (q + 1) * P]
                                       .rearrange("p (k g n) -> p k g n", k=2, g=4))
            link(last)
            dve.sem_inc(slots1, 1)

            def slots_to_index(s):
                for q in range(2):
                    for g in range(4):
                        pq = slice(32 * g, 32 * g + 32)
                        last = dve.scalar_tensor_tensor(s_id[pq, q, :], s_iv[q][pq, 1, g, :], float(P),
                                                        s_iv[q][pq, 0, g, :], ALU.mult, ALU.add)
                link(last)
                for q in range(2):
                    for g in range(4):
                        pq = slice(32 * g, 32 * g + 32)
                        for a in range(4):
                            last = dve.tensor_copy(idx1[32 * a:32 * a + 32, 4 * (4 * q + g):4 * (4 * q + g) + 4],
                                                   s_id[pq, q, 4 * a:4 * a + 4])
                last.then_inc(slots1, 1)

            step_e(Step(t // 2, 1), between=slots_to_index)
            for t in range(SH + NT // HT + 2, NT + 1):
                step_e(Step(t // 2, t % 2))
            end_stage(dve, 4)

            def low_x(s):
                for c in range(DC):
                    dve.wait_ge(xhi_r, DC * s.t + c + 1)
                    dve.tensor_tensor(f_xlo[:, s.par, c, :], bank[4 + c][:, :], f_xhi[:, s.par, c, :].bitcast(F32),
                                      ALU.subtract).then_inc(xlo_r, 1)

            def low_w13(s, c):
                dve.wait_ge(whi_r, DC * s.t + c + 1)
                part = slice(c * 2 * H, (c + 1) * 2 * H)
                dve.tensor_tensor(f_wlo[s.par][:, part], f_w[s.par][:, part], f_whi[s.par][:, part].bitcast(F32),
                                  ALU.subtract).then_inc(wlo_r, 1)

            def low_w2(s):
                dve.wait_ge(w2hi_r, E + s.t + 1)
                part = slice(W13, W13 + W2)
                dve.tensor_tensor(f_wlo[s.par][:, part], f_w[s.par][:, part], f_whi[s.par][:, part].bitcast(F32),
                                  ALU.subtract).then_inc(w2lo_r, 1)

            def weigh(s, lo, hi):
                dve.wait_ge(fwg_r, s.t + 1)
                if s.at_least(1):
                    dve.wait_ge(fy_out, 16 * TE * s.t)
                for i in range(lo, hi):
                    dve.wait_ge(fy_ps, TE * s.t + i + 1)
                    dve.tensor_scalar(f_y[:, i, :], bank[6 + i % 2][:, 0:D], f_wg[:, s.par, i:i + 1], None, ALU.mult)\
                       .then_inc(fy_sb, 1)

            def step_f(s, e, more=True):
                for hb in range(HC):
                    dve.wait_ge(g_r, HC * s.t + hb + 1)
                    if hb >= 2 or s.at_least(1):
                        dve.wait_ge(hlo_r, HC * s.t + hb - 1)
                    dve.tensor_tensor(f_h[:, hb % 2, :], f_g[:, hb % 2, :], bank[2 * (hb % 2) + 1][:, :], ALU.mult)\
                       .then_inc(h1_r, 1)
                    if hb < DC and more:
                        low_w13(s.back(-1), hb)
                    elif hb == DC:
                        low_w2(s)
                    dve.wait_ge(hhi_r, HC * s.t + hb + 1)
                    dve.tensor_tensor(f_hlo[:, s.par, hb, :], f_h[:, hb % 2, :], f_hhi[:, s.par, hb, :].bitcast(F32),
                                      ALU.subtract).then_inc(hlo_r, 1)
                if s.at_least(1):
                    weigh(s.back(1), 0, 1)
                if more:
                    low_x(s.back(-1))
                if s.at_least(1):
                    weigh(s.back(1), 1, TE)
                dve.wait_ge(fwe_r, s.t + 1)
                dve.tensor_scalar(f_wg[:, s.par, :], f_we[:, s.par, :], rz[:, ds(e, 1)], None, ALU.mult).then_inc(fwg_r, 1)

            for c in range(DC):
                low_w13(Step(0, 0), c)
            low_x(Step(0, 0))
            for t in range(2):
                step_f(Step(0, t), t)
            with dve.Fori(1, E // 2 - 1) as m:
                for par in range(2):
                    step_f(Step(m, par), 2 * m + par)
            step_f(Step(E // 2 - 1, 0), E - 2)
            step_f(Step(E // 2 - 1, 1), E - 1, more=False)
            weigh(Step(E // 2 - 1, 1), 0, TE)

        @block.gpsimd
        def _(pool):
            chain = [0]

            def link(ins):
                chain[0] += 1
                ins.then_inc(pseq, 1)
                pool.wait_ge(pseq, chain[0])

            link(pool.memset(ident[:, :], 0.0))
            pool.affine_select(out=ident[:, :], in_=ident[:, :], compare_op=ALU.not_equal, fill=1.0, base=0,
                               pattern=[[-1, P]], channel_multiplier=1)
            pool.memset(eps_c[:, :], EPS)
            link(pool.memset(ones[:, :], 1.0))
            pool.affine_select(out=upper[:, :], in_=ones[:, :], compare_op=ALU.is_gt, fill=0.0, base=0,
                               pattern=[[1, P]], channel_multiplier=-1)
            link(pool.memset(headmask[:, :, :], 0.25))
            hm = headmask[:, :, :].rearrange("p r (h j) -> p r h j", h=8)
            link(pool.affine_select(out=hm, in_=hm, compare_op=ALU.is_ge, fill=0.0, base=0,
                                    pattern=[[0, 2], [-HD0, 8], [0, JR]], channel_multiplier=1))
            link(pool.affine_select(out=hm, in_=hm, compare_op=ALU.is_ge, fill=0.0, base=HD0 - 1,
                                    pattern=[[0, 2], [HD0, 8], [0, JR]], channel_multiplier=-1))
            pool.iota(iota_e[:, :], pattern=[[1, E]], base=0, channel_multiplier=0, allow_small_or_imprecise_dtypes=True)
            pool.iota(iota_p[:, :], pattern=[[1, P]], base=0, channel_multiplier=0, allow_small_or_imprecise_dtypes=True)
            pool.iota(iota_t[:, :], pattern=[[1, ST0]], base=0, channel_multiplier=0, allow_small_or_imprecise_dtypes=True)
            pool.iota(iota_128m[:, :], pattern=[[P, NT]], base=0, channel_multiplier=0, allow_small_or_imprecise_dtypes=True)
            pool.iota(pid1[:, :], pattern=[[0, 1]], base=1, channel_multiplier=1, allow_small_or_imprecise_dtypes=True)
            pool.iota(pid0[:, :], pattern=[[0, 1]], base=0, channel_multiplier=1, allow_small_or_imprecise_dtypes=True)
            pool.iota(number1[:, :], pattern=[[0, TOPK], [P, NT]], base=1, channel_multiplier=1,
                      allow_small_or_imprecise_dtypes=True)
            pool.memset(one8[:, :], 1.0)
            link(pool.memset(not_first[:, :, :], 1.0))
            link(pool.memset(not_first[:, :, 0:1], 0.0))
            for i in range(1, NT):
                last = pool.memset(bit_i[:, i:i + 1], 1 << (NT - 1 - i))
            link(last)
            pool.sem_inc(made, 1)
            last_row = pool.to_reg(N - 1)
            pool.wait_ge(consts, 16 * 7)

            def add_bias(z, s, xt, xb, bo):
                pool.wait_ge(z.x_in[s.par], 16 * (s.half + 1))
                if s.at_least(2):
                    pool.wait_ge(z.xb_out[s.par], 16 * s.half)
                pool.tensor_tensor(xb[:, s.par, :], xt[:, s.par, :], bo[:, :], ALU.add).then_inc(z.xb, 1)

            def step_a(s, second):
                if in_range(s, NT):
                    add_bias(sa, s, a_x, a_xb, bo0_s)
                if s.at_least(2) and in_range(s.back(2), NT):
                    b = s.back(2)
                    tb = b.t - BT if second else b.t
                    pool.wait_ge(q_sb, 2 * (b.t + 1))
                    q = a_q[:, b.par, :, :]
                    t = [a_pt[:, i, :].rearrange("p (r n) -> p r n", r=2) for i in range(2)]
                    cq = cosq_s[:, ds(tb * P, P)]
                    if not b.at_least(1):
                        pool.wait_ge(tables, 16 * 2)
                    if b.at_least(2):
                        pool.wait_ge(tables_b, 16 * 2)
                    if b.at_least(1):
                        pool.wait_ge(qrot, b.t)
                    for r in range(2):
                        pool.tensor_tensor(t[0][:, r, :], q[:, r, :], cq, ALU.mult)
                        last = pool.tensor_tensor(t[1][:, r, :], q[:, 1 - r, :], sinq_s[:, r, ds(tb * P, P)], ALU.mult)
                    last.then_inc(qprod, 1)
                    pool.wait_ge(qprod, b.t + 1)
                    pool.tensor_tensor(qrot_all[:, :, ds(b.t * P, P)], t[0], t[1], ALU.add).then_inc(qrot, 1)

            for t in range(4):
                step_a(Step(t // 2, t % 2), False)
            with pool.Fori(2, 9) as m:
                for par in range(2):
                    step_a(Step(m, par), False)
            with pool.Fori(9, NT // 2) as m:
                for par in range(2):
                    step_a(Step(m, par), True)
            for t in (32, 33):
                step_a(Step(t // 2, t % 2), True)

            pool.wait_ge(bounds_r, 1)
            past = [r_big[:, k * ST0 * E:(k + 1) * ST0 * E].rearrange("p (e j) -> p e j", e=E) for k in range(2)]
            for k, bound in enumerate((t_incl, t_excl)):
                for e in range(E):
                    last = pool.tensor_scalar(past[k][:, e, :], iota_t[:, :], bound[:, e:e + 1], None, ALU.is_ge)
            link(last)
            link(pool.tensor_tensor(tile_1h[:, :].rearrange("p (j e) -> p e j", e=E), past[1], past[0], ALU.subtract))
            for n in (4, 2, 1):
                link(pool.tensor_tensor(past[0][:, 0:n, :], past[0][:, 0:n, :], past[0][:, n:2 * n, :], ALU.add))
            pool.tensor_scalar(tile_e[:, :], past[0][:, 0, :], float(E - 1), None, ALU.min)
            end_stage(pool, 1)

            pool.memset(c_xg, 0.0).then_inc(xg_clear, 1)
            pool.wait_ge(xg_clear, 1)

            def gather(s):
                if s.at_least(2):
                    pool.wait_ge(xg_in[s.par], 16 * s.half)
                pool.tensor_copy(c_gi[:, s.par:s.par + 1], idx0[:, ds(s.t, 1)]).then_inc(gi_r, 1)
                pool.wait_ge(gi_r, s.t + 1)
                if s.at_least(2):
                    pool.wait_ge(cT_ps, s.t - 1)
                    pool.wait_ge(gate_r, s.t - 1)
                pool.nop(nofuse=True)
                pool.indirect_dma_start(c_xg[:, s.par, :], None, xg0_d[:, :],
                                        bass.IndirectOffsetOnAxis(c_gi[:, s.par:s.par + 1], 0),
                                        bounds_check=last_row, oob_is_err=False).then_inc(xg_in[s.par], 16)

            def scatter(s):
                pool.tensor_copy(c_si[:, s.par:s.par + 1], idx0[:, ds(s.t, 1)]).then_inc(si_r, 1)
                pool.wait_ge(si_r, s.t + 1)
                pool.wait_ge(y_sb, s.t + 1)
                if s.at_least(1):
                    pool.wait_ge(y_out, 16 * s.t)
                pool.nop(nofuse=True)
                pool.indirect_dma_start(x1_d[:, :], bass.IndirectOffsetOnAxis(c_si[:, s.par:s.par + 1], 0),
                                        c_y[:, s.par, :], None, bounds_check=last_row, oob_is_err=False,
                                        compute_op=ALU.add).then_inc(y_out, 16)

            for t in range(5):
                gather(Step(t // 2, t % 2))
            scatter(Step(0, 0))
            gather(Step(2, 1))
            with pool.Fori(3, ST0 // 2) as m:
                for par in range(2):
                    s = Step(m, par)
                    scatter(s.back(5))
                    gather(s)
            for t in range(ST0 - 5, ST0):
                scatter(Step(t // 2, t % 2))
            pool.wait_ge(y_out, 16 * ST0)
            end_stage(pool, 2)

            for i in range(2):
                link(pool.memset(e_v[:, i], 0.0))
            for i in range(2):
                for hp in range(2):
                    link(pool.memset(e_v[BLK * hp:BLK * hp + BLK, i, :, hp, :, DK:VC], 1.0))
            link(pool.memset(onesf, 1.0))
            pool.sem_inc(vz, 1)
            for t in range(2):
                add_bias(sd, Step(0, t), d_x, d_xb, bo1_s)
            with pool.Fori(1, NT // 2) as m:
                for par in range(2):
                    add_bias(sd, Step(m, par), d_x, d_xb, bo1_s)
            end_stage(pool, 3)

            pool.wait_ge(gmax, 1)
            pool.partition_all_reduce(scmax[:, :], pmax[:, :], P, RMAX).then_inc(gmax, 1)
            pool.wait_ge(gmax, 2)
            pool.tensor_scalar(nscmax[:, :], scmax[:, :], -1.0, None, ALU.mult).then_inc(gmax, 1)

            def add_x(s):
                pool.wait_ge(y1_sb, s.t + 1)
                pool.wait_ge(xbl[s.par], 16 * (s.half + 1))
                pool.tensor_tensor(e_y[:, s.par, :], e_y[:, s.par, :], e_xb[:, s.par, :], ALU.add).then_inc(fin_r, 1)

            def gather1(s, e):
                if s.at_least(2):
                    pool.wait_ge(fT_ps, s.t - 1)
                    pool.wait_ge(fwe_r, s.t - 1)
                if s.at_least(1):
                    pool.wait_ge(fx_in[(s.back(1)).par], 16 * TE * (s.back(1).half + 1))
                pool.tensor_copy(f_gi[:, :], idx1[:, ds(e * TE, TE)]).then_inc(fgi_r, 1)
                pool.wait_ge(fgi_r, s.t + 1)
                for i in range(TE):
                    pool.nop(nofuse=True)
                    pool.indirect_dma_start(f_xg[:, s.par, i, :], None, xg1_d[:, :],
                                            bass.IndirectOffsetOnAxis(f_gi[:, i:i + 1], 0),
                                            bounds_check=last_row, oob_is_err=False).then_inc(fx_in[s.par], 16)

            with pool.Fori(0, NT // 2 - 2) as m:
                for par in range(2):
                    add_x(Step(m, par))
            pool.wait_ge(qkl[0], 16 * 9)
            pool.wait_ge(qkl[1], 16 * 8)
            pool.wait_ge(slots1, 3)
            gather1(Step(0, 0), 0)
            for t in range(NT - 4, NT):
                add_x(Step(t // 2, t % 2))
            end_stage(pool, 4)

            def scatter1(s, e):
                if s.at_least(1):
                    pool.wait_ge(fy_out, 16 * TE * s.t)
                pool.tensor_copy(f_si[:, :], idx1[:, ds(e * TE, TE)]).then_inc(fsi_r, 1)
                pool.wait_ge(fsi_r, s.t + 1)
                for i in range(TE):
                    pool.wait_ge(fy_sb, TE * s.t + i + 1)
                    pool.nop(nofuse=True)
                    pool.indirect_dma_start(out[:, :], bass.IndirectOffsetOnAxis(f_si[:, i:i + 1], 0),
                                            f_y[:, i, :], None, bounds_check=last_row, oob_is_err=False,
                                            compute_op=ALU.add).then_inc(fy_out, 16)

            gather1(Step(0, 1), 1)
            gather1(Step(1, 0), 2)
            gather1(Step(1, 1), 3)
            scatter1(Step(0, 0), 0)
            with pool.Fori(2, E // 2) as m:
                for par in range(2):
                    s = Step(m, par)
                    gather1(s, 2 * m + par)
                    scatter1(s.back(3), 2 * m + par - 3)
            for t in (E - 3, E - 2, E - 1):
                scatter1(Step(t // 2, t % 2), t)


def kernel(**inputs):
    import numpy as np
    import concourse.bacc as bacc
    from concourse.bass_utils import run_bass_kernel_spmd

    a = {k: np.asarray(v) for k, v in inputs.items()}

    pairs = np.arange(D).reshape(NH0 * JR, 2).T.reshape(-1)
    wq, wk, wv = (a["L0_attn_" + n] for n in ("Wq", "Wk", "Wv"))
    heads = np.arange(D).reshape(2, NH1 // 2, DK).transpose(1, 0, 2).reshape(-1)

    scale = np.arange(0, HD0, 2, dtype=np.float32)[:JR]
    with np.errstate(over="ignore"):
        freqs = np.float32(1.0) / np.power(np.float32(10000.0), scale)
    angles = np.arange(L, dtype=np.float32)[:, None] * freqs[None, :]
    cos = np.cos(angles.astype(np.float64)).astype(np.float32)
    sin = np.sin(angles.astype(np.float64)).astype(np.float32)
    signed = np.stack([-sin, sin], axis=1)
    cos_k = cos.reshape(BT, P, JR).transpose(1, 0, 2).reshape(P, BT * JR)
    sin_k = signed.reshape(BT, P, 2, JR).transpose(1, 0, 2, 3).reshape(P, BT * 2 * JR)
    cos_q = np.tile(cos.T, (NH0, 1))
    sin_q = np.tile(signed.transpose(2, 1, 0), (NH0, 1, 1)).reshape(P, 2 * L)

    arrays = {
        "x": a["L0_attn_x"].reshape(N, D),
        "wqkv0": np.concatenate([wq[:, pairs], wk[:, pairs], wv], axis=1),
        "bq0": a["L0_attn_bq"][pairs].reshape(DC, P).T,
        "bkv0": np.concatenate([a["L0_attn_bk"][pairs], a["L0_attn_bv"]]),
        "wo0": a["L0_attn_Wo"], "bo0": a["L0_attn_bo"],
        "rw0": a["L0_ffn_router_w"].T,
        "w1_0": a["L0_ffn_w1"], "w2_0": a["L0_ffn_w2"],
        "wqkv1": np.concatenate([a["L1_attn_Wq"], a["L1_attn_Wk"], a["L1_attn_Wv"]], axis=1),
        "bqk1": np.concatenate([a["L1_attn_bq"], a["L1_attn_bk"]]).reshape(2 * DC, P).T, "bv1": a["L1_attn_bv"],
        "wo1": a["L1_attn_Wo"][heads], "bo1": a["L1_attn_bo"],
        "wg1": a["L1_ffn_Wg"].T,
        "w13_1": np.concatenate([a["L1_ffn_W1"].transpose(0, 2, 1), a["L1_ffn_W3"].transpose(0, 2, 1)], axis=2),
        "w2_1": a["L1_ffn_W2"].transpose(0, 2, 1),
        "cos_q": cos_q, "sin_q": sin_q, "cos_k": cos_k, "sin_k": sin_k,
    }
    arrays = {k: np.ascontiguousarray(v) for k, v in arrays.items()}

    nc = bacc.Bacc("TRN2", target_bir_lowering=False, num_devices=1)
    args = [nc.dram_tensor("in_" + k, v.shape, mybir.dt.from_np(v.dtype), kind="ExternalInput").ap()
            for k, v in arrays.items()]
    args.append(nc.dram_tensor("out_x", (N, D), F32, kind="ExternalOutput").ap())
    two_layers(nc, *args)
    r = run_bass_kernel_spmd(nc, [{"in_" + k: v for k, v in arrays.items()}], core_ids=[0])
    return r.results[0]["out_x"].reshape(NB, L, D)
```
